# Optimizing a Trainium2 kernel written in Bass

```python
import numpy as np
import jax
import jax.numpy as jnp

def _softmax(x, axis=-1):
    return jax.nn.softmax(x, axis=axis)

def _gelu(x):
    return jax.nn.gelu(x, approximate=True)

def _silu(x):
    return jax.nn.silu(x)

def _sigmoid(x):
    return jax.nn.sigmoid(x)

def _layernorm(x, axis=-1, eps=1e-05):
    m = jnp.mean(x, axis=axis, keepdims=True)
    v = jnp.var(x, axis=axis, keepdims=True)
    return (x - m) / jnp.sqrt(v + eps)

def _scatter_add(tgt, idx, src, axis=0):
    return tgt.at[idx].add(src)

def _segment_sum(src, seg, n):
    return jax.ops.segment_sum(src, seg, n)
kernel_name = 'mk_seq_preln_d1_jaxref_r2_e9754b'

def setup_inputs(seed: int=0):
    np.random.seed(seed)
    _w = jnp.asarray

    def _L0_attn_setup():
        import jax, jax.numpy as jnp
        import numpy as np
        import math
        DIM_MODEL = 512
        DIM_STATE = 128
        DIM_CONV = 4
        EXPAND = 2
        DIM_HEAD = 64
        NGROUPS = 1
        CHUNK = 128
        DIM_INNER = EXPAND * DIM_MODEL
        DIM_SSD = DIM_INNER
        NHEAD = DIM_SSD // DIM_HEAD
        D_IN_PROJ = 2 * DIM_INNER + 2 * NGROUPS * DIM_STATE + NHEAD
        CONV_DIM = DIM_SSD + 2 * NGROUPS * DIM_STATE
        EPS = 1e-05

        def _ssd(x, dt, A, Bm, Cm):
            b, L, h, p = x.shape
            n = Bm.shape[-1]
            c = L // CHUNK
            xc = x.reshape(b, c, CHUNK, h, p)
            dtc = dt.reshape(b, c, CHUNK, h)
            Bc = Bm.reshape(b, c, CHUNK, n)
            Cc = Cm.reshape(b, c, CHUNK, n)
            a = dtc * A
            A_cs = jnp.cumsum(a, axis=2)
            Lmat = jnp.exp(A_cs[:, :, :, None, :] - A_cs[:, :, None, :, :])
            causal = jnp.tril(jnp.ones((CHUNK, CHUNK), bool))
            Lmat = jnp.where(causal[None, None, :, :, None], Lmat, 0.0)
            CB = jnp.einsum('bcin,bcjn->bcij', Cc, Bc)
            scores = CB[..., None] * Lmat * dtc[:, :, None, :, :]
            y = jnp.einsum('bcijh,bcjhp->bcihp', scores, xc)
            decay_end = jnp.exp(A_cs[:, :, -1:, :] - A_cs)
            states = jnp.einsum('bcjh,bcjn,bcjhp->bchpn', dtc * decay_end, Bc, xc)
            chunk_decay = jnp.exp(A_cs[:, :, -1, :])

            def step(carry, inp):
                s, d = inp
                return (carry * d[:, :, None, None] + s, carry)
            init = jnp.zeros((b, h, p, n), x.dtype)
            _, prevs = jax.lax.scan(step, init, (jnp.moveaxis(states, 1, 0), jnp.moveaxis(chunk_decay, 1, 0)))
            prevs = jnp.moveaxis(prevs, 0, 1)
            y = y + jnp.einsum('bcin,bchpn->bcihp', Cc, prevs) * jnp.exp(A_cs)[..., None]
            return y.reshape(b, L, h, p)
        key = jax.random.key(seed)
        ks = jax.random.split(key, 8)
        B, L = (2, 2048)
        u = jax.random.normal(ks[0], (B, L, DIM_MODEL), dtype=jnp.float32)
        in_proj_w = jax.random.normal(ks[1], (D_IN_PROJ, DIM_MODEL), dtype=jnp.float32) / np.sqrt(DIM_MODEL)
        conv_w = jax.random.normal(ks[2], (CONV_DIM, DIM_CONV), dtype=jnp.float32) / np.sqrt(DIM_CONV)
        conv_b = jnp.zeros((CONV_DIM,), jnp.float32)
        dt = jnp.exp(jax.random.uniform(ks[3], (NHEAD,)) * (math.log(0.1) - math.log(0.001)) + math.log(0.001))
        dt_bias = dt + jnp.log(-jnp.expm1(-dt))
        A_log = jnp.log(jax.random.uniform(ks[4], (NHEAD,), minval=1.0, maxval=16.0))
        D = jnp.ones((NHEAD,), jnp.float32)
        norm_w = jnp.ones((DIM_SSD,), jnp.float32)
        out_proj_w = jax.random.normal(ks[5], (DIM_MODEL, DIM_INNER), dtype=jnp.float32) / np.sqrt(DIM_INNER)
        return dict(u=u, in_proj_w=in_proj_w, conv_w=conv_w, conv_b=conv_b, dt_bias=dt_bias, A_log=A_log, D=D, norm_w=norm_w, out_proj_w=out_proj_w)
    _L0_attn_in = _L0_attn_setup()

    def _L0_ffn_setup():
        import jax, jax.numpy as jnp
        import numpy as np

        def _bitlinear(x, w_latent):
            scale = jax.lax.stop_gradient(jnp.clip(jnp.mean(jnp.abs(w_latent), axis=1, keepdims=True), 1e-05, None))
            tern = jnp.clip(jnp.round(w_latent / scale), -1.0, 1.0)
            w = w_latent + jax.lax.stop_gradient(tern - w_latent)
            return x @ (w * scale).T
        key = jax.random.key(seed)
        ks = jax.random.split(key, 6)
        dim, hidden, rank = (512, 2048, 16)
        B, S = (4, 2048)
        x = jax.random.normal(ks[0], (B, S, dim), dtype=jnp.float32)
        w_fc = 0.02 * jax.random.normal(ks[1], (hidden, dim), dtype=jnp.float32)
        w_proj = 0.02 * jax.random.normal(ks[2], (dim, hidden), dtype=jnp.float32)
        u = 0.02 * jax.random.normal(ks[3], (hidden, rank), dtype=jnp.float32)
        v = 0.02 * jax.random.normal(ks[4], (rank, dim), dtype=jnp.float32)
        fast_b = jax.random.normal(ks[5], (rank, rank), dtype=jnp.float32)
        gate = jnp.float32(0.05)
        return {'x': x, 'fast_b': fast_b, 'w_fc': w_fc, 'w_proj': w_proj, 'u': u, 'v': v, 'gate': gate}
    _L0_ffn_in = _L0_ffn_setup()
    _d = {'L0_attn_u': _L0_attn_in['u'], 'L0_attn_in_proj_w': _L0_attn_in['in_proj_w'], 'L0_attn_conv_w': _L0_attn_in['conv_w'], 'L0_attn_conv_b': _L0_attn_in['conv_b'], 'L0_attn_dt_bias': _L0_attn_in['dt_bias'], 'L0_attn_A_log': _L0_attn_in['A_log'], 'L0_attn_D': _L0_attn_in['D'], 'L0_attn_norm_w': _L0_attn_in['norm_w'], 'L0_attn_out_proj_w': _L0_attn_in['out_proj_w'], 'L0_ffn_fast_b': _L0_ffn_in['fast_b'], 'L0_ffn_w_fc': _L0_ffn_in['w_fc'], 'L0_ffn_w_proj': _L0_ffn_in['w_proj'], 'L0_ffn_u': _L0_ffn_in['u'], 'L0_ffn_v': _L0_ffn_in['v'], 'L0_ffn_gate': _L0_ffn_in['gate']}
    _x0 = _d['L0_attn_u']
    _d['L0_attn_u'] = jax.random.normal(jax.random.fold_in(jax.random.key(seed), 1), (2, 4096, 512), dtype=_x0.dtype)
    del _x0
    return _d

def reference(L0_attn_u, L0_attn_in_proj_w, L0_attn_conv_w, L0_attn_conv_b, L0_attn_dt_bias, L0_attn_A_log, L0_attn_D, L0_attn_norm_w, L0_attn_out_proj_w, L0_ffn_fast_b, L0_ffn_w_fc, L0_ffn_w_proj, L0_ffn_u, L0_ffn_v, L0_ffn_gate):

    def _L0_attn_ref(u, in_proj_w, conv_w, conv_b, dt_bias, A_log, D, norm_w, out_proj_w):
        import jax, jax.numpy as jnp
        import numpy as np
        import math
        DIM_MODEL = 512
        DIM_STATE = 128
        DIM_CONV = 4
        EXPAND = 2
        DIM_HEAD = 64
        NGROUPS = 1
        CHUNK = 128
        DIM_INNER = EXPAND * DIM_MODEL
        DIM_SSD = DIM_INNER
        NHEAD = DIM_SSD // DIM_HEAD
        D_IN_PROJ = 2 * DIM_INNER + 2 * NGROUPS * DIM_STATE + NHEAD
        CONV_DIM = DIM_SSD + 2 * NGROUPS * DIM_STATE
        EPS = 1e-05

        def _ssd(x, dt, A, Bm, Cm):
            b, L, h, p = x.shape
            n = Bm.shape[-1]
            c = L // CHUNK
            xc = x.reshape(b, c, CHUNK, h, p)
            dtc = dt.reshape(b, c, CHUNK, h)
            Bc = Bm.reshape(b, c, CHUNK, n)
            Cc = Cm.reshape(b, c, CHUNK, n)
            a = dtc * A
            A_cs = jnp.cumsum(a, axis=2)
            Lmat = jnp.exp(A_cs[:, :, :, None, :] - A_cs[:, :, None, :, :])
            causal = jnp.tril(jnp.ones((CHUNK, CHUNK), bool))
            Lmat = jnp.where(causal[None, None, :, :, None], Lmat, 0.0)
            CB = jnp.einsum('bcin,bcjn->bcij', Cc, Bc)
            scores = CB[..., None] * Lmat * dtc[:, :, None, :, :]
            y = jnp.einsum('bcijh,bcjhp->bcihp', scores, xc)
            decay_end = jnp.exp(A_cs[:, :, -1:, :] - A_cs)
            states = jnp.einsum('bcjh,bcjn,bcjhp->bchpn', dtc * decay_end, Bc, xc)
            chunk_decay = jnp.exp(A_cs[:, :, -1, :])

            def step(carry, inp):
                s, d = inp
                return (carry * d[:, :, None, None] + s, carry)
            init = jnp.zeros((b, h, p, n), x.dtype)
            _, prevs = jax.lax.scan(step, init, (jnp.moveaxis(states, 1, 0), jnp.moveaxis(chunk_decay, 1, 0)))
            prevs = jnp.moveaxis(prevs, 0, 1)
            y = y + jnp.einsum('bcin,bchpn->bcihp', Cc, prevs) * jnp.exp(A_cs)[..., None]
            return y.reshape(b, L, h, p)
        b, L, _ = u.shape
        zxbcdt = u @ in_proj_w.T
        z = zxbcdt[..., :DIM_SSD]
        xBC = zxbcdt[..., DIM_SSD:DIM_SSD + CONV_DIM]
        dt_raw = zxbcdt[..., DIM_SSD + CONV_DIM:]
        xp = jnp.pad(xBC, ((0, 0), (DIM_CONV - 1, 0), (0, 0)))
        xconv = conv_b + sum((conv_w[:, k] * xp[:, k:k + L, :] for k in range(DIM_CONV)))
        xBC = jax.nn.silu(xconv)
        x = xBC[..., :DIM_SSD]
        Bm = xBC[..., DIM_SSD:DIM_SSD + DIM_STATE]
        Cm = xBC[..., DIM_SSD + DIM_STATE:]
        dt = jax.nn.softplus(dt_raw + dt_bias)
        A = -jnp.exp(A_log)
        xh = x.reshape(b, L, NHEAD, DIM_HEAD)
        y = _ssd(xh, dt, A, Bm, Cm) + xh * D[:, None]
        y = y.reshape(b, L, DIM_SSD)
        y = y * jax.nn.silu(z)
        y = y * jax.lax.rsqrt(jnp.mean(y * y, axis=-1, keepdims=True) + EPS) * norm_w
        return y @ out_proj_w.T

    def _L0_ffn_ref(x, fast_b, w_fc, w_proj, u, v, gate):
        import jax, jax.numpy as jnp
        import numpy as np

        def _bitlinear(x, w_latent):
            scale = jax.lax.stop_gradient(jnp.clip(jnp.mean(jnp.abs(w_latent), axis=1, keepdims=True), 1e-05, None))
            tern = jnp.clip(jnp.round(w_latent / scale), -1.0, 1.0)
            w = w_latent + jax.lax.stop_gradient(tern - w_latent)
            return x @ (w * scale).T
        h = _bitlinear(x, w_fc) + gate * (x @ v.T @ fast_b.T @ u.T)
        r = jnp.maximum(h, 0.0)
        return _bitlinear(r * r, w_proj)
    x = L0_attn_u
    x = x + _L0_attn_ref(_layernorm(x, axis=-1), L0_attn_in_proj_w, L0_attn_conv_w, L0_attn_conv_b, L0_attn_dt_bias, L0_attn_A_log, L0_attn_D, L0_attn_norm_w, L0_attn_out_proj_w)
    x = x + _L0_ffn_ref(_layernorm(x, axis=-1), L0_ffn_fast_b, L0_ffn_w_fc, L0_ffn_w_proj, L0_ffn_u, L0_ffn_v, L0_ffn_gate)
    return x

_drawn_inputs = setup_inputs


def setup_inputs(seed=0):
    import zlib

    import numpy as np

    out = dict(_drawn_inputs(seed))
    spreads = {'L0_attn_conv_b': (0.0, 0.1), 'L0_attn_D': (1.0, 0.2), 'L0_attn_norm_w': (1.0, 0.2)}
    factors = {'L0_ffn_fast_b': 8.0, 'L0_ffn_u': 8.0, 'L0_ffn_v': 8.0}
    for name, (base, spread) in spreads.items():
        noise = np.random.default_rng([zlib.crc32(name.encode()), seed]).standard_normal(out[name].shape)
        drawn = base * np.exp(spread * noise) if base else spread * noise
        out[name] = jnp.asarray(drawn.astype(out[name].dtype))
    for name, factor in factors.items():
        out[name] = (out[name] * factor).astype(out[name].dtype)
    return out
```

```python
from contextlib import ExitStack

import concourse.bass as bass
from concourse import mybir

P = 128
F32 = mybir.dt.float32
F32R = mybir.dt.float32r
ALU = mybir.AluOpType
ACT = mybir.ActivationFunctionType

BATCH = 2
SEQ = 4096
DM = 512
KD = DM // P
HEADS = 16
HD = 64
DI = HEADS * HD
NST = 128
TAPS = 4
HIST = TAPS - 1
MX = (DI + 2 * NST) // P
PAIRS = MX // 2
HID = 2048
MF = HID // P
MI = DI // P
RANK = 16
TOK = 256
CH = TOK // P
UNITS = BATCH * SEQ // TOK
ITERS = UNITS // 2
LN_EPS = 1e-5
QUAD = 4
NQ = HEADS // QUAD
W_ZX = 2 * DI + 2 * NST
W_ALL = W_ZX + HEADS
Z0, X0, DT0 = 0, DI, W_ZX
G2 = DI // 512
LR = 80


class Signal:

    def __init__(self, sem, per_unit):
        self.sem, self.per_unit = sem, per_unit


class Unit:

    def __init__(self, it, b):
        self.it, self.b = it, b
        self.n = it * 2 + b

    def back(self, k):
        return Unit(self.it - k // 2, self.b) if k % 2 == 0 else Unit(
            self.it - (k - self.b + 1) // 2, 1 - self.b)

    def ahead(self, k):
        return Unit(self.it + (self.b + k) // 2, (self.b + k) % 2)

    def exists(self):
        return not isinstance(self.n, int) or 0 <= self.n < UNITS


def wait(eng, signal, unit, k):
    value = unit.n * signal.per_unit + k
    if isinstance(value, int) and value <= 0:
        return
    eng.wait_ge(signal.sem, value)


def over_units(eng, step):
    for b in range(2):
        step(Unit(0, b))
    with eng.Fori(1, ITERS - 1) as it:
        for b in range(2):
            step(Unit(it, b))
    for b in range(2):
        step(Unit(ITERS - 1, b))


def mm3(pe, out, parts_l, parts_r, first=True, last=True):
    n = len(parts_l[0])
    combos = [(0, 0), (0, 1), (1, 0)]
    ins = None
    for k in range(n):
        for j, (a, b) in enumerate(combos):
            ins = pe.matmul(out, parts_l[a][k], parts_r[b][k],
                            start=first and k == 0 and j == 0, stop=last and k == n - 1 and j == 2)
    return ins


def inverse_root(pool, out, mean_square, eps_t, power_t, unit, added, ready):
    pool.tensor_tensor(out, mean_square, eps_t, ALU.add).then_inc(added.sem, 1)
    wait(pool, added, unit, 1)
    pool.tensor_tensor(out, out, power_t, ALU.pow).then_inc(ready.sem, 1)


def phase1(nc, x, w_in, conv_w, conv_b, dt_bias, a_log, d_skip, ident_d, tri_d, yg):
    with ExitStack() as ctx:
        def sb(name, shape, dt=F32):
            return ctx.enter_context(nc.sbuf_tensor(name, shape, dt))

        def ps(name):
            return ctx.enter_context(nc.psum_tensor(name, [P, 512], F32))

        def sem(name):
            return ctx.enter_context(nc.semaphore(name))

        def sig(name, per_unit):
            return Signal(sem(name), per_unit)

        w_hi = sb("w_hi", [P, KD, W_ALL], F32R)
        w_lo = sb("w_lo", [P, KD, W_ALL], F32R)
        x_in = sb("x_in", [P, 2, CH, DM])
        xn = sb("xn", [P, CH, DM])
        xnT_hi = sb("xnT_hi", [P, KD, TOK], F32R)
        xnT_lo = sb("xnT_lo", [P, KD, TOK], F32R)
        raw = sb("raw", [P, 2, MX, TOK + HIST])
        acc = sb("acc", [P, MX, TOK])
        bcT = sb("bcT", [P, 2, 2, TOK])
        b_tok = sb("b_tok", [P, 2, CH, NST])
        x_tok = sb("x_tok", [P, 2, CH, DI])
        zs = sb("zs", [P, 2, CH, DI])
        e_buf = sb("e_buf", [P, 2, QUAD, P])
        xdt = sb("xdt", [P, DI])
        xdd = sb("xdd", [P, DI])
        xd = sb("xd", [P, DI])
        y = sb("y", [P, 2, DI])
        state = sb("state", [P, 2, DI])
        cbm = sb("cbm", [P, 2, P])
        ident = sb("ident", [P, P])
        tri = sb("tri", [P, P])
        ones = sb("ones", [P, P])
        sel = sb("sel", [48, HEADS], F32R)
        acsT = sb("acsT", [48, 2, TOK], F32R)
        st = sb("st", [P, 2, CH, 6])
        mv = sb("mv", [P, 2, CH, 2])
        rstd = sb("rstd", [P, 2, CH])
        eps_t = sb("eps_t", [P, CH])
        pace = sb("pace", [P, 1])
        power_t = sb("power_t", [P, CH])
        v = sb("v", [P, 2, CH, HEADS])
        nabs = sb("nabs", [P, 2, CH, HEADS])
        ex = sb("ex", [P, 2, CH, HEADS])
        ln1p = sb("ln1p", [P, 2, CH, HEADS])
        dt = sb("dt", [P, 2, CH, HEADS])
        a = sb("a", [P, 2, CH, HEADS])
        cum = sb("cum", [P, 2, 3, CH, HEADS])
        ecum = sb("ecum", [P, 2, 3, CH, HEADS])
        neg_a = sb("neg_a", [P, 1, HEADS])
        bias_dt = sb("bias_dt", [HEADS, 1])
        vT = sb("vT", [P, TOK])
        d_b = sb("d_b", [P, HEADS])
        cw = sb("cw", [P, MX, TAPS])
        cb = sb("cb", [P, MX])

        ps_t = ps("ps_t")
        ps_x = [ps(f"ps_x{i}") for i in range(2)]
        ps_b = [ps(f"ps_b{i}") for i in range(2)]
        ps_y = [ps(f"ps_y{i}") for i in range(2)]
        ps_i = ps("ps_i")

        w_load = [sem(f"w_load{i}") for i in range(2)]
        c_load = sem("c_load")
        w_hi_done = sem("w_hi_done")
        w_lo_done = sem("w_lo_done")
        setup = sem("setup")
        setup_act = sem("setup_act")

        def stage(k):
            t = x_tok if k % 2 == 0 else zs
            return t[:, :, :, :].rearrange("p b c d -> p (b c d)")[:, 0:W_ALL]

        with nc.Block() as block:
            @block.sync
            def _(sp):
                for k in range(KD):
                    if k >= 2:
                        sp.wait_ge(w_lo_done, k - 1)
                    sp.dma_start(stage(k), w_in[k * P:(k + 1) * P, :]).then_inc(w_load[k % 2], 16)
                sp.dma_start(ident[:, :], ident_d).then_inc(c_load, 16)
                sp.dma_start(tri[:, :], tri_d).then_inc(c_load, 16)
                sp.dma_start(neg_a[:, 0, :], a_log.partition_broadcast(P)).then_inc(c_load, 16)
                sp.dma_start(bias_dt[:, :], dt_bias.unsqueeze(1)).then_inc(c_load, 16)
                sp.dma_start(d_b[:, :], d_skip.partition_broadcast(P)).then_inc(c_load, 16)
                sp.dma_start(cw[:, :, :], conv_w.rearrange("(m p) k -> p m k", p=P)).then_inc(c_load, 16)
                sp.dma_start(cb[:, :], conv_b.rearrange("(m p) -> p m", p=P),
                             allow_slow_non_contiguous=True).then_inc(c_load, 16)

            @block.scalar
            def _(act):
                for k in range(KD):
                    act.wait_ge(w_load[k % 2], 16 * (k // 2 + 1))
                    act.activation(w_hi[:, k, :], stage(k), ACT.Copy).then_inc(w_hi_done, 1)
                act.wait_ge(c_load, 16 * 7)
                act.activation(neg_a[:, 0, :], neg_a[:, 0, :], ACT.Exp).then_inc(setup_act, 1)

            @block.vector
            def _(dve):
                dve.memset(state[:, :, :], 0.0).then_inc(setup, 1)
                dve.memset(raw[:, :, :, 0:HIST], 0.0).then_inc(setup, 1)
                dve.memset(ones[:, :], 1.0).then_inc(setup, 1)
                dve.memset(acsT[:, :, :].bitcast(F32), 0.0).then_inc(setup, 1)
                dve.memset(sel[:, :].bitcast(F32), 0.0).then_inc(setup, 1)
                dve.memset(eps_t[:, :], LN_EPS).then_inc(setup, 1)
                dve.memset(power_t[:, :], -0.5).then_inc(setup, 1)
                dve.memset(vT[:, :], 0.0).then_inc(setup, 1)
                dve.wait_ge(setup, 8)
                for k in range(KD):
                    dve.wait_ge(w_hi_done, k + 1)
                    dve.tensor_tensor(w_lo[:, k, :], stage(k), w_hi[:, k, :].bitcast(F32),
                                      ALU.subtract).then_inc(w_lo_done, 1)
                dve.wait_ge(c_load, 16 * 7)
                dve.tensor_copy(sel[0:HEADS, :], ident[0:HEADS, 0:HEADS]).then_inc(setup, 1)
                dve.tensor_copy(sel[32:32 + HEADS, :], ident[32:32 + HEADS, 32:32 + HEADS]).then_inc(setup, 1)
                dve.wait_ge(setup_act, 1)
                dve.tensor_scalar(neg_a[:, 0, :], neg_a[:, 0, :], -1.0, None, ALU.mult).then_inc(setup, 1)

        x_loaded = [sig(f"x_loaded{b}", 8) for b in range(2)]
        ln_step = sig("ln_step", 4)
        rstd_eps = sig("rstd_eps", 1)
        rstd_ready = sig("rstd_ready", 1)
        xn_ready = sig("xn_ready", 2)
        xnT_ps = sig("xnT_ps", 2)
        hi_ready = sig("hi_ready", 2)
        lo_ready = sig("lo_ready", 2)
        dt_ps = sig("dt_ps", 1)
        dt_vT = sig("dt_vT", 1)
        vT_ps = sig("vT_ps", 1)
        dt_v = sig("dt_v", 1)
        dt_nabs = sig("dt_nabs", 1)
        dt_ex = sig("dt_ex", 1)
        dt_ln = sig("dt_ln", 1)
        dt_ready = sig("dt_ready", 1)
        a_ready = sig("a_ready", 1)
        cum_ps = sig("cum_ps", 1)
        cum_step = sig("cum_step", 4)
        cum_ready = sig("cum_ready", 1)
        ecum_ready = sig("ecum_ready", 1)
        x_ps = sig("x_ps", PAIRS)
        raw_ready = sig("raw_ready", PAIRS)
        tap_ready = sig("tap_ready", PAIRS)
        conv_step = sig("conv_step", MX * (TAPS - 1))
        hist_done = sig("hist_done", 1)
        xc_ready = sig("xc_ready", PAIRS)
        xT_ps = sig("xT_ps", PAIRS)
        x_tok_ready = sig("x_tok_ready", PAIRS)
        z_ps = sig("z_ps", CH * G2)
        zs_ready = sig("zs_ready", CH * G2)
        cb_ps = sig("cb_ps", CH)
        cbm_ready = sig("cbm_ready", CH)
        bc_ps = sig("bc_ps", CH * NQ)
        seg_ready = sig("seg_ready", CH * NQ)
        e_ready = sig("e_ready", CH * NQ)
        s_ready = sig("s_ready", CH * NQ)
        off_ps = sig("off_ps", CH * G2)
        y_off = sig("y_off", CH * G2)
        st_ps = sig("st_ps", CH * G2)
        st_decayed = sig("st_decayed", CH)
        st_added = sig("st_added", CH * G2)
        intra_ps = sig("intra_ps", CH * NQ)
        y_intra = sig("y_intra", CH * G2)
        xdt_ready = sig("xdt_ready", CH)
        xdd_ready = sig("xdd_ready", CH)
        xd_ready = sig("xd_ready", CH)
        y_skip = sig("y_skip", CH)
        y_ready = sig("y_ready", CH)
        y_stored = [sig(f"y_stored{c}", 16) for c in range(CH)]

        x_v = x.rearrange("b (i c p) d -> b i p c d", c=CH, p=P)
        yg_v = yg.rearrange("b (i c p) d -> b i c p d", c=CH, p=P)

        X_ORDER = [("dt", 0), ("z", 0), ("z", 1), ("z", 2), ("z", 3), ("x", 0), ("x", 1), ("x", 2),
                   ("cum", 0), ("x", 3), ("x", 4)]
        NX = len(X_ORDER)
        X_FREED = {"dt": dt_vT, "x": tap_ready, "cum": cum_ready, "z": zs_ready}
        XT_BANK = [ps_t, ps_b[0], ps_b[1], ps_t, ps_b[0]]

        def x_bank(u, use):
            return ps_x[(u.b * NX + X_ORDER.index(use)) % 2]

        with nc.Block() as block:
            @block.sync
            def _(sp):
                def load(u):
                    if u.exists():
                        wait(sp, xn_ready, u.back(2), CH)
                        sp.dma_start(x_in[:, u.b, :, :], x_v[u.b, u.it]).then_inc(x_loaded[u.b].sem, 16)

                def step(u):
                    load(u.ahead(2))
                    for c in range(CH):
                        wait(sp, y_ready, u, c + 1)
                        sp.dma_start(yg_v[u.b, u.it, c], y[:, c, :]).then_inc(y_stored[c].sem, 16)

                for n in range(2):
                    load(Unit(0, 0).ahead(n))
                over_units(sp, step)
                for c in range(CH):
                    sp.wait_ge(y_stored[c].sem, 16 * UNITS)

            @block.gpsimd
            def _(pool):
                def ln_root(u):
                    if u.exists():
                        wait(pool, ln_step, u, 4)
                        wait(pool, xn_ready, u.back(2), CH)
                        inverse_root(pool, rstd[:, u.b, :], mv[:, u.b, :, 1], eps_t[:, :],
                                     power_t[:, :], u, rstd_eps, rstd_ready)

                def step(u):
                    for c in range(CH):
                        if c == 1:
                            ln_root(u.ahead(2))
                        if c == 0:
                            wait(pool, x_tok_ready, u, PAIRS)
                        wait(pool, y_skip, u, c)
                        pool.tensor_tensor(
                            xd[:, :].rearrange("p (h d) -> p h d", d=HD),
                            x_tok[:, u.b, c, :].rearrange("p (h d) -> p h d", d=HD),
                            d_b[:, :].unsqueeze(2).to_broadcast([P, HEADS, HD]),
                            ALU.mult).then_inc(xd_ready.sem, 1)

                ln_root(Unit(0, 0))
                ln_root(Unit(0, 1))
                over_units(pool, step)

            @block.tensor
            def _(pe):
                def x_free(u, use):
                    j = X_ORDER.index(use) - 2
                    w = u if j >= 0 else u.back(1)
                    kind, i = X_ORDER[j % NX]
                    wait(pe, X_FREED[kind], w, i + 1)

                def transpose_xn(u):
                    if not u.exists():
                        return
                    for c in range(CH):
                        wait(pe, xn_ready, u, c + 1)
                        if c == 0:
                            wait(pe, x_tok_ready, u.back(2), 4)
                        else:
                            wait(pe, lo_ready, u, c)
                        for k in range(KD):
                            ins = pe.transpose(ps_t[:, k * P:(k + 1) * P], xn[:, c, k * P:(k + 1) * P],
                                               ident[:, :])
                        ins.then_inc(xnT_ps.sem, 1)

                def xn_parts(c0, n):
                    return [[t[:, k, c0:c0 + n] for k in range(KD)] for t in (xnT_hi, xnT_lo)]

                def w_parts(c0, n):
                    return [[t[:, k, c0:c0 + n] for k in range(KD)] for t in (w_hi, w_lo)]

                def project_dt(u):
                    x_free(u, ("dt", 0))
                    wait(pe, lo_ready, u, CH)
                    mm3(pe, x_bank(u, ("dt", 0))[0:HEADS, 0:TOK], w_parts(DT0, HEADS),
                        xn_parts(0, TOK)).then_inc(dt_ps.sem, 1)

                def transpose_dt(u):
                    wait(pe, dt_vT, u, 1)
                    for c in range(CH):
                        ins = pe.transpose(ps_t[:, c * P:(c + 1) * P], vT[:, c * P:(c + 1) * P], ident[:, :])
                    ins.then_inc(vT_ps.sem, 1)

                def project_x(u, i):
                    x_free(u, ("x", i))
                    bank = x_bank(u, ("x", i))
                    for m in (2 * i, 2 * i + 1):
                        ins = mm3(pe, bank[:, (m % 2) * TOK:(m % 2 + 1) * TOK],
                                  w_parts(X0 + m * P, P), xn_parts(0, TOK))
                    ins.then_inc(x_ps.sem, 1)

                def cumulate(u):
                    x_free(u, ("cum", 0))
                    wait(pe, a_ready, u, 1)
                    bank = x_bank(u, ("cum", 0))
                    a_u = a[:, u.b, :, :].rearrange("p c h -> p (c h)")
                    pe.matmul(bank[:, 0:CH * HEADS], tri[:, :], a_u, start=True, stop=True)
                    pe.matmul(bank[:, 32:32 + CH * HEADS], ones[:, :], a_u, start=True, stop=True)
                    for c in range(CH):
                        ins = pe.matmul(bank[0:HEADS, (c + 1) * P:(c + 2) * P], a[:, u.b, c, :], tri[:, :],
                                        start=True, stop=True)
                    ins.then_inc(cum_ps.sem, 1)

                def project_z(u, i):
                    x_free(u, ("z", i))
                    c, g = divmod(i, G2)
                    mm3(pe, x_bank(u, ("z", i))[:, :], xn_parts(c * P, P),
                        w_parts(Z0 + g * 512, 512)).then_inc(z_ps.sem, 1)

                def transpose_x(u, i):
                    bank = XT_BANK[i]
                    if i == 0 and u.ahead(1).exists():
                        wait(pe, dt_v, u.ahead(1), 1)
                    elif i == 0:
                        wait(pe, x_tok_ready, u.back(1), 4)
                    elif i < 3:
                        wait(pe, seg_ready, u, i)
                    else:
                        wait(pe, x_tok_ready, u, i - 2)
                    wait(pe, xc_ready, u, i + 1)
                    if i < PAIRS - 1:
                        for c in range(CH):
                            for m in range(2):
                                o = (c * 2 + m) * P
                                ins = pe.transpose(bank[:, o:o + P], acc[:, 2 * i + m, c * P:(c + 1) * P],
                                                   ident[:, :])
                    else:
                        for c in range(CH):
                            ins = pe.transpose(bank[:, c * P:(c + 1) * P], bcT[:, u.b, 0, c * P:(c + 1) * P],
                                               ident[:, :])
                    ins.then_inc(xT_ps.sem, 1)

                def y_bank(c, i):
                    return ps_y[(c * 5 + i) % 2]

                def c_dot_b(u, c):
                    if c == 0:
                        wait(pe, xc_ready, u, PAIRS)
                    wait(pe, st_added, u, G2 * c - 1)
                    s = slice(c * P, (c + 1) * P)
                    pe.matmul(y_bank(c, 0)[:, 0:P], bcT[:, u.b, 0, s], bcT[:, u.b, 1, s],
                              start=True, stop=True).then_inc(cb_ps.sem, 1)

                def broadcast(u, c, q):
                    if not u.exists():
                        return
                    wait(pe, seg_ready, u, c * NQ + q - 1)
                    if c == 0 and q == 0:
                        wait(pe, cum_ready, u, 1)
                    if c == 0 and q == 2:
                        wait(pe, x_tok_ready, u, PAIRS)
                    for h in range(QUAD):
                        ins = pe.matmul(ps_b[q % 2][:, h * P:(h + 1) * P],
                                        sel[:, q * QUAD + h:q * QUAD + h + 1].to_broadcast([48, P]),
                                        acsT[:, u.b, c * P:(c + 1) * P], start=True, stop=True)
                    ins.then_inc(bc_ps.sem, 1)

                def off_diagonal(u, c, g):
                    wait(pe, st_added, u.back(1 + 1), 2 * G2) if c == 0 else None
                    wait(pe, st_added, u, G2 * c)
                    if g == 1:
                        wait(pe, cbm_ready, u, c + 1)
                    pe.matmul(y_bank(c, 1 + g)[:, :], bcT[:, u.b, 1, c * P:(c + 1) * P],
                              state[:, u.b, g * 512:(g + 1) * 512], start=True, stop=True
                              ).then_inc(off_ps.sem, 1)

                def new_state(u, c, g):
                    wait(pe, y_off, u, G2 * c + g + 1)
                    wait(pe, xdd_ready, u, c + 1)
                    if c == 0 and g == 0:
                        wait(pe, x_tok_ready, u, PAIRS)
                    pe.matmul(y_bank(c, 3 + g)[:, :], b_tok[:, u.b, c, :], xdd[:, g * 512:(g + 1) * 512],
                              start=True, stop=True).then_inc(st_ps.sem, 1)

                def intra(u, c, q):
                    if q % 2 == 0:
                        wait(pe, y_intra, u, G2 * c + q // 2)
                    if q == 0:
                        wait(pe, xdt_ready, u, c + 1)
                    wait(pe, s_ready, u, c * NQ + q + 1)
                    for h in range(QUAD):
                        hh = q * QUAD + h
                        o = (hh % 8) * HD
                        ins = pe.matmul(ps_i[:, o:o + HD], e_buf[:, q % 2, h, :],
                                        xdt[:, hh * HD:(hh + 1) * HD], start=True, stop=True)
                    ins.then_inc(intra_ps.sem, 1)

                def scan(u, c, fill):
                    c_dot_b(u, c)
                    if c:
                        broadcast(u, c, 0)
                        broadcast(u, c, 1)
                    fill(0)
                    off_diagonal(u, c, 0)
                    off_diagonal(u, c, 1)
                    intra(u, c, 0)
                    broadcast(u, c, 2)
                    intra(u, c, 1)
                    new_state(u, c, 0)
                    broadcast(u, c, 3)
                    fill(1)
                    intra(u, c, 2)
                    new_state(u, c, 1)
                    intra(u, c, 3)

                def step(u):
                    n = u.ahead(1)
                    more = n.exists()
                    if more:
                        project_dt(n)
                    for i in range(CH * G2):
                        if more:
                            project_z(n, i)
                            if i == 0:
                                transpose_dt(n)
                        transpose_x(u, i)
                    transpose_x(u, 4)

                    def fill0(k):
                        if more:
                            project_x(n, k)

                    def fill1(k):
                        if more:
                            project_x(n, 2 + k)
                            if k == 0:
                                cumulate(n)
                            else:
                                project_x(n, 4)

                    scan(u, 0, fill0)
                    scan(u, 1, fill1)
                    if more:
                        broadcast(n, 0, 0)
                        broadcast(n, 0, 1)
                        transpose_xn(n.ahead(1))

                u0 = Unit(0, 0)
                transpose_xn(u0)
                project_dt(u0)
                for i in range(CH * G2):
                    project_z(u0, i)
                    if i == 0:
                        transpose_dt(u0)
                for i in range(PAIRS):
                    if i == 3:
                        cumulate(u0)
                    project_x(u0, i)
                broadcast(u0, 0, 0)
                broadcast(u0, 0, 1)
                transpose_xn(u0.ahead(1))
                over_units(pe, step)

            @block.scalar
            def _(act):
                def xn_high(u):
                    if not u.exists():
                        return
                    for c in range(CH):
                        wait(act, xnT_ps, u, c + 1)
                        wait(act, x_ps, u.back(1), PAIRS)
                        act.activation(xnT_hi[:, :, c * P:(c + 1) * P],
                                       ps_t[:, :].rearrange("p (k t) -> p k t", k=KD),
                                       ACT.Copy).then_inc(hi_ready.sem, 1)

                def softplus(u):
                    wait(act, dt_nabs, u, 1)
                    act.activation(ex[:, u.b], nabs[:, u.b], ACT.Exp).then_inc(dt_ex.sem, 1)
                    wait(act, dt_ex, u, 1)
                    act.activation(ln1p[:, u.b], ex[:, u.b], ACT.Ln, bias=1.0).then_inc(dt_ln.sem, 1)

                def exp_cum(u):
                    wait(act, cum_ready, u, 1)
                    act.activation(ecum[:, u.b], cum[:, u.b], ACT.Exp).then_inc(ecum_ready.sem, 1)

                def raw_copy(u, i):
                    wait(act, x_ps, u, i + 1)
                    wait(act, hist_done, u.back(2), 1)
                    act.activation(raw[:, u.b, 2 * i:2 * i + 2, HIST:HIST + TOK],
                                   x_bank(u, ("x", i))[:, :].rearrange("p (m t) -> p m t", m=2),
                                   ACT.Copy).then_inc(raw_ready.sem, 1)
                    wait(act, xT_ps, u.back(1), min(i + 1, 4))
                    if i == 4:
                        wait(act, xc_ready, u.back(1), PAIRS)
                    for s in range(2):
                        m = 2 * i + s
                        ins = act.activation(acc[:, m, :], x_bank(u, ("x", i))[:, s * TOK:(s + 1) * TOK],
                                             ACT.Identity, bias=cb[:, m:m + 1],
                                             scale=cw[:, m, TAPS - 1:TAPS])
                    ins.then_inc(tap_ready.sem, 1)

                def silu_x(u, i):
                    wait(act, conv_step, u, 2 * (TAPS - 1) * (i + 1))
                    src = acc[:, 2 * i:2 * i + 2, :]
                    dst = src if i < PAIRS - 1 else bcT[:, u.b, :, :]
                    act.activation(dst, src, ACT.Silu).then_inc(xc_ready.sem, 1)

                def x_tok_copy(u, i):
                    wait(act, xT_ps, u, i + 1)
                    if i < PAIRS - 1:
                        act.activation(x_tok[:, u.b, :, i * 256:(i + 1) * 256],
                                       XT_BANK[i][:, :].rearrange("p (c d) -> p c d", c=CH),
                                       ACT.Copy).then_inc(x_tok_ready.sem, 1)
                    else:
                        act.activation(b_tok[:, u.b, :, :],
                                       XT_BANK[i][:, 0:CH * P].rearrange("p (c d) -> p c d", c=CH),
                                       ACT.Copy).then_inc(x_tok_ready.sem, 1)

                def silu_z(u, i):
                    c, g = divmod(i, G2)
                    wait(act, z_ps, u, i + 1)
                    wait(act, y_ready, u.back(2), CH)
                    act.activation(zs[:, u.b, c, g * 512:(g + 1) * 512], x_bank(u, ("z", i))[:, :],
                                   ACT.Silu).then_inc(zs_ready.sem, 1)

                def decay(u, c, q):
                    if not u.exists():
                        return
                    wait(act, bc_ps, u, c * NQ + q + 1)
                    wait(act, intra_ps, u, c * NQ + q - 1)
                    for h in range(QUAD):
                        ins = act.activation(e_buf[:, q % 2, h, :], ps_b[q % 2][:, h * P:(h + 1) * P],
                                             ACT.Relu, bias=cum[:, u.b, 0, c, q * QUAD + h:q * QUAD + h + 1],
                                             scale=-1.0)
                    ins.then_inc(seg_ready.sem, 1)
                    wait(act, seg_ready, u, c * NQ + q + 1)
                    act.activation(e_buf[:, q % 2], e_buf[:, q % 2], ACT.Exp, scale=-1.0
                                   ).then_inc(e_ready.sem, 1)

                def step(u):
                    n = u.ahead(1)
                    more = n.exists()
                    for i in range(PAIRS):
                        silu_x(u, i)
                        if i:
                            x_tok_copy(u, i - 1)
                        if more and i < CH * G2:
                            silu_z(n, i)
                    x_tok_copy(u, 4)
                    decay(u, 0, 2)
                    if more:
                        raw_copy(n, 0)
                    decay(u, 0, 3)
                    if more:
                        raw_copy(n, 1)
                        softplus(n)
                    decay(u, 1, 0)
                    decay(u, 1, 1)
                    if more:
                        raw_copy(n, 2)
                    decay(u, 1, 2)
                    if more:
                        exp_cum(n)
                    decay(u, 1, 3)
                    if more:
                        raw_copy(n, 3)
                        raw_copy(n, 4)
                        decay(n, 0, 0)
                        decay(n, 0, 1)
                        xn_high(n.ahead(1))

                u0 = Unit(0, 0)
                xn_high(u0)
                for i in range(CH * G2):
                    silu_z(u0, i)
                softplus(u0)
                for i in range(PAIRS):
                    raw_copy(u0, i)
                    if i == 2:
                        exp_cum(u0)
                decay(u0, 0, 0)
                decay(u0, 0, 1)
                xn_high(u0.ahead(1))
                over_units(act, step)

            @block.vector
            def _(dve):
                def heads(t):
                    return t.rearrange("p (h d) -> p h d", d=HD)

                def per_head(t, n=HEADS):
                    return t.unsqueeze(2).to_broadcast([P, n, HD])

                def statistics(u):
                    if not u.exists():
                        return
                    b = u.b
                    dve.wait_ge(x_loaded[b].sem, (u.it + 1) * 16)
                    for c in range(CH):
                        dve.bn_stats(st[:, b, c, :], x_in[:, b, c, :]).then_inc(ln_step.sem, 1)
                    wait(dve, ln_step, u, CH)
                    dve.memset(pace[:, :], 0.0)
                    for c in range(CH):
                        dve.bn_aggr(mv[:, b, c, :], st[:, b, c, :]).then_inc(ln_step.sem, 1)

                def normalise(u):
                    if not u.exists():
                        return
                    b = u.b
                    wait(dve, rstd_ready, u, 1)
                    wait(dve, xnT_ps, u.back(1), CH)
                    for c in range(CH):
                        dve.tensor_scalar(xn[:, c, :], x_in[:, b, c, :], mv[:, b, c, 0:1],
                                          rstd[:, b, c:c + 1], ALU.subtract, ALU.mult
                                          ).then_inc(xn_ready.sem, 1)

                def xn_low(u):
                    if not u.exists():
                        return
                    for c in range(CH):
                        wait(dve, hi_ready, u, c + 1)
                        dve.tensor_tensor(xnT_lo[:, :, c * P:(c + 1) * P],
                                          ps_t[:, :].rearrange("p (k t) -> p k t", k=KD),
                                          xnT_hi[:, :, c * P:(c + 1) * P].bitcast(F32), ALU.subtract
                                          ).then_inc(lo_ready.sem, 1)

                def dt_bias(u):
                    wait(dve, dt_ps, u, 1)
                    dve.tensor_scalar(vT[0:HEADS, :], x_bank(u, ("dt", 0))[0:HEADS, 0:TOK], bias_dt[:, 0:1], None,
                                      ALU.add).then_inc(dt_vT.sem, 1)

                def dt_first(u):
                    b = u.b
                    wait(dve, vT_ps, u, 1)
                    dve.tensor_copy(v[:, b], ps_t[:, 0:CH * P].rearrange("p (c h) -> p c h", c=CH)[:, :, 0:HEADS]
                                    ).then_inc(dt_v.sem, 1)
                    wait(dve, dt_v, u, 1)
                    dve.scalar_tensor_tensor(nabs[:, b], v[:, b], -1.0, v[:, b], ALU.mult, ALU.min
                                             ).then_inc(dt_nabs.sem, 1)

                def dt_second(u):
                    b = u.b
                    wait(dve, dt_ln, u, 1)
                    dve.scalar_tensor_tensor(dt[:, b], v[:, b], 0.0, ln1p[:, b], ALU.max, ALU.add
                                             ).then_inc(dt_ready.sem, 1)
                    wait(dve, dt_ready, u, 1)
                    dve.tensor_tensor(a[:, b], dt[:, b], neg_a[:, :, :].to_broadcast([P, CH, HEADS]),
                                      ALU.mult).then_inc(a_ready.sem, 1)

                def cum_copy(u):
                    b = u.b
                    bank = x_bank(u, ("cum", 0))
                    acs = bank[:, 0:CH * HEADS].rearrange("p (c h) -> p c h", c=CH)
                    tot = bank[:, 32:32 + CH * HEADS].rearrange("p (c h) -> p c h", c=CH)
                    accT = bank[0:HEADS, P:P + TOK]
                    wait(dve, cum_ps, u, 1)
                    dve.tensor_copy(cum[:, b, 0], acs).then_inc(cum_step.sem, 1)
                    dve.tensor_copy(acsT[0:HEADS, b, :], accT).then_inc(cum_step.sem, 1)
                    dve.tensor_copy(cum[:, b, 2], tot).then_inc(cum_step.sem, 1)
                    wait(dve, cum_step, u, 1)
                    dve.tensor_tensor(cum[:, b, 1], tot, cum[:, b, 0], ALU.subtract
                                      ).then_inc(cum_step.sem, 1)
                    wait(dve, cum_step, u, 2)
                    dve.tensor_tensor(acsT[32:32 + HEADS, b, :], accT, acsT[0:HEADS, b, :].bitcast(F32),
                                      ALU.subtract).then_inc(cum_ready.sem, 1)

                def convolve(u, i):
                    b = u.b
                    wait(dve, tap_ready, u, i + 1)
                    k0 = i * 2 * (TAPS - 1)
                    for j in range(TAPS - 1):
                        tap = TAPS - 2 - j
                        for s in range(2):
                            m = 2 * i + s
                            if j:
                                wait(dve, conv_step, u, k0 + 2 * j + s - 1)
                            dve.scalar_tensor_tensor(acc[:, m, :], raw[:, b, m, tap:tap + TOK],
                                                     cw[:, m, tap:tap + 1], acc[:, m, :],
                                                     ALU.mult, ALU.add).then_inc(conv_step.sem, 1)

                def keep_history(u):
                    b = u.b
                    wait(dve, conv_step, u, MX * (TAPS - 1))
                    dve.tensor_copy(raw[:, b, :, 0:HIST], raw[:, b, :, TOK:TOK + HIST]
                                    ).then_inc(hist_done.sem, 1)

                def prepare(u, c):
                    b = u.b
                    wait(dve, cb_ps, u, c + 1)
                    wait(dve, intra_ps, u, c * NQ)
                    wait(dve, st_ps, u, G2 * c)
                    dve.tensor_tensor(cbm[:, c, :], ps_y[(c * 5) % 2][:, 0:P], tri[:, :], ALU.mult
                                      ).then_inc(cbm_ready.sem, 1)
                    if c == 0:
                        wait(dve, x_tok_ready, u, PAIRS)
                        wait(dve, ecum_ready, u, 1)
                    dve.tensor_tensor(heads(xdt[:, :]), heads(x_tok[:, b, c, :]), per_head(dt[:, b, c, :]),
                                      ALU.mult).then_inc(xdt_ready.sem, 1)
                    wait(dve, xdt_ready, u, c + 1)
                    dve.tensor_tensor(heads(xdd[:, :]), heads(xdt[:, :]), per_head(ecum[:, b, 1, c, :]),
                                      ALU.mult).then_inc(xdd_ready.sem, 1)

                def mask(u, c, q):
                    wait(dve, e_ready, u, c * NQ + q + 1)
                    if q == 0:
                        wait(dve, cbm_ready, u, c + 1)
                    e = e_buf[:, q % 2]
                    dve.tensor_tensor(e, e, cbm[:, c:c + 1, :].to_broadcast([P, QUAD, P]), ALU.mult
                                      ).then_inc(s_ready.sem, 1)

                def from_state(u, c, g):
                    wait(dve, off_ps, u, G2 * c + g + 1)
                    if g == 0:
                        wait(dve, y_stored[c], u, 0)
                    n = HEADS // G2
                    dve.tensor_tensor(heads(y[:, c, g * 512:(g + 1) * 512]),
                                      heads(ps_y[(c * 5 + 1 + g) % 2][:, :]),
                                      per_head(ecum[:, u.b, 0, c, g * n:(g + 1) * n], n), ALU.mult
                                      ).then_inc(y_off.sem, 1)

                def decay_state(u, c):
                    wait(dve, off_ps, u, G2 * c + 2)
                    wait(dve, st_added, u, G2 * c)
                    dve.tensor_tensor(heads(state[:, u.b, :]), heads(state[:, u.b, :]),
                                      per_head(ecum[:, u.b, 2, c, :]), ALU.mult
                                      ).then_inc(st_decayed.sem, 1)

                def add_state(u, c, g):
                    wait(dve, st_ps, u, G2 * c + g + 1)
                    wait(dve, st_decayed, u, c + 1)
                    s = state[:, u.b, g * 512:(g + 1) * 512]
                    dve.tensor_tensor(s, ps_y[(c * 5 + 3 + g) % 2][:, :], s, ALU.add
                                      ).then_inc(st_added.sem, 1)

                def add_intra(u, c, g):
                    wait(dve, intra_ps, u, c * NQ + 2 * g + 2)
                    wait(dve, y_off, u, G2 * c + g + 1)
                    s = y[:, c, g * 512:(g + 1) * 512]
                    dve.tensor_tensor(s, ps_i[:, :], s, ALU.add).then_inc(y_intra.sem, 1)

                def finish(u, c):
                    wait(dve, xd_ready, u, c + 1)
                    wait(dve, y_intra, u, G2 * c + 2)
                    dve.tensor_tensor(y[:, c, :], y[:, c, :], xd[:, :], ALU.add).then_inc(y_skip.sem, 1)
                    wait(dve, y_skip, u, c + 1)
                    if c == 0:
                        wait(dve, zs_ready, u, CH * G2)
                    dve.tensor_tensor(y[:, c, :], y[:, c, :], zs[:, u.b, c, :], ALU.mult
                                      ).then_inc(y_ready.sem, 1)

                def scan(u, c, fill):
                    prepare(u, c)
                    mask(u, c, 0)
                    fill(0)
                    from_state(u, c, 0)
                    mask(u, c, 1)
                    from_state(u, c, 1)
                    decay_state(u, c)
                    mask(u, c, 2)
                    fill(1)
                    add_intra(u, c, 0)
                    add_state(u, c, 0)
                    mask(u, c, 3)
                    add_state(u, c, 1)
                    fill(2)
                    add_intra(u, c, 1)
                    finish(u, c)

                def step(u):
                    n = u.ahead(1)
                    more = n.exists()
                    if more:
                        dt_bias(n)
                    convolve(u, 3)
                    if more:
                        dt_first(n)
                    convolve(u, 4)
                    keep_history(u)

                    def fill0(k):
                        if not more:
                            return
                        if k == 0:
                            statistics(n.ahead(1))
                        elif k == 1:
                            convolve(n, 0)
                        else:
                            dt_second(n)

                    def fill1(k):
                        if not more:
                            return
                        if k == 0:
                            convolve(n, 1)
                        elif k == 1:
                            normalise(n.ahead(1))
                            cum_copy(n)
                        else:
                            convolve(n, 2)

                    scan(u, 0, fill0)
                    scan(u, 1, fill1)
                    if more:
                        xn_low(n.ahead(1))

                u0 = Unit(0, 0)
                statistics(u0)
                normalise(u0)
                xn_low(u0)
                dt_bias(u0)
                dt_first(u0)
                dt_second(u0)
                statistics(u0.ahead(1))
                for i in range(3):
                    convolve(u0, i)
                cum_copy(u0)
                normalise(u0.ahead(1))
                xn_low(u0.ahead(1))
                over_units(dve, step)


def phase2(nc, x, yg, norm_w, w_out, w_fc, w_proj, u_t, v_lr, fast_bt, gate, ident_d, out):
    with ExitStack() as ctx:
        def sb(name, shape, dt=F32):
            return ctx.enter_context(nc.sbuf_tensor(name, shape, dt))

        def sem(name):
            return ctx.enter_context(nc.semaphore(name))

        def sig(name, per_unit):
            return Signal(sem(name), per_unit)

        wo_hi = sb("wo_hi", [P, MI, DM], F32R)
        wo_lo = sb("wo_lo", [P, MI, DM], F32R)
        fc = sb("fc", [P, KD, HID], F32R)
        proj = sb("proj", [P, MF, DM], F32R)
        lr_u = sb("lr_u", [LR, HID], F32R)
        lr_v_hi = sb("lr_v_hi", [P, KD, RANK], F32R)
        lr_v_lo = sb("lr_v_lo", [P, KD, RANK], F32R)
        y_in = sb("y_in", [P, 2, CH, DI])
        x1 = sb("x1", [P, 2, CH, DM])
        yT_hi = sb("yT_hi", [P, MI, TOK], F32R)
        yT_lo = sb("yT_lo", [P, MI, TOK], F32R)
        xn = sb("xn2", [P, CH, DM])
        xnT_hi = sb("x2T_hi", [P, KD, TOK], F32R)
        xnT_lo = sb("x2T_lo", [P, KD, TOK], F32R)
        zl = sb("zl", [LR, TOK], F32R)
        r = sb("r", [P, 2, 2, TOK])
        r_hi = sb("r_hi", [P, MF, TOK], F32R)
        r_lo = sb("r_lo", [P, MF, TOK], F32R)
        o_buf = sb("o_buf", [P, CH, DM])
        so = sb("so", [P, DM])
        sfc = sb("sfc", [P, MF])
        ident = sb("ident2", [P, P])
        ones = sb("ones2", [P, P])
        nw = sb("nw", [P, MI])
        gate_b = sb("gate_b", [P, 1])
        vr = sb("vr", [RANK, DM])
        fbt = sb("fbt", [RANK, RANK])
        st = sb("st2", [P, 2, CH, 6])
        mv = sb("mv2", [P, 2, CH, 2])
        rstd = sb("rstd2", [P, 2, CH])
        yst = sb("yst", [P, 2, CH, 2, 6])
        ymv = sb("ymv", [P, 2, CH, 2])
        msq = sb("msq", [P, 2, CH])
        eps_t = sb("eps2_t", [P, CH])
        pace = sb("pace2", [P, 1])
        power_t = sb("power2_t", [P, CH])
        rms = sb("rms", [P, 2, CH])

        banks = [ctx.enter_context(nc.psum_tensor(f"q{i}", [P, 512], F32)) for i in range(8)]
        ps_t, ps_u, ps_o, ps_d = banks[0:2], banks[2:4], banks[4:6], banks[6:8]

        piece_in = [sem(f"piece_in{i}") for i in range(2)]
        const_in = sem("const_in")
        lr_in = sem("lr_in")
        wo_in = sem("wo_in")
        zeroed = sem("zeroed")
        abs_done = sem("abs_done")
        sums_done = sem("sums_done")
        half_done = sem("half_done")
        tern_step = sem("tern_step")
        tern_done = sem("tern_done")
        col_ps = sem("col_ps")
        col_read = sem("col_read")
        lr_step = sem("lr_step")
        lr_ps = sem("lr_ps")
        wo_step = sem("wo_step")
        wo_hi_done = sem("wo_hi_done")
        wo_lo_done = sem("wo_lo_done")

        def flat(t):
            return t.rearrange("p a b -> p (a b)")

        def piece(i):
            return flat(y_in[:, i % 2])

        absw = x1[:, :, :, :].rearrange("p b c d -> p (b c d)")
        half = absw
        u_half = [flat(o_buf[0:RANK]), flat(xn[0:RANK])]
        rec = r[0:RANK, :, :, :].rearrange("p a b c -> p (a b c)")
        fc_v = w_fc.rearrange("(k p) n -> k p n", p=P)
        proj_v = w_proj.rearrange("(j f p) n -> j p f n", f=4, p=P)
        wo_v = w_out.rearrange("(m p) n -> p m n", p=P)
        wo_raw = y_in[:, :, :, :].rearrange("p b c (x n) -> p (b c x) n", n=DM)
        LR_STEPS = 10

        with nc.Block() as block:
            @block.sync
            def _(sp):
                sp.dma_start(ident[:, :], ident_d).then_inc(const_in, 16)
                sp.dma_start(gate_b[:, :], gate.partition_broadcast(P)).then_inc(const_in, 16)
                sp.dma_start(vr[:, :], v_lr).then_inc(const_in, 16)
                sp.dma_start(fbt[:, :], fast_bt).then_inc(const_in, 16)
                sp.dma_start(nw[:, :], norm_w.rearrange("(m p) -> p m", p=P),
                             allow_slow_non_contiguous=True).then_inc(const_in, 16)
                for h in range(2):
                    sp.dma_start(u_half[h], u_t[:, h * 1024:(h + 1) * 1024]).then_inc(lr_in, 16)
                for n in range(16):
                    if n >= 2:
                        before = n - 2
                        done = before // 8 * 4 + before % 4 + 1
                        sp.wait_ge(abs_done if before // 4 % 2 == 0 else tern_done, done)
                    if n < 8:
                        sp.dma_start(piece(n), fc_v[n % 4]).then_inc(piece_in[n % 2], 16)
                    else:
                        sp.dma_start(piece(n).rearrange("p (f n) -> p f n", f=4), proj_v[n % 4]
                                     ).then_inc(piece_in[n % 2], 16)
                sp.wait_ge(tern_done, 8)
                sp.dma_start(wo_raw, wo_v).then_inc(wo_in, 16)

            @block.scalar
            def _(act):
                for w in range(2):
                    for k in range(4):
                        act.wait_ge(piece_in[k % 2], 16 * (w * 4 + k // 2 + 1))
                        if w or k:
                            act.wait_ge(sums_done, w * 4 + k)
                        if w == 1 and k == 0:
                            act.wait_ge(tern_done, 4)
                            act.wait_ge(lr_step, LR_STEPS)
                            act.wait_ge(col_ps, 4)
                        act.activation(absw, piece(k), ACT.Abs).then_inc(abs_done, 1)
                act.wait_ge(wo_in, 16)
                for m in range(MI):
                    act.wait_ge(wo_step, m + 1)
                    act.activation(wo_hi[:, m, :], wo_raw[:, m, :], ACT.Copy).then_inc(wo_hi_done, 1)

            @block.tensor
            def _(pe):
                pe.wait_ge(zeroed, 1)
                pe.wait_ge(const_in, 16 * 5)
                for k in range(4):
                    pe.wait_ge(abs_done, k + 1)
                    for j in range(4):
                        ins = pe.matmul(banks[j][:, :], ones[:, :], absw[:, j * 512:(j + 1) * 512],
                                        start=(k == 0), stop=(k == 3))
                    ins.then_inc(sums_done, 1)
                for k in range(KD):
                    ins = pe.matmul(banks[7][:, k * RANK:(k + 1) * RANK], vr[:, k * P:(k + 1) * P],
                                    fbt[:, :], start=True, stop=True)
                ins.then_inc(lr_ps, 1)
                pe.wait_ge(half_done, 4)
                for j in range(4):
                    if j == 3:
                        pe.wait_ge(lr_step, 2)
                    for i in range(4):
                        m = 4 * j + i
                        ins = pe.transpose(banks[4 + j][:, i * P:(i + 1) * P],
                                           half[:, m * P:(m + 1) * P], ident[:, :])
                    ins.then_inc(col_ps, 1)
                for k in range(4):
                    pe.wait_ge(abs_done, 4 + k + 1)
                    for f in range(4):
                        ins = pe.matmul(banks[0][:, :], ones[:, :], absw[:, f * 512:(f + 1) * 512],
                                        start=(k == 0 and f == 0), stop=(k == 3 and f == 3))
                    ins.then_inc(sums_done, 1)

            @block.vector
            def _(dve):
                dve.memset(ones[:, :], 1.0).then_inc(zeroed, 1)
                dve.memset(lr_u[:, :].bitcast(F32), 0.0).then_inc(zeroed, 1)
                dve.memset(zl[:, :].bitcast(F32), 0.0).then_inc(zeroed, 1)
                dve.memset(eps_t[:, :], LN_EPS).then_inc(zeroed, 1)
                dve.memset(power_t[:, :], -0.5).then_inc(zeroed, 1)

                def ternary(i, w, src, thresholds):
                    loads = 4 * (i // 4) + 2 + i % 4 // 2 + 1
                    dve.wait_ge(piece_in[i % 2], 16 * loads)
                    dve.tensor_tensor(w, src, thresholds, ALU.is_gt).then_inc(tern_step, 1)
                    dve.scalar_tensor_tensor(src, src, -1.0, thresholds, ALU.mult, ALU.is_gt
                                             ).then_inc(tern_step, 1)
                    dve.wait_ge(tern_step, 2 * (i + 1))
                    dve.tensor_tensor(w, w.bitcast(F32), src, ALU.subtract).then_inc(tern_done, 1)

                dve.wait_ge(lr_ps, 1)
                bv = banks[7][:, 0:KD * RANK].rearrange("p (k q) -> p k q", k=KD)
                dve.tensor_copy(lr_v_hi[:, :, :], bv).then_inc(lr_step, 1)
                dve.wait_ge(lr_step, 1)
                dve.tensor_tensor(lr_v_lo[:, :, :], bv, lr_v_hi[:, :, :].bitcast(F32), ALU.subtract
                                  ).then_inc(lr_step, 1)
                dve.wait_ge(sums_done, 4)
                for j in range(4):
                    dve.tensor_scalar(half[:, j * 512:(j + 1) * 512], banks[j][:, :], 0.5 / DM, 0.5e-5,
                                      ALU.mult, ALU.max).then_inc(half_done, 1)
                dve.wait_ge(half_done, 4)
                for k in range(KD):
                    ternary(k, fc[:, k, :], piece(k), half)
                for j in range(4):
                    dve.wait_ge(col_ps, j + 1)
                    dve.tensor_scalar(sfc[:, 4 * j:4 * j + 4],
                                      banks[4 + j][:, :].rearrange("p (i t) -> p i t", i=4)[:, :, 0],
                                      2.0, None, ALU.mult).then_inc(col_read, 1)
                dve.wait_ge(lr_in, 16 * 2)
                dve.wait_ge(const_in, 16 * 5)
                dve.wait_ge(zeroed, 3)
                for h in range(2):
                    cols = slice(h * 1024, (h + 1) * 1024)
                    n = 2 + 4 * h
                    dve.reciprocal(rec, half[0:RANK, cols]).then_inc(lr_step, 1)
                    dve.wait_ge(lr_step, n + 1)
                    dve.scalar_tensor_tensor(u_half[h], u_half[h], gate_b[0:RANK, 0:1], rec,
                                             ALU.mult, ALU.mult).then_inc(lr_step, 1)
                    dve.wait_ge(lr_step, n + 2)
                    dve.tensor_scalar(u_half[h], u_half[h], 0.5, None, ALU.mult).then_inc(lr_step, 1)
                    dve.wait_ge(lr_step, n + 3)
                    dve.tensor_copy(lr_u[0:RANK, cols], u_half[h])
                    dve.tensor_copy(lr_u[32:32 + RANK, cols], u_half[h]).then_inc(lr_step, 1)
                    dve.wait_ge(lr_step, n + 4)
                    dve.tensor_tensor(lr_u[64:64 + RANK, cols], u_half[h], lr_u[0:RANK, cols].bitcast(F32),
                                      ALU.subtract).then_inc(zeroed, 1)
                dve.wait_ge(sums_done, 8)
                dve.tensor_scalar(so[:, :], banks[0][:, :], 0.5 / HID, 0.5e-5, ALU.mult, ALU.max
                                  ).then_inc(half_done, 1)
                dve.wait_ge(half_done, 5)
                for k in range(4):
                    ternary(4 + k, proj[:, 4 * k:4 * k + 4, :], piece(k).rearrange("p (f n) -> p f n", f=4),
                            so[:, :].unsqueeze(1).to_broadcast([P, 4, DM]))
                dve.wait_ge(tern_done, 8)
                dve.tensor_scalar(so[:, :], so[:, :], 2.0, None, ALU.mult).then_inc(half_done, 1)
                dve.wait_ge(wo_in, 16)
                for m in range(MI):
                    dve.tensor_scalar(wo_raw[:, m, :], wo_raw[:, m, :], nw[:, m:m + 1], None, ALU.mult
                                      ).then_inc(wo_step, 1)
                for m in range(MI):
                    dve.wait_ge(wo_hi_done, m + 1)
                    dve.tensor_tensor(wo_lo[:, m, :], wo_raw[:, m, :], wo_hi[:, m, :].bitcast(F32),
                                      ALU.subtract).then_inc(wo_lo_done, 1)

        y_loaded = [sig(f"y_loaded{s}", 8) for s in range(2)]
        xr_loaded = [sig(f"xr_loaded{s}", 8) for s in range(2)]
        stored = [sig(f"stored{c}", 16) for c in range(CH)]
        rms_step = sig("rms_step", 8)
        yT_ps = sig("yT_ps", 4)
        yT_hi_ready = sig("yT_hi_ready", 4)
        yT_lo_ready = sig("yT_lo_ready", 4)
        o_ps = sig("o_ps", CH)
        x1_ready = sig("x1_ready", CH)
        ln_step = sig("ln2_step", 4)
        rstd_eps = sig("rstd2_eps", 1)
        rstd_ready = sig("rstd2_ready", 1)
        rms_eps = sig("rms_eps", 1)
        rms_ready = sig("rms_ready", 1)
        xn_ready = sig("xn2_ready", CH)
        xT_ps = sig("x2T_ps", CH)
        xT_hi_ready = sig("x2T_hi_ready", CH)
        xT_lo_ready = sig("x2T_lo_ready", CH)
        zl_ps = sig("zl_ps", 1)
        zl_step = sig("zl_step", 2)
        zl_ready = sig("zl_ready", 1)
        up_ps = sig("up_ps", MF // 2)
        relu_done = sig("relu_done", MF // 2)
        sq_ready = sig("sq_ready", MF // 2)
        r_hi_ready = sig("r_hi_ready", MF // 2)
        r_lo_ready = sig("r_lo_ready", MF // 2)
        down_ps = sig("down_ps", CH)
        scaled = sig("scaled", CH)
        out_ready = sig("out_ready", CH)

        x_v = x.rearrange("b (i s c p) d -> (b i) s p c d", s=2, c=CH, p=P)
        y_v = yg.rearrange("b (i s c p) d -> (b i) s p c d", s=2, c=CH, p=P)
        out_v = out.rearrange("b (i s c p) d -> (b i) s c p d", s=2, c=CH, p=P)

        with nc.Block() as block:
            @block.sync
            def _(sp):
                def load(u):
                    if not u.exists():
                        return
                    wait(sp, yT_ps, u.back(2), 4)
                    wait(sp, rms_step, u.back(2), 4)
                    sp.dma_start(y_in[:, u.b], y_v[u.it, u.b]).then_inc(y_loaded[u.b].sem, 16)
                    wait(sp, out_ready, u.back(2), CH)
                    sp.dma_start(x1[:, u.b], x_v[u.it, u.b]).then_inc(xr_loaded[u.b].sem, 16)

                def step(u):
                    for c in range(CH):
                        wait(sp, out_ready, u, c + 1)
                        sp.dma_start(out_v[u.it, u.b, c], o_buf[:, c, :]).then_inc(stored[c].sem, 16)
                    load(u.ahead(2))

                load(Unit(0, 0))
                load(Unit(0, 1))
                over_units(sp, step)
                for c in range(CH):
                    sp.wait_ge(stored[c].sem, 16 * UNITS)

            @block.gpsimd
            def _(pool):
                def roots(u):
                    if not u.exists():
                        return
                    wait(pool, rms_step, u, 8)
                    wait(pool, x1_ready, u.back(2), CH)
                    inverse_root(pool, rms[:, u.b, :], msq[:, u.b, :], eps_t[:, :], power_t[:, :],
                                 u, rms_eps, rms_ready)
                    wait(pool, ln_step, u, 4)
                    wait(pool, xn_ready, u.back(2), CH)
                    inverse_root(pool, rstd[:, u.b, :], mv[:, u.b, :, 1], eps_t[:, :], power_t[:, :],
                                 u, rstd_eps, rstd_ready)

                roots(Unit(0, 0))
                over_units(pool, lambda u: roots(u.ahead(1)))

            @block.tensor
            def _(pe):
                def parts(hi, lo, n, c0, w):
                    return [[t[:, k, c0:c0 + w] for k in range(n)] for t in (hi, lo)]

                def transpose_y(u, i):
                    if i == 0:
                        pe.wait_ge(y_loaded[u.b].sem, (u.it + 1) * 16)
                    if i < 2:
                        wait(pe, xT_lo_ready, u.back(1), i + 1)
                    else:
                        wait(pe, yT_lo_ready, u, i - 1)
                    for m in range(2):
                        for c in range(CH):
                            o = (m * CH + c) * P
                            ins = pe.transpose(ps_t[i % 2][:, o:o + P],
                                               y_in[:, u.b, c, (2 * i + m) * P:(2 * i + m + 1) * P],
                                               ident[:, :])
                    ins.then_inc(yT_ps.sem, 1)

                def project_out(u, c):
                    if c == 0:
                        wait(pe, yT_lo_ready, u, 4)
                        wait(pe, zl_ready, u.back(1), 1)
                    else:
                        wait(pe, x1_ready, u.back(1), c + 1)
                    mm3(pe, ps_o[c][:, :], parts(yT_hi, yT_lo, MI, c * P, P),
                        parts(wo_hi, wo_lo, MI, 0, DM)).then_inc(o_ps.sem, 1)

                def transpose_xn(u, c):
                    wait(pe, xn_ready, u, c + 1)
                    wait(pe, yT_lo_ready, u, 3 + c)
                    for k in range(KD):
                        ins = pe.transpose(ps_t[c][:, k * P:(k + 1) * P], xn[:, c, k * P:(k + 1) * P],
                                           ident[:, :])
                    ins.then_inc(xT_ps.sem, 1)

                def low_rank(u):
                    wait(pe, xT_lo_ready, u, CH)
                    wait(pe, x1_ready, u, 1)
                    mm3(pe, ps_o[0][0:RANK, 0:TOK], parts(lr_v_hi, lr_v_lo, KD, 0, RANK),
                        parts(xnT_hi, xnT_lo, KD, 0, TOK)).then_inc(zl_ps.sem, 1)

                def up(u, i):
                    if i == 0:
                        wait(pe, zl_ready, u, 1)
                    wait(pe, relu_done, u, i - 1)
                    for j in range(2):
                        m = 2 * i + j
                        dst = ps_u[i % 2][:, j * TOK:(j + 1) * TOK]
                        for k in range(KD):
                            w = fc[:, k, m * P:(m + 1) * P]
                            pe.matmul(dst, w, xnT_hi[:, k, :], start=(k == 0), stop=False)
                            pe.matmul(dst, w, xnT_lo[:, k, :], start=False, stop=False)
                        ins = pe.matmul(dst, lr_u[:, m * P:(m + 1) * P], zl[:, :], start=False, stop=True)
                    ins.then_inc(up_ps.sem, 1)

                def down(u, c):
                    wait(pe, scaled, u.back(1), c + 1)
                    for f in range(MF):
                        if c == 0 and f % 2 == 0:
                            wait(pe, r_lo_ready, u, f // 2 + 1)
                        for t in (r_hi, r_lo):
                            ins = pe.matmul(ps_d[c][:, :], t[:, f, c * P:(c + 1) * P], proj[:, f, :],
                                            start=(f == 0 and t is r_hi), stop=(f == MF - 1 and t is r_lo))
                    ins.then_inc(down_ps.sem, 1)

                def step(u):
                    n = u.ahead(1)
                    more = n.exists()
                    for i in range(MF // 2):
                        up(u, i)
                        if more and i % 2 == 1:
                            transpose_y(n, i // 2)
                    if more:
                        for c in range(CH):
                            project_out(n, c)
                    for c in range(CH):
                        down(u, c)
                    if more:
                        for c in range(CH):
                            transpose_xn(n, c)
                        low_rank(n)

                u0 = Unit(0, 0)
                for i in range(4):
                    transpose_y(u0, i)
                for c in range(CH):
                    project_out(u0, c)
                for c in range(CH):
                    transpose_xn(u0, c)
                low_rank(u0)
                over_units(pe, step)

            @block.scalar
            def _(act):
                def y_high(u, i):
                    wait(act, yT_ps, u, i + 1)
                    wait(act, o_ps, u.back(1), CH)
                    act.activation(flat(yT_hi[:, 2 * i:2 * i + 2, :]), ps_t[i % 2][:, :], ACT.Copy
                                   ).then_inc(yT_hi_ready.sem, 1)

                def x_high(u, c):
                    wait(act, xT_ps, u, c + 1)
                    wait(act, up_ps, u.back(1), MF // 2)
                    act.activation(xnT_hi[:, :, c * P:(c + 1) * P],
                                   ps_t[c][:, :].rearrange("p (k t) -> p k t", k=KD),
                                   ACT.Copy).then_inc(xT_hi_ready.sem, 1)

                def squared_relu(u, i):
                    wait(act, up_ps, u, i + 1)
                    wait(act, r_lo_ready, u, i - 1)
                    for j in range(2):
                        m = 2 * i + j
                        ins = act.activation(r[:, i % 2, j, :], ps_u[i % 2][:, j * TOK:(j + 1) * TOK],
                                             ACT.Relu, scale=sfc[:, m:m + 1])
                    ins.then_inc(relu_done.sem, 1)
                    wait(act, relu_done, u, i + 1)
                    act.activation(r[:, i % 2], r[:, i % 2], ACT.Square).then_inc(sq_ready.sem, 1)

                def step(u):
                    n = u.ahead(1)
                    more = n.exists()
                    for i in range(MF // 2):
                        squared_relu(u, i)
                        if more and i % 2 == 1:
                            y_high(n, i // 2)
                    if more:
                        for c in range(CH):
                            x_high(n, c)

                u0 = Unit(0, 0)
                for i in range(4):
                    y_high(u0, i)
                for c in range(CH):
                    x_high(u0, c)
                over_units(act, step)

            @block.vector
            def _(dve):
                def mean_square(u):
                    b = u.b
                    dve.wait_ge(y_loaded[b].sem, (u.it + 1) * 16)
                    for c in range(CH):
                        for g in range(2):
                            dve.bn_stats(yst[:, b, c, g, :], y_in[:, b, c, g * 512:(g + 1) * 512]
                                         ).then_inc(rms_step.sem, 1)
                    wait(dve, rms_step, u, 2 * CH)
                    dve.memset(pace[:, :], 0.0)
                    for c in range(CH):
                        dve.bn_aggr(ymv[:, b, c, :], yst[:, b, c].rearrange("p g s -> p (g s)")
                                    ).then_inc(rms_step.sem, 1)
                    wait(dve, rms_step, u, 6)
                    dve.tensor_tensor(msq[:, b, :], ymv[:, b, :, 0], ymv[:, b, :, 0], ALU.mult
                                      ).then_inc(rms_step.sem, 1)
                    wait(dve, rms_step, u, 7)
                    dve.tensor_tensor(msq[:, b, :], msq[:, b, :], ymv[:, b, :, 1], ALU.add
                                      ).then_inc(rms_step.sem, 1)

                def y_low(u, i):
                    wait(dve, yT_hi_ready, u, i + 1)
                    hi = flat(yT_hi[:, 2 * i:2 * i + 2, :]).bitcast(F32)
                    dve.tensor_tensor(flat(yT_lo[:, 2 * i:2 * i + 2, :]), ps_t[i % 2][:, :], hi,
                                      ALU.subtract).then_inc(yT_lo_ready.sem, 1)

                def residual(u, c):
                    b = u.b
                    wait(dve, o_ps, u, c + 1)
                    if c == 0:
                        dve.wait_ge(xr_loaded[b].sem, (u.it + 1) * 16)
                        wait(dve, rms_ready, u, 1)
                    dve.scalar_tensor_tensor(x1[:, b, c, :], ps_o[c][:, :], rms[:, b, c:c + 1],
                                             x1[:, b, c, :], ALU.mult, ALU.add).then_inc(x1_ready.sem, 1)

                def normalise(u):
                    b = u.b
                    for c in range(CH):
                        wait(dve, x1_ready, u, c + 1)
                        dve.bn_stats(st[:, b, c, :], x1[:, b, c, :]).then_inc(ln_step.sem, 1)
                    wait(dve, ln_step, u, CH)
                    dve.memset(pace[:, :], 0.0)
                    for c in range(CH):
                        dve.bn_aggr(mv[:, b, c, :], st[:, b, c, :]).then_inc(ln_step.sem, 1)
                    wait(dve, rstd_ready, u, 1)
                    wait(dve, xT_ps, u.back(1), CH)
                    for c in range(CH):
                        dve.tensor_scalar(xn[:, c, :], x1[:, b, c, :], mv[:, b, c, 0:1],
                                          rstd[:, b, c:c + 1], ALU.subtract, ALU.mult
                                          ).then_inc(xn_ready.sem, 1)

                def x_low(u, c):
                    wait(dve, xT_hi_ready, u, c + 1)
                    dve.tensor_tensor(xnT_lo[:, :, c * P:(c + 1) * P],
                                      ps_t[c][:, :].rearrange("p (k t) -> p k t", k=KD),
                                      xnT_hi[:, :, c * P:(c + 1) * P].bitcast(F32), ALU.subtract
                                      ).then_inc(xT_lo_ready.sem, 1)

                def split_low_rank(u):
                    src = ps_o[0][0:RANK, 0:TOK]
                    wait(dve, zl_ps, u, 1)
                    dve.tensor_copy(zl[0:RANK, :], src).then_inc(zl_step.sem, 1)
                    dve.tensor_copy(zl[64:64 + RANK, :], src).then_inc(zl_step.sem, 1)
                    wait(dve, zl_step, u, 1)
                    dve.tensor_tensor(zl[32:32 + RANK, :], src, zl[0:RANK, :].bitcast(F32), ALU.subtract
                                      ).then_inc(zl_ready.sem, 1)

                def split_squares(u, i):
                    wait(dve, sq_ready, u, i + 1)
                    if i == 0:
                        wait(dve, down_ps, u.back(1), CH)
                    dve.tensor_copy(r_hi[:, 2 * i:2 * i + 2, :], r[:, i % 2]).then_inc(r_hi_ready.sem, 1)
                    wait(dve, r_hi_ready, u, i + 1)
                    dve.tensor_tensor(r_lo[:, 2 * i:2 * i + 2, :], r[:, i % 2],
                                      r_hi[:, 2 * i:2 * i + 2, :].bitcast(F32), ALU.subtract
                                      ).then_inc(r_lo_ready.sem, 1)

                def output(u, c):
                    wait(dve, down_ps, u, c + 1)
                    wait(dve, stored[c], u, 0)
                    dve.tensor_tensor(o_buf[:, c, :], ps_d[c][:, :], so[:, :], ALU.mult
                                      ).then_inc(scaled.sem, 1)
                    wait(dve, scaled, u, c + 1)
                    dve.tensor_tensor(o_buf[:, c, :], o_buf[:, c, :], x1[:, u.b, c, :], ALU.add
                                      ).then_inc(out_ready.sem, 1)

                def step(u):
                    n = u.ahead(1)
                    more = n.exists()
                    for i in range(MF // 2):
                        split_squares(u, i)
                        if more and i % 2 == 1:
                            y_low(n, i // 2)
                    if more:
                        mean_square(n)
                        for c in range(CH):
                            residual(n, c)
                        normalise(n)
                    for c in range(CH):
                        output(u, c)
                    if more:
                        for c in range(CH):
                            x_low(n, c)
                        split_low_rank(n)

                u0 = Unit(0, 0)
                for i in range(4):
                    y_low(u0, i)
                mean_square(u0)
                for c in range(CH):
                    residual(u0, c)
                normalise(u0)
                for c in range(CH):
                    x_low(u0, c)
                split_low_rank(u0)
                over_units(dve, step)


def kernel(**inputs):
    import numpy as np
    import concourse.bacc as bacc
    from concourse.bass_utils import run_bass_kernel_spmd

    def arr(name):
        return np.asarray(inputs[name])

    def turned(name):
        return np.ascontiguousarray(arr(name).T)

    data = {
        "x": arr("L0_attn_u"),
        "w_in": turned("L0_attn_in_proj_w"),
        "conv_w": arr("L0_attn_conv_w"),
        "conv_b": arr("L0_attn_conv_b"),
        "dt_bias": arr("L0_attn_dt_bias"),
        "a_log": arr("L0_attn_A_log"),
        "d_skip": arr("L0_attn_D"),
        "norm_w": arr("L0_attn_norm_w"),
        "w_out": turned("L0_attn_out_proj_w"),
        "w_fc": turned("L0_ffn_w_fc"),
        "w_proj": turned("L0_ffn_w_proj"),
        "u_t": turned("L0_ffn_u"),
        "v_lr": arr("L0_ffn_v"),
        "fast_bt": turned("L0_ffn_fast_b"),
        "gate": arr("L0_ffn_gate").reshape(1),
        "ident": np.eye(P, dtype=np.float32),
        "tri": np.triu(np.ones((P, P), np.float32)),
    }
    nc = bacc.Bacc("TRN2", target_bir_lowering=False, num_devices=1)
    d = {}
    for name, value in data.items():
        value = np.ascontiguousarray(value)
        data[name] = value
        d[name] = nc.dram_tensor(f"{name}_dram", list(value.shape), mybir.dt.from_np(value.dtype),
                                 kind="ExternalInput").ap()
    yg = nc.dram_tensor("gated_dram", [BATCH, SEQ, DI], F32, kind="Internal").ap()
    out = nc.dram_tensor("out_dram", [BATCH, SEQ, DM], F32, kind="ExternalOutput").ap()
    phase1(nc, d["x"], d["w_in"], d["conv_w"], d["conv_b"], d["dt_bias"], d["a_log"], d["d_skip"],
           d["ident"], d["tri"], yg)
    phase2(nc, d["x"], yg, d["norm_w"], d["w_out"], d["w_fc"], d["w_proj"], d["u_t"], d["v_lr"],
           d["fast_bt"], d["gate"], d["ident"], out)
    result = run_bass_kernel_spmd(nc, [{f"{name}_dram": value for name, value in data.items()}], core_ids=[0])
    return result.results[0]["out_dram"]
```

```python
from contextlib import ExitStack

import concourse.bass as bass
from concourse import mybir

P = 128
F32 = mybir.dt.float32
F32R = mybir.dt.float32r
ALU = mybir.AluOpType
ACT = mybir.ActivationFunctionType

BATCH = 2
SEQ = 4096
DM = 512
KD = DM // P
HEADS = 16
HD = 64
DI = HEADS * HD
NST = 128
TAPS = 4
HIST = TAPS - 1
MX = (DI + 2 * NST) // P
PAIRS = MX // 2
HID = 2048
MF = HID // P
MI = DI // P
RANK = 16
TOK = 256
CH = TOK // P
UNITS = BATCH * SEQ // TOK
ITERS = UNITS // 2
LN_EPS = 1e-5
QUAD = 4
NQ = HEADS // QUAD
W_ZX = 2 * DI + 2 * NST
W_ALL = W_ZX + HEADS
Z0, X0, DT0 = 0, DI, W_ZX
G2 = DI // 512
LR = 80


class Signal:

    def __init__(self, sem, per_unit):
        self.sem, self.per_unit = sem, per_unit


class Unit:

    def __init__(self, it, b):
        self.it, self.b = it, b
        self.n = it * 2 + b

    def back(self, k):
        return Unit(self.it - k // 2, self.b) if k % 2 == 0 else Unit(
            self.it - (k - self.b + 1) // 2, 1 - self.b)

    def ahead(self, k):
        return Unit(self.it + (self.b + k) // 2, (self.b + k) % 2)

    def exists(self):
        return not isinstance(self.n, int) or 0 <= self.n < UNITS


def wait(eng, signal, unit, k):
    value = unit.n * signal.per_unit + k
    if isinstance(value, int) and value <= 0:
        return
    eng.wait_ge(signal.sem, value)


def over_units(eng, step):
    for b in range(2):
        step(Unit(0, b))
    with eng.Fori(1, ITERS - 1) as it:
        for b in range(2):
            step(Unit(it, b))
    for b in range(2):
        step(Unit(ITERS - 1, b))


def mm3(pe, out, parts_l, parts_r, first=True, last=True):
    n = len(parts_l[0])
    combos = [(0, 0), (0, 1), (1, 0)]
    ins = None
    for k in range(n):
        for j, (a, b) in enumerate(combos):
            ins = pe.matmul(out, parts_l[a][k], parts_r[b][k],
                            start=first and k == 0 and j == 0, stop=last and k == n - 1 and j == 2)
    return ins


def inverse_root(pool, out, mean_square, eps_t, power_t, unit, added, ready):
    pool.tensor_tensor(out, mean_square, eps_t, ALU.add).then_inc(added.sem, 1)
    wait(pool, added, unit, 1)
    pool.tensor_tensor(out, out, power_t, ALU.pow).then_inc(ready.sem, 1)


def phase1(nc, x, w_in, conv_w, conv_b, dt_bias, a_log, d_skip, ident_d, tri_d, yg):
    with ExitStack() as ctx:
        def sb(name, shape, dt=F32):
            return ctx.enter_context(nc.sbuf_tensor(name, shape, dt))

        def ps(name):
            return ctx.enter_context(nc.psum_tensor(name, [P, 512], F32))

        def sem(name):
            return ctx.enter_context(nc.semaphore(name))

        def sig(name, per_unit):
            return Signal(sem(name), per_unit)

        w_hi = sb("w_hi", [P, KD, W_ALL], F32R)
        w_lo = sb("w_lo", [P, KD, W_ALL], F32R)
        x_in = sb("x_in", [P, 2, CH, DM])
        xn = sb("xn", [P, CH, DM])
        xnT_hi = sb("xnT_hi", [P, KD, TOK], F32R)
        xnT_lo = sb("xnT_lo", [P, KD, TOK], F32R)
        raw = sb("raw", [P, MX, TOK + HIST])
        hist = sb("hist", [P, 2, MX, HIST])
        acc = sb("acc", [P, MX, TOK])
        bcT = sb("bcT", [P, 2, 2, TOK])
        b_tok = sb("b_tok", [P, 2, CH, NST])
        x_tok = sb("x_tok", [P, 2, CH, DI])
        zs = sb("zs", [P, 2, CH, DI])
        e_buf = sb("e_buf", [P, NQ, QUAD, P])
        xdt = sb("xdt", [P, DI])
        xdd = sb("xdd", [P, DI])
        xd = sb("xd", [P, DI])
        y = sb("y", [P, 2, DI])
        state = sb("state", [P, 2, DI])
        cbm = sb("cbm", [P, 2, P])
        ident = sb("ident", [P, P])
        tri = sb("tri", [P, P])
        ones = sb("ones", [P, P])
        sel = sb("sel", [48, HEADS], F32R)
        acsT = sb("acsT", [48, 2, TOK], F32R)
        st = sb("st", [P, 2, CH, 6])
        mv = sb("mv", [P, 2, CH, 2])
        rstd = sb("rstd", [P, 2, CH])
        eps_t = sb("eps_t", [P, CH])
        pace = sb("pace", [P, 1])
        power_t = sb("power_t", [P, CH])
        v = sb("v", [P, 2, CH, HEADS])
        nabs = sb("nabs", [P, 2, CH, HEADS])
        ex = sb("ex", [P, 2, CH, HEADS])
        ln1p = sb("ln1p", [P, 2, CH, HEADS])
        dt = sb("dt", [P, 2, CH, HEADS])
        a = sb("a", [P, 2, CH, HEADS])
        cum = sb("cum", [P, 2, 3, CH, HEADS])
        ecum = sb("ecum", [P, 2, 3, CH, HEADS])
        neg_a = sb("neg_a", [P, 1, HEADS])
        bias_dt = sb("bias_dt", [HEADS, 1])
        vT = sb("vT", [P, TOK])
        d_b = sb("d_b", [P, HEADS])
        cw = sb("cw", [P, MX, TAPS])
        cb = sb("cb", [P, MX])

        ps_t = ps("ps_t")
        ps_x = [ps(f"ps_x{i}") for i in range(2)]
        ps_b = [ps(f"ps_b{i}") for i in range(2)]
        ps_y = [ps(f"ps_y{i}") for i in range(2)]
        ps_i = ps("ps_i")

        w_load = [sem(f"w_load{i}") for i in range(2)]
        c_load = sem("c_load")
        w_hi_done = sem("w_hi_done")
        w_lo_done = sem("w_lo_done")
        setup = sem("setup")
        setup_act = sem("setup_act")

        def stage(k):
            t = x_tok if k % 2 == 0 else zs
            return t[:, :, :, :].rearrange("p b c d -> p (b c d)")[:, 0:W_ALL]

        with nc.Block() as block:
            @block.sync
            def _(sp):
                for k in range(KD):
                    if k >= 2:
                        sp.wait_ge(w_lo_done, k - 1)
                    sp.dma_start(stage(k), w_in[k * P:(k + 1) * P, :]).then_inc(w_load[k % 2], 16)
                sp.dma_start(ident[:, :], ident_d).then_inc(c_load, 16)
                sp.dma_start(tri[:, :], tri_d).then_inc(c_load, 16)
                sp.dma_start(neg_a[:, 0, :], a_log.partition_broadcast(P)).then_inc(c_load, 16)
                sp.dma_start(bias_dt[:, :], dt_bias.unsqueeze(1)).then_inc(c_load, 16)
                sp.dma_start(d_b[:, :], d_skip.partition_broadcast(P)).then_inc(c_load, 16)
                sp.dma_start(cw[:, :, :], conv_w.rearrange("(m p) k -> p m k", p=P)).then_inc(c_load, 16)
                sp.dma_start(cb[:, :], conv_b.rearrange("(m p) -> p m", p=P),
                             allow_slow_non_contiguous=True).then_inc(c_load, 16)

            @block.scalar
            def _(act):
                for k in range(KD):
                    act.wait_ge(w_load[k % 2], 16 * (k // 2 + 1))
                    act.activation(w_hi[:, k, :], stage(k), ACT.Copy).then_inc(w_hi_done, 1)
                act.wait_ge(c_load, 16 * 7)
                act.activation(neg_a[:, 0, :], neg_a[:, 0, :], ACT.Exp).then_inc(setup_act, 1)

            @block.vector
            def _(dve):
                dve.memset(state[:, :, :], 0.0).then_inc(setup, 1)
                dve.memset(raw[:, :, 0:HIST], 0.0).then_inc(setup, 1)
                dve.memset(hist[:, :, :, :], 0.0).then_inc(setup, 1)
                dve.memset(ones[:, :], 1.0).then_inc(setup, 1)
                dve.memset(acsT[:, :, :].bitcast(F32), 0.0).then_inc(setup, 1)
                dve.memset(sel[:, :].bitcast(F32), 0.0).then_inc(setup, 1)
                dve.memset(eps_t[:, :], LN_EPS).then_inc(setup, 1)
                dve.memset(power_t[:, :], -0.5).then_inc(setup, 1)
                dve.memset(vT[:, :], 0.0).then_inc(setup, 1)
                dve.wait_ge(setup, 9)
                for k in range(KD):
                    dve.wait_ge(w_hi_done, k + 1)
                    dve.tensor_tensor(w_lo[:, k, :], stage(k), w_hi[:, k, :].bitcast(F32),
                                      ALU.subtract).then_inc(w_lo_done, 1)
                dve.wait_ge(c_load, 16 * 7)
                dve.tensor_copy(sel[0:HEADS, :], ident[0:HEADS, 0:HEADS]).then_inc(setup, 1)
                dve.tensor_copy(sel[32:32 + HEADS, :], ident[32:32 + HEADS, 32:32 + HEADS]).then_inc(setup, 1)
                dve.wait_ge(setup_act, 1)
                dve.tensor_scalar(neg_a[:, 0, :], neg_a[:, 0, :], -1.0, None, ALU.mult).then_inc(setup, 1)

        x_loaded = [sig(f"x_loaded{b}", 8) for b in range(2)]
        ln_step = sig("ln_step", 4)
        rstd_eps = sig("rstd_eps", 1)
        rstd_ready = sig("rstd_ready", 1)
        xn_ready = sig("xn_ready", 2)
        xnT_ps = sig("xnT_ps", 2)
        hi_ready = sig("hi_ready", 2)
        lo_ready = sig("lo_ready", 2)
        dt_ps = sig("dt_ps", 1)
        dt_vT = sig("dt_vT", 1)
        vT_ps = sig("vT_ps", 1)
        dt_v = sig("dt_v", 1)
        dt_nabs = sig("dt_nabs", 1)
        dt_ex = sig("dt_ex", 1)
        dt_ln = sig("dt_ln", 1)
        dt_ready = sig("dt_ready", 1)
        a_ready = sig("a_ready", 1)
        cum_ps = sig("cum_ps", 1)
        cum_step = sig("cum_step", 4)
        cum_ready = sig("cum_ready", 1)
        ecum_ready = sig("ecum_ready", 1)
        x_ps = sig("x_ps", PAIRS)
        raw_ready = sig("raw_ready", PAIRS)
        tap_ready = sig("tap_ready", PAIRS)
        conv_step = sig("conv_step", MX * (TAPS - 1))
        hist_done = sig("hist_done", 2)
        xc_ready = sig("xc_ready", PAIRS)
        xT_ps = sig("xT_ps", PAIRS)
        x_tok_ready = sig("x_tok_ready", PAIRS)
        z_ps = sig("z_ps", CH * G2)
        z_copied = sig("z_copied", CH * G2)
        zs_ready = sig("zs_ready", 1)
        cb_ps = sig("cb_ps", CH)
        cbm_ready = sig("cbm_ready", CH)
        bc_ps = sig("bc_ps", CH * NQ)
        seg_ready = sig("seg_ready", CH * NQ)
        e_ready = sig("e_ready", CH * NQ)
        s_ready = sig("s_ready", CH * NQ)
        off_ps = sig("off_ps", CH * G2)
        y_off = sig("y_off", CH * G2)
        st_ps = sig("st_ps", CH * G2)
        st_decayed = sig("st_decayed", CH)
        st_added = sig("st_added", CH * G2)
        intra_ps = sig("intra_ps", CH * NQ)
        y_intra = sig("y_intra", CH * G2)
        xdt_ready = sig("xdt_ready", CH)
        xdd_ready = sig("xdd_ready", CH)
        xd_ready = sig("xd_ready", CH)
        y_skip = sig("y_skip", CH)
        y_ready = sig("y_ready", CH)
        y_stored = [sig(f"y_stored{c}", 16) for c in range(CH)]

        x_v = x.rearrange("b (i c p) d -> b i p c d", c=CH, p=P)
        yg_v = yg.rearrange("b (i c p) d -> b i c p d", c=CH, p=P)

        X_ORDER = ([("x", i) for i in range(PAIRS)] + [("dt", 0)] + [("z", i) for i in range(CH * G2)]
                   + [("cum", 0)] + [("xT", i) for i in range(PAIRS)])
        NX = len(X_ORDER)
        X_FREED = {"dt": dt_vT, "x": tap_ready, "cum": cum_ready, "z": z_copied, "xT": x_tok_ready}
        def x_bank(u, use):
            return ps_x[(u.b * NX + X_ORDER.index(use)) % 2]

        with nc.Block() as block:
            @block.sync
            def _(sp):
                def load(u):
                    if u.exists():
                        wait(sp, xn_ready, u.back(2), CH)
                        sp.dma_start(x_in[:, u.b, :, :], x_v[u.b, u.it]).then_inc(x_loaded[u.b].sem, 16)

                def step(u):
                    load(u.ahead(2))
                    for c in range(CH):
                        wait(sp, y_ready, u, c + 1)
                        sp.dma_start(yg_v[u.b, u.it, c], y[:, c, :]).then_inc(y_stored[c].sem, 16)

                for n in range(2):
                    load(Unit(0, 0).ahead(n))
                over_units(sp, step)
                for c in range(CH):
                    sp.wait_ge(y_stored[c].sem, 16 * UNITS)

            @block.gpsimd
            def _(pool):
                def ln_root(u):
                    if u.exists():
                        wait(pool, ln_step, u, 4)
                        wait(pool, xn_ready, u.back(2), CH)
                        inverse_root(pool, rstd[:, u.b, :], mv[:, u.b, :, 1], eps_t[:, :],
                                     power_t[:, :], u, rstd_eps, rstd_ready)

                def step(u):
                    for c in range(CH):
                        if c == 1:
                            ln_root(u.ahead(2))
                        if c == 0:
                            wait(pool, x_tok_ready, u, PAIRS)
                        wait(pool, y_skip, u, c)
                        pool.tensor_tensor(
                            xd[:, :].rearrange("p (h d) -> p h d", d=HD),
                            x_tok[:, u.b, c, :].rearrange("p (h d) -> p h d", d=HD),
                            d_b[:, :].unsqueeze(2).to_broadcast([P, HEADS, HD]),
                            ALU.mult).then_inc(xd_ready.sem, 1)

                ln_root(Unit(0, 0))
                ln_root(Unit(0, 1))
                over_units(pool, step)

            @block.tensor
            def _(pe):
                def x_free(u, use):
                    j = X_ORDER.index(use) - 2
                    w = u if j >= 0 else u.back(1)
                    kind, i = X_ORDER[j % NX]
                    wait(pe, X_FREED[kind], w, i + 1)

                def transpose_xn(u, c):
                    if not u.exists():
                        return
                    wait(pe, xn_ready, u, c + 1)
                    if c == 0:
                        wait(pe, dt_v, u.back(1), 1)
                    else:
                        wait(pe, lo_ready, u, c)
                    for k in range(KD):
                        ins = pe.transpose(ps_t[:, k * P:(k + 1) * P], xn[:, c, k * P:(k + 1) * P],
                                           ident[:, :])
                    ins.then_inc(xnT_ps.sem, 1)

                def xn_parts(c0, n):
                    return [[t[:, k, c0:c0 + n] for k in range(KD)] for t in (xnT_hi, xnT_lo)]

                def w_parts(c0, n):
                    return [[t[:, k, c0:c0 + n] for k in range(KD)] for t in (w_hi, w_lo)]

                def project_dt(u):
                    x_free(u, ("dt", 0))
                    mm3(pe, x_bank(u, ("dt", 0))[0:HEADS, 0:TOK], w_parts(DT0, HEADS),
                        xn_parts(0, TOK)).then_inc(dt_ps.sem, 1)

                def transpose_dt(u):
                    wait(pe, dt_vT, u, 1)
                    for c in range(CH):
                        ins = pe.transpose(ps_t[:, c * P:(c + 1) * P], vT[:, c * P:(c + 1) * P], ident[:, :])
                    ins.then_inc(vT_ps.sem, 1)

                def project_x(u, i):
                    x_free(u, ("x", i))
                    if i == 0:
                        wait(pe, lo_ready, u, CH)
                    bank = x_bank(u, ("x", i))
                    for m in (2 * i, 2 * i + 1):
                        ins = mm3(pe, bank[:, (m % 2) * TOK:(m % 2 + 1) * TOK],
                                  w_parts(X0 + m * P, P), xn_parts(0, TOK))
                    ins.then_inc(x_ps.sem, 1)

                def cumulate(u):
                    x_free(u, ("cum", 0))
                    wait(pe, a_ready, u, 1)
                    bank = x_bank(u, ("cum", 0))
                    a_u = a[:, u.b, :, :].rearrange("p c h -> p (c h)")
                    pe.matmul(bank[:, 0:CH * HEADS], tri[:, :], a_u, start=True, stop=True)
                    pe.matmul(bank[:, 32:32 + CH * HEADS], ones[:, :], a_u, start=True, stop=True)
                    for c in range(CH):
                        ins = pe.matmul(bank[0:HEADS, (c + 1) * P:(c + 2) * P], a[:, u.b, c, :], tri[:, :],
                                        start=True, stop=True)
                    ins.then_inc(cum_ps.sem, 1)

                def project_z(u, i):
                    x_free(u, ("z", i))
                    c, g = divmod(i, G2)
                    mm3(pe, x_bank(u, ("z", i))[:, :], xn_parts(c * P, P),
                        w_parts(Z0 + g * 512, 512)).then_inc(z_ps.sem, 1)

                def transpose_x(u, i):
                    x_free(u, ("xT", i))
                    bank = x_bank(u, ("xT", i))
                    wait(pe, xc_ready, u, i + 1)
                    if i < PAIRS - 1:
                        for c in range(CH):
                            for m in range(2):
                                o = (c * 2 + m) * P
                                ins = pe.transpose(bank[:, o:o + P], acc[:, 2 * i + m, c * P:(c + 1) * P],
                                                   ident[:, :])
                    else:
                        for c in range(CH):
                            ins = pe.transpose(bank[:, c * P:(c + 1) * P], bcT[:, u.b, 0, c * P:(c + 1) * P],
                                               ident[:, :])
                    ins.then_inc(xT_ps.sem, 1)

                def y_bank(c, i):
                    return ps_y[(c * 5 + i) % 2]

                def c_dot_b(u, c):
                    if c == 0:
                        wait(pe, xc_ready, u, PAIRS)
                    wait(pe, st_added, u, G2 * c - 1)
                    s = slice(c * P, (c + 1) * P)
                    pe.matmul(y_bank(c, 0)[:, 0:P], bcT[:, u.b, 0, s], bcT[:, u.b, 1, s],
                              start=True, stop=True).then_inc(cb_ps.sem, 1)

                def broadcast(u, c, q):
                    if not u.exists():
                        return
                    wait(pe, seg_ready, u, c * NQ + q - 1)
                    if c == 0 and q == 0:
                        wait(pe, cum_ready, u, 1)
                    for h in range(QUAD):
                        ins = pe.matmul(ps_b[q % 2][:, h * P:(h + 1) * P],
                                        sel[:, q * QUAD + h:q * QUAD + h + 1].to_broadcast([48, P]),
                                        acsT[:, u.b, c * P:(c + 1) * P], start=True, stop=True)
                    ins.then_inc(bc_ps.sem, 1)

                def off_diagonal(u, c, g):
                    wait(pe, st_added, u.back(1 + 1), 2 * G2) if c == 0 else None
                    wait(pe, st_added, u, G2 * c)
                    if g == 1:
                        wait(pe, cbm_ready, u, c + 1)
                    pe.matmul(y_bank(c, 1 + g)[:, :], bcT[:, u.b, 1, c * P:(c + 1) * P],
                              state[:, u.b, g * 512:(g + 1) * 512], start=True, stop=True
                              ).then_inc(off_ps.sem, 1)

                def new_state(u, c, g):
                    wait(pe, y_off, u, G2 * c + g + 1)
                    wait(pe, xdd_ready, u, c + 1)
                    if c == 0 and g == 0:
                        wait(pe, x_tok_ready, u, PAIRS)
                    pe.matmul(y_bank(c, 3 + g)[:, :], b_tok[:, u.b, c, :], xdd[:, g * 512:(g + 1) * 512],
                              start=True, stop=True).then_inc(st_ps.sem, 1)

                def intra(u, c, q):
                    if q % 2 == 0:
                        wait(pe, y_intra, u, G2 * c + q // 2)
                    if q == 0:
                        wait(pe, xdt_ready, u, c + 1)
                    wait(pe, s_ready, u, c * NQ + q + 1)
                    for h in range(QUAD):
                        hh = q * QUAD + h
                        o = (hh % 8) * HD
                        ins = pe.matmul(ps_i[:, o:o + HD], e_buf[:, q, h, :],
                                        xdt[:, hh * HD:(hh + 1) * HD], start=True, stop=True)
                    ins.then_inc(intra_ps.sem, 1)

                def step(u):
                    n = u.ahead(1)
                    more = n.exists()

                    def next_x(i):
                        if more:
                            project_x(n, i)

                    def next_z(i):
                        if more:
                            project_z(n, i)

                    def next_turned(i):
                        if more:
                            transpose_x(n, i)

                    next_x(0)
                    c_dot_b(u, 0)
                    next_x(1)
                    next_x(2)
                    off_diagonal(u, 0, 0)
                    next_x(3)
                    off_diagonal(u, 0, 1)
                    intra(u, 0, 0)
                    intra(u, 0, 1)
                    new_state(u, 0, 0)
                    next_x(4)
                    new_state(u, 0, 1)
                    broadcast(u, 1, 0)
                    if more:
                        project_dt(n)
                    intra(u, 0, 2)
                    intra(u, 0, 3)
                    next_z(0)
                    c_dot_b(u, 1)
                    broadcast(u, 1, 1)
                    next_z(1)
                    if more:
                        transpose_dt(n)
                    next_z(2)
                    off_diagonal(u, 1, 0)
                    off_diagonal(u, 1, 1)
                    next_z(3)
                    intra(u, 1, 0)
                    intra(u, 1, 1)
                    broadcast(u, 1, 2)
                    if more:
                        cumulate(n)
                    transpose_xn(n.ahead(1), 0)
                    broadcast(u, 1, 3)
                    new_state(u, 1, 0)
                    new_state(u, 1, 1)
                    next_turned(0)
                    next_turned(1)
                    transpose_xn(n.ahead(1), 1)
                    next_turned(2)
                    intra(u, 1, 2)
                    intra(u, 1, 3)
                    broadcast(n, 0, 0)
                    next_turned(3)
                    broadcast(n, 0, 1)
                    next_turned(4)
                    broadcast(n, 0, 2)
                    broadcast(n, 0, 3)

                u0 = Unit(0, 0)
                for c in range(CH):
                    transpose_xn(u0, c)
                for i in range(PAIRS):
                    project_x(u0, i)
                project_dt(u0)
                for i in range(CH * G2):
                    project_z(u0, i)
                    if i == 1:
                        transpose_dt(u0)
                for c in range(CH):
                    transpose_xn(u0.ahead(1), c)
                cumulate(u0)
                for i in range(PAIRS):
                    transpose_x(u0, i)
                for q in range(NQ):
                    broadcast(u0, 0, q)
                over_units(pe, step)

            @block.scalar
            def _(act):
                def xn_high(u, c):
                    if not u.exists():
                        return
                    wait(act, xnT_ps, u, c + 1)
                    wait(act, z_ps, u.back(1), CH * G2)
                    act.activation(xnT_hi[:, :, c * P:(c + 1) * P],
                                   ps_t[:, :].rearrange("p (k t) -> p k t", k=KD),
                                   ACT.Copy).then_inc(hi_ready.sem, 1)

                def softplus(u):
                    wait(act, dt_nabs, u, 1)
                    act.activation(ex[:, u.b], nabs[:, u.b], ACT.Exp).then_inc(dt_ex.sem, 1)
                    wait(act, dt_ex, u, 1)
                    act.activation(ln1p[:, u.b], ex[:, u.b], ACT.Ln, bias=1.0).then_inc(dt_ln.sem, 1)

                def exp_cum(u):
                    wait(act, cum_ready, u, 1)
                    act.activation(ecum[:, u.b], cum[:, u.b], ACT.Exp).then_inc(ecum_ready.sem, 1)

                def raw_copy(u, i):
                    wait(act, x_ps, u, i + 1)
                    wait(act, hist_done, u.back(1), 2)
                    act.activation(raw[:, 2 * i:2 * i + 2, HIST:HIST + TOK],
                                   x_bank(u, ("x", i))[:, :].rearrange("p (m t) -> p m t", m=2),
                                   ACT.Copy).then_inc(raw_ready.sem, 1)
                    wait(act, xT_ps, u.back(1), min(i + 1, 4))
                    if i == 4:
                        wait(act, xc_ready, u.back(1), PAIRS)
                    for s in range(2):
                        m = 2 * i + s
                        ins = act.activation(acc[:, m, :], x_bank(u, ("x", i))[:, s * TOK:(s + 1) * TOK],
                                             ACT.Identity, bias=cb[:, m:m + 1],
                                             scale=cw[:, m, TAPS - 1:TAPS])
                    ins.then_inc(tap_ready.sem, 1)

                def silu_x(u, i):
                    wait(act, conv_step, u, 2 * (TAPS - 1) * (i + 1))
                    src = acc[:, 2 * i:2 * i + 2, :]
                    dst = src if i < PAIRS - 1 else bcT[:, u.b, :, :]
                    act.activation(dst, src, ACT.Silu).then_inc(xc_ready.sem, 1)

                def x_tok_copy(u, i):
                    wait(act, xT_ps, u, i + 1)
                    if i < PAIRS - 1:
                        act.activation(x_tok[:, u.b, :, i * 256:(i + 1) * 256],
                                       x_bank(u, ("xT", i))[:, :].rearrange("p (c d) -> p c d", c=CH),
                                       ACT.Copy).then_inc(x_tok_ready.sem, 1)
                    else:
                        act.activation(b_tok[:, u.b, :, :],
                                       x_bank(u, ("xT", i))[:, 0:CH * P].rearrange("p (c d) -> p c d", c=CH),
                                       ACT.Copy).then_inc(x_tok_ready.sem, 1)

                def z_copy(u, i):
                    c, g = divmod(i, G2)
                    wait(act, z_ps, u, i + 1)
                    wait(act, y_ready, u.back(2), CH)
                    act.activation(zs[:, u.b, c, g * 512:(g + 1) * 512], x_bank(u, ("z", i))[:, :],
                                   ACT.Copy).then_inc(z_copied.sem, 1)

                def silu_z(u):
                    wait(act, z_copied, u, CH * G2)
                    act.activation(zs[:, u.b], zs[:, u.b], ACT.Silu).then_inc(zs_ready.sem, 1)

                def decay(u, c, q):
                    if not u.exists():
                        return
                    wait(act, bc_ps, u, c * NQ + q + 1)
                    wait(act, intra_ps, u, c * NQ + q - (NQ - 1))
                    for h in range(QUAD):
                        ins = act.activation(e_buf[:, q, h, :], ps_b[q % 2][:, h * P:(h + 1) * P],
                                             ACT.Relu, bias=cum[:, u.b, 0, c, q * QUAD + h:q * QUAD + h + 1],
                                             scale=-1.0)
                    ins.then_inc(seg_ready.sem, 1)
                    wait(act, seg_ready, u, c * NQ + q + 1)
                    act.activation(e_buf[:, q], e_buf[:, q], ACT.Exp, scale=-1.0
                                   ).then_inc(e_ready.sem, 1)

                def step(u):
                    n = u.ahead(1)
                    more = n.exists()
                    silu_z(u)
                    if more:
                        raw_copy(n, 0)
                        for i in range(1, PAIRS):
                            raw_copy(n, i)
                            silu_x(n, i - 1)
                        z_copy(n, 0)
                        silu_x(n, 4)
                    decay(u, 1, 0)
                    if more:
                        z_copy(n, 1)
                    decay(u, 1, 1)
                    if more:
                        softplus(n)
                        z_copy(n, 2)
                        z_copy(n, 3)
                    decay(u, 1, 2)
                    if more:
                        exp_cum(n)
                        xn_high(n.ahead(1), 0)
                    decay(u, 1, 3)
                    if more:
                        x_tok_copy(n, 0)
                        x_tok_copy(n, 1)
                        xn_high(n.ahead(1), 1)
                        x_tok_copy(n, 2)
                        decay(n, 0, 0)
                        x_tok_copy(n, 3)
                        decay(n, 0, 1)
                        x_tok_copy(n, 4)
                        decay(n, 0, 2)
                        decay(n, 0, 3)

                u0 = Unit(0, 0)
                for c in range(CH):
                    xn_high(u0, c)
                raw_copy(u0, 0)
                for i in range(1, PAIRS):
                    raw_copy(u0, i)
                    silu_x(u0, i - 1)
                silu_x(u0, 4)
                for i in range(CH * G2):
                    z_copy(u0, i)
                softplus(u0)
                for c in range(CH):
                    xn_high(u0.ahead(1), c)
                exp_cum(u0)
                for i in range(PAIRS):
                    x_tok_copy(u0, i)
                for q in range(NQ):
                    decay(u0, 0, q)
                over_units(act, step)

            @block.vector
            def _(dve):
                def heads(t):
                    return t.rearrange("p (h d) -> p h d", d=HD)

                def per_head(t, n=HEADS):
                    return t.unsqueeze(2).to_broadcast([P, n, HD])

                def statistics(u):
                    if not u.exists():
                        return
                    b = u.b
                    dve.wait_ge(x_loaded[b].sem, (u.it + 1) * 16)
                    for c in range(CH):
                        dve.bn_stats(st[:, b, c, :], x_in[:, b, c, :]).then_inc(ln_step.sem, 1)
                    wait(dve, ln_step, u, CH)
                    dve.memset(pace[:, :], 0.0)
                    for c in range(CH):
                        dve.bn_aggr(mv[:, b, c, :], st[:, b, c, :]).then_inc(ln_step.sem, 1)

                def normalise(u):
                    if not u.exists():
                        return
                    b = u.b
                    wait(dve, rstd_ready, u, 1)
                    wait(dve, xnT_ps, u.back(1), CH)
                    for c in range(CH):
                        dve.tensor_scalar(xn[:, c, :], x_in[:, b, c, :], mv[:, b, c, 0:1],
                                          rstd[:, b, c:c + 1], ALU.subtract, ALU.mult
                                          ).then_inc(xn_ready.sem, 1)

                def xn_low(u, c):
                    if not u.exists():
                        return
                    wait(dve, hi_ready, u, c + 1)
                    dve.tensor_tensor(xnT_lo[:, :, c * P:(c + 1) * P],
                                      ps_t[:, :].rearrange("p (k t) -> p k t", k=KD),
                                      xnT_hi[:, :, c * P:(c + 1) * P].bitcast(F32), ALU.subtract
                                      ).then_inc(lo_ready.sem, 1)

                def dt_bias(u):
                    wait(dve, dt_ps, u, 1)
                    dve.tensor_scalar(vT[0:HEADS, :], x_bank(u, ("dt", 0))[0:HEADS, 0:TOK], bias_dt[:, 0:1], None,
                                      ALU.add).then_inc(dt_vT.sem, 1)

                def dt_first(u):
                    b = u.b
                    wait(dve, vT_ps, u, 1)
                    dve.tensor_copy(v[:, b], ps_t[:, 0:CH * P].rearrange("p (c h) -> p c h", c=CH)[:, :, 0:HEADS]
                                    ).then_inc(dt_v.sem, 1)
                    wait(dve, dt_v, u, 1)
                    dve.scalar_tensor_tensor(nabs[:, b], v[:, b], -1.0, v[:, b], ALU.mult, ALU.min
                                             ).then_inc(dt_nabs.sem, 1)

                def dt_second(u):
                    b = u.b
                    wait(dve, dt_ln, u, 1)
                    dve.scalar_tensor_tensor(dt[:, b], v[:, b], 0.0, ln1p[:, b], ALU.max, ALU.add
                                             ).then_inc(dt_ready.sem, 1)
                    wait(dve, dt_ready, u, 1)
                    dve.tensor_tensor(a[:, b], dt[:, b], neg_a[:, :, :].to_broadcast([P, CH, HEADS]),
                                      ALU.mult).then_inc(a_ready.sem, 1)

                def cum_copy(u):
                    b = u.b
                    bank = x_bank(u, ("cum", 0))
                    acs = bank[:, 0:CH * HEADS].rearrange("p (c h) -> p c h", c=CH)
                    tot = bank[:, 32:32 + CH * HEADS].rearrange("p (c h) -> p c h", c=CH)
                    accT = bank[0:HEADS, P:P + TOK]
                    wait(dve, cum_ps, u, 1)
                    dve.tensor_copy(cum[:, b, 0], acs).then_inc(cum_step.sem, 1)
                    dve.tensor_copy(acsT[0:HEADS, b, :], accT).then_inc(cum_step.sem, 1)
                    dve.tensor_copy(cum[:, b, 2], tot).then_inc(cum_step.sem, 1)
                    wait(dve, cum_step, u, 1)
                    dve.tensor_tensor(cum[:, b, 1], tot, cum[:, b, 0], ALU.subtract
                                      ).then_inc(cum_step.sem, 1)
                    wait(dve, cum_step, u, 2)
                    dve.tensor_tensor(acsT[32:32 + HEADS, b, :], accT, acsT[0:HEADS, b, :].bitcast(F32),
                                      ALU.subtract).then_inc(cum_ready.sem, 1)

                def convolve(u, i):
                    b = u.b
                    wait(dve, tap_ready, u, i + 1)
                    k0 = i * 2 * (TAPS - 1)
                    for j in range(TAPS - 1):
                        tap = TAPS - 2 - j
                        for s in range(2):
                            m = 2 * i + s
                            if j:
                                wait(dve, conv_step, u, k0 + 2 * j + s - 1)
                            dve.scalar_tensor_tensor(acc[:, m, :], raw[:, m, tap:tap + TOK],
                                                     cw[:, m, tap:tap + 1], acc[:, m, :],
                                                     ALU.mult, ALU.add).then_inc(conv_step.sem, 1)

                def keep_history(u):
                    b = u.b
                    wait(dve, conv_step, u, MX * (TAPS - 1))
                    wait(dve, hist_done, u.back(1), 2)
                    dve.tensor_copy(hist[:, b], raw[:, :, TOK:TOK + HIST]).then_inc(hist_done.sem, 1)
                    dve.tensor_copy(raw[:, :, 0:HIST], hist[:, 1 - b]).then_inc(hist_done.sem, 1)

                def mask_cb(u, c):
                    wait(dve, cb_ps, u, c + 1)
                    wait(dve, s_ready, u.back(1), (c + 1) * NQ)
                    dve.tensor_tensor(cbm[:, c, :], ps_y[(c * 5) % 2][:, 0:P], tri[:, :], ALU.mult
                                      ).then_inc(cbm_ready.sem, 1)

                def scale_inputs(u, c):
                    b = u.b
                    wait(dve, intra_ps, u, c * NQ)
                    wait(dve, st_ps, u, G2 * c)
                    if c == 0:
                        wait(dve, x_tok_ready, u, PAIRS)
                        wait(dve, ecum_ready, u, 1)
                    dve.tensor_tensor(heads(xdt[:, :]), heads(x_tok[:, b, c, :]), per_head(dt[:, b, c, :]),
                                      ALU.mult).then_inc(xdt_ready.sem, 1)
                    wait(dve, xdt_ready, u, c + 1)
                    dve.tensor_tensor(heads(xdd[:, :]), heads(xdt[:, :]), per_head(ecum[:, b, 1, c, :]),
                                      ALU.mult).then_inc(xdd_ready.sem, 1)

                def mask(u, c, q):
                    wait(dve, e_ready, u, c * NQ + q + 1)
                    if q == 0:
                        wait(dve, cbm_ready, u, c + 1)
                    e = e_buf[:, q]
                    dve.tensor_tensor(e, e, cbm[:, c:c + 1, :].to_broadcast([P, QUAD, P]), ALU.mult
                                      ).then_inc(s_ready.sem, 1)

                def from_state(u, c, g):
                    wait(dve, off_ps, u, G2 * c + g + 1)
                    if g == 0:
                        wait(dve, y_stored[c], u, 0)
                    n = HEADS // G2
                    dve.tensor_tensor(heads(y[:, c, g * 512:(g + 1) * 512]),
                                      heads(ps_y[(c * 5 + 1 + g) % 2][:, :]),
                                      per_head(ecum[:, u.b, 0, c, g * n:(g + 1) * n], n), ALU.mult
                                      ).then_inc(y_off.sem, 1)

                def decay_state(u, c):
                    wait(dve, off_ps, u, G2 * c + 2)
                    wait(dve, st_added, u, G2 * c)
                    dve.tensor_tensor(heads(state[:, u.b, :]), heads(state[:, u.b, :]),
                                      per_head(ecum[:, u.b, 2, c, :]), ALU.mult
                                      ).then_inc(st_decayed.sem, 1)

                def add_state(u, c, g):
                    wait(dve, st_ps, u, G2 * c + g + 1)
                    wait(dve, st_decayed, u, c + 1)
                    s = state[:, u.b, g * 512:(g + 1) * 512]
                    dve.tensor_tensor(s, ps_y[(c * 5 + 3 + g) % 2][:, :], s, ALU.add
                                      ).then_inc(st_added.sem, 1)

                def add_intra(u, c, g):
                    wait(dve, intra_ps, u, c * NQ + 2 * g + 2)
                    wait(dve, y_off, u, G2 * c + g + 1)
                    s = y[:, c, g * 512:(g + 1) * 512]
                    dve.tensor_tensor(s, ps_i[:, :], s, ALU.add).then_inc(y_intra.sem, 1)

                def finish(u, c):
                    wait(dve, xd_ready, u, c + 1)
                    wait(dve, y_intra, u, G2 * c + 2)
                    dve.tensor_tensor(y[:, c, :], y[:, c, :], xd[:, :], ALU.add).then_inc(y_skip.sem, 1)
                    wait(dve, y_skip, u, c + 1)
                    if c == 0:
                        wait(dve, zs_ready, u, 1)
                    dve.tensor_tensor(y[:, c, :], y[:, c, :], zs[:, u.b, c, :], ALU.mult
                                      ).then_inc(y_ready.sem, 1)

                def step(u):
                    n = u.ahead(1)
                    more = n.exists()

                    def next_conv(i):
                        if more:
                            convolve(n, i)

                    scale_inputs(u, 0)
                    next_conv(0)
                    mask_cb(u, 0)
                    mask(u, 0, 0)
                    next_conv(1)
                    mask(u, 0, 1)
                    from_state(u, 0, 0)
                    next_conv(2)
                    from_state(u, 0, 1)
                    decay_state(u, 0)
                    add_intra(u, 0, 0)
                    mask(u, 0, 2)
                    next_conv(3)
                    mask(u, 0, 3)
                    add_state(u, 0, 0)
                    next_conv(4)
                    if more:
                        keep_history(n)
                    add_state(u, 0, 1)
                    if more:
                        dt_bias(n)
                    add_intra(u, 0, 1)
                    mask_cb(u, 1)
                    mask(u, 1, 0)
                    scale_inputs(u, 1)
                    if more:
                        dt_first(n)
                        statistics(n.ahead(1))
                    finish(u, 0)
                    mask(u, 1, 1)
                    if more:
                        dt_second(n)
                    from_state(u, 1, 0)
                    from_state(u, 1, 1)
                    decay_state(u, 1)
                    if more:
                        normalise(n.ahead(1))
                    add_intra(u, 1, 0)
                    if more:
                        cum_copy(n)
                    mask(u, 1, 2)
                    if more:
                        xn_low(n.ahead(1), 0)
                    add_state(u, 1, 0)
                    add_state(u, 1, 1)
                    mask(u, 1, 3)
                    if more:
                        xn_low(n.ahead(1), 1)
                    add_intra(u, 1, 1)
                    finish(u, 1)

                u0 = Unit(0, 0)
                statistics(u0)
                normalise(u0)
                for c in range(CH):
                    xn_low(u0, c)
                statistics(u0.ahead(1))
                for i in range(PAIRS):
                    convolve(u0, i)
                keep_history(u0)
                dt_bias(u0)
                dt_first(u0)
                dt_second(u0)
                normalise(u0.ahead(1))
                for c in range(CH):
                    xn_low(u0.ahead(1), c)
                cum_copy(u0)
                over_units(dve, step)


def phase2(nc, x, yg, norm_w, w_out, w_fc, w_proj, u_t, v_lr, fast_bt, gate, ident_d, out):
    with ExitStack() as ctx:
        def sb(name, shape, dt=F32):
            return ctx.enter_context(nc.sbuf_tensor(name, shape, dt))

        def sem(name):
            return ctx.enter_context(nc.semaphore(name))

        def sig(name, per_unit):
            return Signal(sem(name), per_unit)

        wo_hi = sb("wo_hi", [P, MI, DM], F32R)
        wo_lo = sb("wo_lo", [P, MI, DM], F32R)
        fc = sb("fc", [P, KD, HID], F32R)
        proj = sb("proj", [P, MF, DM], F32R)
        lr_u = sb("lr_u", [LR, HID], F32R)
        lr_v_hi = sb("lr_v_hi", [P, KD, RANK], F32R)
        lr_v_lo = sb("lr_v_lo", [P, KD, RANK], F32R)
        y_in = sb("y_in", [P, 2, CH, DI])
        x1 = sb("x1", [P, 2, CH, DM])
        yT_hi = sb("yT_hi", [P, MI, TOK], F32R)
        yT_lo = sb("yT_lo", [P, MI, TOK], F32R)
        xn = sb("xn2", [P, CH, DM])
        xnT_hi = sb("x2T_hi", [P, KD, TOK], F32R)
        xnT_lo = sb("x2T_lo", [P, KD, TOK], F32R)
        zl = sb("zl", [LR, TOK], F32R)
        r = sb("r", [P, 2, 2, TOK])
        r_hi = sb("r_hi", [P, MF, TOK], F32R)
        r_lo = sb("r_lo", [P, MF, TOK], F32R)
        o_buf = sb("o_buf", [P, CH, DM])
        so = sb("so", [P, DM])
        sfc = sb("sfc", [P, MF])
        ident = sb("ident2", [P, P])
        ones = sb("ones2", [P, P])
        nw = sb("nw", [P, MI])
        gate_b = sb("gate_b", [P, 1])
        vr = sb("vr", [RANK, DM])
        fbt = sb("fbt", [RANK, RANK])
        st = sb("st2", [P, 2, CH, 6])
        mv = sb("mv2", [P, 2, CH, 2])
        rstd = sb("rstd2", [P, 2, CH])
        yst = sb("yst", [P, 2, CH, 2, 6])
        ymv = sb("ymv", [P, 2, CH, 2])
        msq = sb("msq", [P, 2, CH])
        eps_t = sb("eps2_t", [P, CH])
        pace = sb("pace2", [P, 1])
        power_t = sb("power2_t", [P, CH])
        rms = sb("rms", [P, 2, CH])

        banks = [ctx.enter_context(nc.psum_tensor(f"q{i}", [P, 512], F32)) for i in range(8)]
        ps_t, ps_u, ps_o, ps_d = banks[0:2], banks[2:4], banks[4:6], banks[6:8]

        piece_in = [sem(f"piece_in{i}") for i in range(2)]
        const_in = sem("const_in")
        lr_in = sem("lr_in")
        wo_in = sem("wo_in")
        zeroed = sem("zeroed")
        abs_done = sem("abs_done")
        sums_done = sem("sums_done")
        half_done = sem("half_done")
        tern_step = sem("tern_step")
        tern_done = sem("tern_done")
        col_ps = sem("col_ps")
        col_read = sem("col_read")
        lr_step = sem("lr_step")
        lr_ps = sem("lr_ps")
        wo_step = sem("wo_step")
        wo_hi_done = sem("wo_hi_done")
        wo_lo_done = sem("wo_lo_done")

        def flat(t):
            return t.rearrange("p a b -> p (a b)")

        def piece(i):
            return flat(y_in[:, i % 2])

        absw = x1[:, :, :, :].rearrange("p b c d -> p (b c d)")
        half = absw
        u_half = [flat(o_buf[0:RANK]), flat(xn[0:RANK])]
        rec = r[0:RANK, :, :, :].rearrange("p a b c -> p (a b c)")
        fc_v = w_fc.rearrange("(k p) n -> k p n", p=P)
        proj_v = w_proj.rearrange("(j f p) n -> j p f n", f=4, p=P)
        wo_v = w_out.rearrange("(m p) n -> p m n", p=P)
        wo_raw = y_in[:, :, :, :].rearrange("p b c (x n) -> p (b c x) n", n=DM)
        LR_STEPS = 10

        with nc.Block() as block:
            @block.sync
            def _(sp):
                sp.dma_start(ident[:, :], ident_d).then_inc(const_in, 16)
                sp.dma_start(gate_b[:, :], gate.partition_broadcast(P)).then_inc(const_in, 16)
                sp.dma_start(vr[:, :], v_lr).then_inc(const_in, 16)
                sp.dma_start(fbt[:, :], fast_bt).then_inc(const_in, 16)
                sp.dma_start(nw[:, :], norm_w.rearrange("(m p) -> p m", p=P),
                             allow_slow_non_contiguous=True).then_inc(const_in, 16)
                for h in range(2):
                    sp.dma_start(u_half[h], u_t[:, h * 1024:(h + 1) * 1024]).then_inc(lr_in, 16)
                for n in range(16):
                    if n >= 2:
                        before = n - 2
                        done = before // 8 * 4 + before % 4 + 1
                        sp.wait_ge(abs_done if before // 4 % 2 == 0 else tern_done, done)
                    if n < 8:
                        sp.dma_start(piece(n), fc_v[n % 4]).then_inc(piece_in[n % 2], 16)
                    else:
                        sp.dma_start(piece(n).rearrange("p (f n) -> p f n", f=4), proj_v[n % 4]
                                     ).then_inc(piece_in[n % 2], 16)
                sp.wait_ge(tern_done, 8)
                sp.dma_start(wo_raw, wo_v).then_inc(wo_in, 16)

            @block.scalar
            def _(act):
                for w in range(2):
                    for k in range(4):
                        act.wait_ge(piece_in[k % 2], 16 * (w * 4 + k // 2 + 1))
                        if w or k:
                            act.wait_ge(sums_done, w * 4 + k)
                        if w == 1 and k == 0:
                            act.wait_ge(tern_done, 4)
                            act.wait_ge(lr_step, LR_STEPS)
                            act.wait_ge(col_ps, 4)
                        act.activation(absw, piece(k), ACT.Abs).then_inc(abs_done, 1)
                act.wait_ge(wo_in, 16)
                for m in range(MI):
                    act.wait_ge(wo_step, m + 1)
                    act.activation(wo_hi[:, m, :], wo_raw[:, m, :], ACT.Copy).then_inc(wo_hi_done, 1)

            @block.tensor
            def _(pe):
                pe.wait_ge(zeroed, 1)
                pe.wait_ge(const_in, 16 * 5)
                for k in range(4):
                    pe.wait_ge(abs_done, k + 1)
                    for j in range(4):
                        ins = pe.matmul(banks[j][:, :], ones[:, :], absw[:, j * 512:(j + 1) * 512],
                                        start=(k == 0), stop=(k == 3))
                    ins.then_inc(sums_done, 1)
                for k in range(KD):
                    ins = pe.matmul(banks[7][:, k * RANK:(k + 1) * RANK], vr[:, k * P:(k + 1) * P],
                                    fbt[:, :], start=True, stop=True)
                ins.then_inc(lr_ps, 1)
                pe.wait_ge(half_done, 4)
                for j in range(4):
                    if j == 3:
                        pe.wait_ge(lr_step, 2)
                    for i in range(4):
                        m = 4 * j + i
                        ins = pe.transpose(banks[4 + j][:, i * P:(i + 1) * P],
                                           half[:, m * P:(m + 1) * P], ident[:, :])
                    ins.then_inc(col_ps, 1)
                for k in range(4):
                    pe.wait_ge(abs_done, 4 + k + 1)
                    for f in range(4):
                        ins = pe.matmul(banks[0][:, :], ones[:, :], absw[:, f * 512:(f + 1) * 512],
                                        start=(k == 0 and f == 0), stop=(k == 3 and f == 3))
                    ins.then_inc(sums_done, 1)

            @block.vector
            def _(dve):
                dve.memset(ones[:, :], 1.0).then_inc(zeroed, 1)
                dve.memset(lr_u[:, :].bitcast(F32), 0.0).then_inc(zeroed, 1)
                dve.memset(zl[:, :].bitcast(F32), 0.0).then_inc(zeroed, 1)
                dve.memset(eps_t[:, :], LN_EPS).then_inc(zeroed, 1)
                dve.memset(power_t[:, :], -0.5).then_inc(zeroed, 1)

                def ternary(i, w, src, thresholds):
                    loads = 4 * (i // 4) + 2 + i % 4 // 2 + 1
                    dve.wait_ge(piece_in[i % 2], 16 * loads)
                    dve.tensor_tensor(w, src, thresholds, ALU.is_gt).then_inc(tern_step, 1)
                    dve.scalar_tensor_tensor(src, src, -1.0, thresholds, ALU.mult, ALU.is_gt
                                             ).then_inc(tern_step, 1)
                    dve.wait_ge(tern_step, 2 * (i + 1))
                    dve.tensor_tensor(w, w.bitcast(F32), src, ALU.subtract).then_inc(tern_done, 1)

                dve.wait_ge(lr_ps, 1)
                bv = banks[7][:, 0:KD * RANK].rearrange("p (k q) -> p k q", k=KD)
                dve.tensor_copy(lr_v_hi[:, :, :], bv).then_inc(lr_step, 1)
                dve.wait_ge(lr_step, 1)
                dve.tensor_tensor(lr_v_lo[:, :, :], bv, lr_v_hi[:, :, :].bitcast(F32), ALU.subtract
                                  ).then_inc(lr_step, 1)
                dve.wait_ge(sums_done, 4)
                for j in range(4):
                    dve.tensor_scalar(half[:, j * 512:(j + 1) * 512], banks[j][:, :], 0.5 / DM, 0.5e-5,
                                      ALU.mult, ALU.max).then_inc(half_done, 1)
                dve.wait_ge(half_done, 4)
                for k in range(KD):
                    ternary(k, fc[:, k, :], piece(k), half)
                for j in range(4):
                    dve.wait_ge(col_ps, j + 1)
                    dve.tensor_scalar(sfc[:, 4 * j:4 * j + 4],
                                      banks[4 + j][:, :].rearrange("p (i t) -> p i t", i=4)[:, :, 0],
                                      2.0, None, ALU.mult).then_inc(col_read, 1)
                dve.wait_ge(lr_in, 16 * 2)
                dve.wait_ge(const_in, 16 * 5)
                dve.wait_ge(zeroed, 3)
                for h in range(2):
                    cols = slice(h * 1024, (h + 1) * 1024)
                    n = 2 + 4 * h
                    dve.reciprocal(rec, half[0:RANK, cols]).then_inc(lr_step, 1)
                    dve.wait_ge(lr_step, n + 1)
                    dve.scalar_tensor_tensor(u_half[h], u_half[h], gate_b[0:RANK, 0:1], rec,
                                             ALU.mult, ALU.mult).then_inc(lr_step, 1)
                    dve.wait_ge(lr_step, n + 2)
                    dve.tensor_scalar(u_half[h], u_half[h], 0.5, None, ALU.mult).then_inc(lr_step, 1)
                    dve.wait_ge(lr_step, n + 3)
                    dve.tensor_copy(lr_u[0:RANK, cols], u_half[h])
                    dve.tensor_copy(lr_u[32:32 + RANK, cols], u_half[h]).then_inc(lr_step, 1)
                    dve.wait_ge(lr_step, n + 4)
                    dve.tensor_tensor(lr_u[64:64 + RANK, cols], u_half[h], lr_u[0:RANK, cols].bitcast(F32),
                                      ALU.subtract).then_inc(zeroed, 1)
                dve.wait_ge(sums_done, 8)
                dve.tensor_scalar(so[:, :], banks[0][:, :], 0.5 / HID, 0.5e-5, ALU.mult, ALU.max
                                  ).then_inc(half_done, 1)
                dve.wait_ge(half_done, 5)
                for k in range(4):
                    ternary(4 + k, proj[:, 4 * k:4 * k + 4, :], piece(k).rearrange("p (f n) -> p f n", f=4),
                            so[:, :].unsqueeze(1).to_broadcast([P, 4, DM]))
                dve.wait_ge(tern_done, 8)
                dve.tensor_scalar(so[:, :], so[:, :], 2.0, None, ALU.mult).then_inc(half_done, 1)
                dve.wait_ge(wo_in, 16)
                for m in range(MI):
                    dve.tensor_scalar(wo_raw[:, m, :], wo_raw[:, m, :], nw[:, m:m + 1], None, ALU.mult
                                      ).then_inc(wo_step, 1)
                for m in range(MI):
                    dve.wait_ge(wo_hi_done, m + 1)
                    dve.tensor_tensor(wo_lo[:, m, :], wo_raw[:, m, :], wo_hi[:, m, :].bitcast(F32),
                                      ALU.subtract).then_inc(wo_lo_done, 1)

        y_loaded = [sig(f"y_loaded{s}", 8) for s in range(2)]
        xr_loaded = [sig(f"xr_loaded{s}", 8) for s in range(2)]
        stored = [sig(f"stored{c}", 16) for c in range(CH)]
        rms_step = sig("rms_step", 8)
        yT_ps = sig("yT_ps", 4)
        yT_hi_ready = sig("yT_hi_ready", 4)
        yT_lo_ready = sig("yT_lo_ready", 4)
        o_ps = sig("o_ps", CH)
        x1_ready = sig("x1_ready", CH)
        ln_step = sig("ln2_step", 4)
        rstd_eps = sig("rstd2_eps", 1)
        rstd_ready = sig("rstd2_ready", 1)
        rms_eps = sig("rms_eps", 1)
        rms_ready = sig("rms_ready", 1)
        xn_ready = sig("xn2_ready", CH)
        xT_ps = sig("x2T_ps", CH)
        xT_hi_ready = sig("x2T_hi_ready", CH)
        xT_lo_ready = sig("x2T_lo_ready", CH)
        zl_ps = sig("zl_ps", 1)
        zl_step = sig("zl_step", 2)
        zl_ready = sig("zl_ready", 1)
        up_ps = sig("up_ps", MF // 2)
        relu_done = sig("relu_done", MF // 2)
        sq_ready = sig("sq_ready", MF // 2)
        r_hi_ready = sig("r_hi_ready", MF // 2)
        r_lo_ready = sig("r_lo_ready", MF // 2)
        down_ps = sig("down_ps", CH)
        scaled = sig("scaled", CH)
        out_ready = sig("out_ready", CH)

        x_v = x.rearrange("b (i s c p) d -> (b i) s p c d", s=2, c=CH, p=P)
        y_v = yg.rearrange("b (i s c p) d -> (b i) s p c d", s=2, c=CH, p=P)
        out_v = out.rearrange("b (i s c p) d -> (b i) s c p d", s=2, c=CH, p=P)

        with nc.Block() as block:
            @block.sync
            def _(sp):
                def load(u):
                    if not u.exists():
                        return
                    wait(sp, yT_ps, u.back(2), 4)
                    wait(sp, rms_step, u.back(2), 4)
                    sp.dma_start(y_in[:, u.b], y_v[u.it, u.b]).then_inc(y_loaded[u.b].sem, 16)
                    wait(sp, out_ready, u.back(2), CH)
                    sp.dma_start(x1[:, u.b], x_v[u.it, u.b]).then_inc(xr_loaded[u.b].sem, 16)

                def step(u):
                    for c in range(CH):
                        wait(sp, out_ready, u, c + 1)
                        sp.dma_start(out_v[u.it, u.b, c], o_buf[:, c, :]).then_inc(stored[c].sem, 16)
                    load(u.ahead(2))

                load(Unit(0, 0))
                load(Unit(0, 1))
                over_units(sp, step)
                for c in range(CH):
                    sp.wait_ge(stored[c].sem, 16 * UNITS)

            @block.gpsimd
            def _(pool):
                def roots(u):
                    if not u.exists():
                        return
                    wait(pool, rms_step, u, 8)
                    wait(pool, x1_ready, u.back(2), CH)
                    inverse_root(pool, rms[:, u.b, :], msq[:, u.b, :], eps_t[:, :], power_t[:, :],
                                 u, rms_eps, rms_ready)
                    wait(pool, ln_step, u, 4)
                    wait(pool, xn_ready, u.back(2), CH)
                    inverse_root(pool, rstd[:, u.b, :], mv[:, u.b, :, 1], eps_t[:, :], power_t[:, :],
                                 u, rstd_eps, rstd_ready)

                roots(Unit(0, 0))
                over_units(pool, lambda u: roots(u.ahead(1)))

            @block.tensor
            def _(pe):
                def parts(hi, lo, n, c0, w):
                    return [[t[:, k, c0:c0 + w] for k in range(n)] for t in (hi, lo)]

                def transpose_y(u, i):
                    if i == 0:
                        pe.wait_ge(y_loaded[u.b].sem, (u.it + 1) * 16)
                    if i < 2:
                        wait(pe, xT_lo_ready, u.back(1), i + 1)
                    else:
                        wait(pe, yT_lo_ready, u, i - 1)
                    for m in range(2):
                        for c in range(CH):
                            o = (m * CH + c) * P
                            ins = pe.transpose(ps_t[i % 2][:, o:o + P],
                                               y_in[:, u.b, c, (2 * i + m) * P:(2 * i + m + 1) * P],
                                               ident[:, :])
                    ins.then_inc(yT_ps.sem, 1)

                def project_out(u, c):
                    if c == 0:
                        wait(pe, yT_lo_ready, u, 4)
                        wait(pe, zl_ready, u.back(1), 1)
                    else:
                        wait(pe, x1_ready, u.back(1), c + 1)
                    mm3(pe, ps_o[c][:, :], parts(yT_hi, yT_lo, MI, c * P, P),
                        parts(wo_hi, wo_lo, MI, 0, DM)).then_inc(o_ps.sem, 1)

                def transpose_xn(u, c):
                    wait(pe, xn_ready, u, c + 1)
                    wait(pe, yT_lo_ready, u, 3 + c)
                    for k in range(KD):
                        ins = pe.transpose(ps_t[c][:, k * P:(k + 1) * P], xn[:, c, k * P:(k + 1) * P],
                                           ident[:, :])
                    ins.then_inc(xT_ps.sem, 1)

                def low_rank(u):
                    wait(pe, xT_lo_ready, u, CH)
                    wait(pe, x1_ready, u, 1)
                    mm3(pe, ps_o[0][0:RANK, 0:TOK], parts(lr_v_hi, lr_v_lo, KD, 0, RANK),
                        parts(xnT_hi, xnT_lo, KD, 0, TOK)).then_inc(zl_ps.sem, 1)

                def up(u, i):
                    if i == 0:
                        wait(pe, zl_ready, u, 1)
                    wait(pe, relu_done, u, i - 1)
                    for j in range(2):
                        m = 2 * i + j
                        dst = ps_u[i % 2][:, j * TOK:(j + 1) * TOK]
                        for k in range(KD):
                            w = fc[:, k, m * P:(m + 1) * P]
                            pe.matmul(dst, w, xnT_hi[:, k, :], start=(k == 0), stop=False)
                            pe.matmul(dst, w, xnT_lo[:, k, :], start=False, stop=False)
                        ins = pe.matmul(dst, lr_u[:, m * P:(m + 1) * P], zl[:, :], start=False, stop=True)
                    ins.then_inc(up_ps.sem, 1)

                def down(u, c):
                    wait(pe, scaled, u.back(1), c + 1)
                    for f in range(MF):
                        if c == 0 and f % 2 == 0:
                            wait(pe, r_lo_ready, u, f // 2 + 1)
                        for t in (r_hi, r_lo):
                            ins = pe.matmul(ps_d[c][:, :], t[:, f, c * P:(c + 1) * P], proj[:, f, :],
                                            start=(f == 0 and t is r_hi), stop=(f == MF - 1 and t is r_lo))
                    ins.then_inc(down_ps.sem, 1)

                def step(u):
                    n = u.ahead(1)
                    more = n.exists()
                    for i in range(MF // 2):
                        up(u, i)
                        if more and i % 2 == 1:
                            transpose_y(n, i // 2)
                    if more:
                        for c in range(CH):
                            project_out(n, c)
                    for c in range(CH):
                        down(u, c)
                    if more:
                        for c in range(CH):
                            transpose_xn(n, c)
                        low_rank(n)

                u0 = Unit(0, 0)
                for i in range(4):
                    transpose_y(u0, i)
                for c in range(CH):
                    project_out(u0, c)
                for c in range(CH):
                    transpose_xn(u0, c)
                low_rank(u0)
                over_units(pe, step)

            @block.scalar
            def _(act):
                def y_high(u, i):
                    wait(act, yT_ps, u, i + 1)
                    wait(act, o_ps, u.back(1), CH)
                    act.activation(flat(yT_hi[:, 2 * i:2 * i + 2, :]), ps_t[i % 2][:, :], ACT.Copy
                                   ).then_inc(yT_hi_ready.sem, 1)

                def x_high(u, c):
                    wait(act, xT_ps, u, c + 1)
                    wait(act, up_ps, u.back(1), MF // 2)
                    act.activation(xnT_hi[:, :, c * P:(c + 1) * P],
                                   ps_t[c][:, :].rearrange("p (k t) -> p k t", k=KD),
                                   ACT.Copy).then_inc(xT_hi_ready.sem, 1)

                def squared_relu(u, i):
                    wait(act, up_ps, u, i + 1)
                    wait(act, r_lo_ready, u, i - 1)
                    for j in range(2):
                        m = 2 * i + j
                        ins = act.activation(r[:, i % 2, j, :], ps_u[i % 2][:, j * TOK:(j + 1) * TOK],
                                             ACT.Relu, scale=sfc[:, m:m + 1])
                    ins.then_inc(relu_done.sem, 1)
                    wait(act, relu_done, u, i + 1)
                    act.activation(r[:, i % 2], r[:, i % 2], ACT.Square).then_inc(sq_ready.sem, 1)

                def step(u):
                    n = u.ahead(1)
                    more = n.exists()
                    for i in range(MF // 2):
                        squared_relu(u, i)
                        if more and i % 2 == 1:
                            y_high(n, i // 2)
                    if more:
                        for c in range(CH):
                            x_high(n, c)

                u0 = Unit(0, 0)
                for i in range(4):
                    y_high(u0, i)
                for c in range(CH):
                    x_high(u0, c)
                over_units(act, step)

            @block.vector
            def _(dve):
                def mean_square(u):
                    b = u.b
                    dve.wait_ge(y_loaded[b].sem, (u.it + 1) * 16)
                    for c in range(CH):
                        for g in range(2):
                            dve.bn_stats(yst[:, b, c, g, :], y_in[:, b, c, g * 512:(g + 1) * 512]
                                         ).then_inc(rms_step.sem, 1)
                    wait(dve, rms_step, u, 2 * CH)
                    dve.memset(pace[:, :], 0.0)
                    for c in range(CH):
                        dve.bn_aggr(ymv[:, b, c, :], yst[:, b, c].rearrange("p g s -> p (g s)")
                                    ).then_inc(rms_step.sem, 1)
                    wait(dve, rms_step, u, 6)
                    dve.tensor_tensor(msq[:, b, :], ymv[:, b, :, 0], ymv[:, b, :, 0], ALU.mult
                                      ).then_inc(rms_step.sem, 1)
                    wait(dve, rms_step, u, 7)
                    dve.tensor_tensor(msq[:, b, :], msq[:, b, :], ymv[:, b, :, 1], ALU.add
                                      ).then_inc(rms_step.sem, 1)

                def y_low(u, i):
                    wait(dve, yT_hi_ready, u, i + 1)
                    hi = flat(yT_hi[:, 2 * i:2 * i + 2, :]).bitcast(F32)
                    dve.tensor_tensor(flat(yT_lo[:, 2 * i:2 * i + 2, :]), ps_t[i % 2][:, :], hi,
                                      ALU.subtract).then_inc(yT_lo_ready.sem, 1)

                def residual(u, c):
                    b = u.b
                    wait(dve, o_ps, u, c + 1)
                    if c == 0:
                        dve.wait_ge(xr_loaded[b].sem, (u.it + 1) * 16)
                        wait(dve, rms_ready, u, 1)
                    dve.scalar_tensor_tensor(x1[:, b, c, :], ps_o[c][:, :], rms[:, b, c:c + 1],
                                             x1[:, b, c, :], ALU.mult, ALU.add).then_inc(x1_ready.sem, 1)

                def normalise(u):
                    b = u.b
                    for c in range(CH):
                        wait(dve, x1_ready, u, c + 1)
                        dve.bn_stats(st[:, b, c, :], x1[:, b, c, :]).then_inc(ln_step.sem, 1)
                    wait(dve, ln_step, u, CH)
                    dve.memset(pace[:, :], 0.0)
                    for c in range(CH):
                        dve.bn_aggr(mv[:, b, c, :], st[:, b, c, :]).then_inc(ln_step.sem, 1)
                    wait(dve, rstd_ready, u, 1)
                    wait(dve, xT_ps, u.back(1), CH)
                    for c in range(CH):
                        dve.tensor_scalar(xn[:, c, :], x1[:, b, c, :], mv[:, b, c, 0:1],
                                          rstd[:, b, c:c + 1], ALU.subtract, ALU.mult
                                          ).then_inc(xn_ready.sem, 1)

                def x_low(u, c):
                    wait(dve, xT_hi_ready, u, c + 1)
                    dve.tensor_tensor(xnT_lo[:, :, c * P:(c + 1) * P],
                                      ps_t[c][:, :].rearrange("p (k t) -> p k t", k=KD),
                                      xnT_hi[:, :, c * P:(c + 1) * P].bitcast(F32), ALU.subtract
                                      ).then_inc(xT_lo_ready.sem, 1)

                def split_low_rank(u):
                    src = ps_o[0][0:RANK, 0:TOK]
                    wait(dve, zl_ps, u, 1)
                    dve.tensor_copy(zl[0:RANK, :], src).then_inc(zl_step.sem, 1)
                    dve.tensor_copy(zl[64:64 + RANK, :], src).then_inc(zl_step.sem, 1)
                    wait(dve, zl_step, u, 1)
                    dve.tensor_tensor(zl[32:32 + RANK, :], src, zl[0:RANK, :].bitcast(F32), ALU.subtract
                                      ).then_inc(zl_ready.sem, 1)

                def split_squares(u, i):
                    wait(dve, sq_ready, u, i + 1)
                    if i == 0:
                        wait(dve, down_ps, u.back(1), CH)
                    dve.tensor_copy(r_hi[:, 2 * i:2 * i + 2, :], r[:, i % 2]).then_inc(r_hi_ready.sem, 1)
                    wait(dve, r_hi_ready, u, i + 1)
                    dve.tensor_tensor(r_lo[:, 2 * i:2 * i + 2, :], r[:, i % 2],
                                      r_hi[:, 2 * i:2 * i + 2, :].bitcast(F32), ALU.subtract
                                      ).then_inc(r_lo_ready.sem, 1)

                def output(u, c):
                    wait(dve, down_ps, u, c + 1)
                    wait(dve, stored[c], u, 0)
                    dve.tensor_tensor(o_buf[:, c, :], ps_d[c][:, :], so[:, :], ALU.mult
                                      ).then_inc(scaled.sem, 1)
                    wait(dve, scaled, u, c + 1)
                    dve.tensor_tensor(o_buf[:, c, :], o_buf[:, c, :], x1[:, u.b, c, :], ALU.add
                                      ).then_inc(out_ready.sem, 1)

                def step(u):
                    n = u.ahead(1)
                    more = n.exists()
                    for i in range(MF // 2):
                        split_squares(u, i)
                        if more and i % 2 == 1:
                            y_low(n, i // 2)
                    if more:
                        mean_square(n)
                        for c in range(CH):
                            residual(n, c)
                        normalise(n)
                    for c in range(CH):
                        output(u, c)
                    if more:
                        for c in range(CH):
                            x_low(n, c)
                        split_low_rank(n)

                u0 = Unit(0, 0)
                for i in range(4):
                    y_low(u0, i)
                mean_square(u0)
                for c in range(CH):
                    residual(u0, c)
                normalise(u0)
                for c in range(CH):
                    x_low(u0, c)
                split_low_rank(u0)
                over_units(dve, step)


def kernel(**inputs):
    import numpy as np
    import concourse.bacc as bacc
    from concourse.bass_utils import run_bass_kernel_spmd

    def arr(name):
        return np.asarray(inputs[name])

    def turned(name):
        return np.ascontiguousarray(arr(name).T)

    data = {
        "x": arr("L0_attn_u"),
        "w_in": turned("L0_attn_in_proj_w"),
        "conv_w": arr("L0_attn_conv_w"),
        "conv_b": arr("L0_attn_conv_b"),
        "dt_bias": arr("L0_attn_dt_bias"),
        "a_log": arr("L0_attn_A_log"),
        "d_skip": arr("L0_attn_D"),
        "norm_w": arr("L0_attn_norm_w"),
        "w_out": turned("L0_attn_out_proj_w"),
        "w_fc": turned("L0_ffn_w_fc"),
        "w_proj": turned("L0_ffn_w_proj"),
        "u_t": turned("L0_ffn_u"),
        "v_lr": arr("L0_ffn_v"),
        "fast_bt": turned("L0_ffn_fast_b"),
        "gate": arr("L0_ffn_gate").reshape(1),
        "ident": np.eye(P, dtype=np.float32),
        "tri": np.triu(np.ones((P, P), np.float32)),
    }
    nc = bacc.Bacc("TRN2", target_bir_lowering=False, num_devices=1)
    d = {}
    for name, value in data.items():
        value = np.ascontiguousarray(value)
        data[name] = value
        d[name] = nc.dram_tensor(f"{name}_dram", list(value.shape), mybir.dt.from_np(value.dtype),
                                 kind="ExternalInput").ap()
    yg = nc.dram_tensor("gated_dram", [BATCH, SEQ, DI], F32, kind="Internal").ap()
    out = nc.dram_tensor("out_dram", [BATCH, SEQ, DM], F32, kind="ExternalOutput").ap()
    phase1(nc, d["x"], d["w_in"], d["conv_w"], d["conv_b"], d["dt_bias"], d["a_log"], d["d_skip"],
           d["ident"], d["tri"], yg)
    phase2(nc, d["x"], yg, d["norm_w"], d["w_out"], d["w_fc"], d["w_proj"], d["u_t"], d["v_lr"],
           d["fast_bt"], d["gate"], d["ident"], out)
    result = run_bass_kernel_spmd(nc, [{f"{name}_dram": value for name, value in data.items()}], core_ids=[0])
    return result.results[0]["out_dram"]
```

```python
from contextlib import ExitStack

import concourse.bass as bass
from concourse import mybir

P = 128
F32 = mybir.dt.float32
F32R = mybir.dt.float32r
ALU = mybir.AluOpType
ACT = mybir.ActivationFunctionType

BATCH = 2
SEQ = 4096
DM = 512
KD = DM // P
HEADS = 16
HD = 64
DI = HEADS * HD
NST = 128
TAPS = 4
HIST = TAPS - 1
MX = (DI + 2 * NST) // P
PAIRS = MX // 2
HID = 2048
MF = HID // P
MI = DI // P
RANK = 16
TOK = 256
CH = TOK // P
UNITS = BATCH * SEQ // TOK
ITERS = UNITS // 2
LN_EPS = 1e-5
QUAD = 4
NQ = HEADS // QUAD
W_ZX = 2 * DI + 2 * NST
W_ALL = W_ZX + HEADS
Z0, X0, DT0 = 0, DI, W_ZX
G2 = DI // 512
LO = 32
HL = LO + RANK
LR = 96 + RANK


class Signal:

    def __init__(self, sem, per_unit):
        self.sem, self.per_unit = sem, per_unit


class Unit:

    def __init__(self, it, b):
        self.it, self.b = it, b
        self.n = it * 2 + b

    def back(self, k):
        return Unit(self.it - k // 2, self.b) if k % 2 == 0 else Unit(
            self.it - (k - self.b + 1) // 2, 1 - self.b)

    def ahead(self, k):
        return Unit(self.it + (self.b + k) // 2, (self.b + k) % 2)

    def exists(self):
        return not isinstance(self.n, int) or 0 <= self.n < UNITS


def wait(eng, signal, unit, k):
    value = unit.n * signal.per_unit + k
    if isinstance(value, int) and value <= 0:
        return
    eng.wait_ge(signal.sem, value)


def over_units(eng, step):
    for b in range(2):
        step(Unit(0, b))
    with eng.Fori(1, ITERS - 1) as it:
        for b in range(2):
            step(Unit(it, b))
    for b in range(2):
        step(Unit(ITERS - 1, b))


def mm3(pe, out, parts_l, parts_r, first=True, last=True):
    n = len(parts_l[0])
    combos = [(0, 0), (0, 1), (1, 0)]
    ins = None
    for k in range(n):
        for j, (a, b) in enumerate(combos):
            ins = pe.matmul(out, parts_l[a][k], parts_r[b][k],
                            start=first and k == 0 and j == 0, stop=last and k == n - 1 and j == 2)
    return ins


def both_parts(pe, out, w, hi, lo):
    for k in range(KD):
        pe.matmul(out, w[:, k, :], hi[:, k, :], start=(k == 0), stop=False)
        ins = pe.matmul(out, w[:, k, :], lo[:, k, :], start=False, stop=(k == KD - 1))
    return ins


def inverse_root(pool, out, mean_square, eps_t, power_t, unit, added, ready):
    pool.tensor_tensor(out, mean_square, eps_t, ALU.add).then_inc(added.sem, 1)
    wait(pool, added, unit, 1)
    pool.tensor_tensor(out, out, power_t, ALU.pow).then_inc(ready.sem, 1)


def phase1(nc, x, w_in, conv_w, conv_b, dt_bias, a_log, d_skip, ident_d, tri_d, yg):
    with ExitStack() as ctx:
        def sb(name, shape, dt=F32):
            return ctx.enter_context(nc.sbuf_tensor(name, shape, dt))

        def ps(name):
            return ctx.enter_context(nc.psum_tensor(name, [P, 512], F32))

        def sem(name):
            return ctx.enter_context(nc.semaphore(name))

        def sig(name, per_unit):
            return Signal(sem(name), per_unit)

        w_hi = sb("w_hi", [P, KD, W_ALL], F32R)
        w_lo = sb("w_lo", [P, KD, W_ALL], F32R)
        w_dt = sb("w_dt", [P, KD, HL], F32R)
        x_in = sb("x_in", [P, 2, CH, DM])
        xn = sb("xn", [P, CH, DM])
        xnT_hi = sb("xnT_hi", [P, KD, TOK], F32R)
        xnT_lo = sb("xnT_lo", [P, KD, TOK], F32R)
        raw = sb("raw", [P, MX, TOK + HIST])
        hist = sb("hist", [P, 2, MX, HIST])
        acc = sb("acc", [P, MX, TOK])
        bcT = sb("bcT", [P, 2, 2, TOK])
        b_tok = sb("b_tok", [P, 2, CH, NST])
        y = sb("y", [P, 2, DI])
        state = sb("state", [P, 2, DI])
        cbm = sb("cbm", [P, 2, P])
        ident = sb("ident", [P, P])
        tri = sb("tri", [P, P])
        ones = sb("ones", [P, P])
        sel = sb("sel", [48, HEADS], F32R)
        acsT = sb("acsT", [48, 2, TOK], F32R)
        st = sb("st", [P, 2, CH, 6])
        mv = sb("mv", [P, 2, CH, 2])
        rstd = sb("rstd", [P, 2, CH])
        eps_t = sb("eps_t", [P, CH])
        pace = sb("pace", [P, 1])
        power_t = sb("power_t", [P, CH])
        v = sb("v", [P, 2, CH, HEADS])
        nabs = sb("nabs", [P, 2, CH, HEADS])
        ex = sb("ex", [P, 2, CH, HEADS])
        ln1p = sb("ln1p", [P, 2, CH, HEADS])
        dt = sb("dt", [P, 2, CH, HEADS])
        a = sb("a", [P, 2, CH, HEADS])
        cum = sb("cum", [P, 2, 3, CH, HEADS])
        ecum = sb("ecum", [P, 2, 3, CH, HEADS])
        neg_a = sb("neg_a", [P, 1, HEADS])
        bias_dt = sb("bias_dt", [HL, 1])
        vT = sb("vT", [P, TOK])
        d_b = sb("d_b", [P, HEADS])
        cw = sb("cw", [P, MX, TAPS])
        cb = sb("cb", [P, MX])

        ps_t = ps("ps_t")
        ps_x = [ps(f"ps_x{i}") for i in range(2)]
        ps_b = [ps(f"ps_b{i}") for i in range(2)]
        ps_y = [ps(f"ps_y{i}") for i in range(2)]
        ps_i = ps("ps_i")

        w_load = [sem(f"w_load{k}") for k in range(KD)]
        c_load = sem("c_load")
        w_hi_done = sem("w_hi_done")
        w_lo_done = sem("w_lo_done")
        setup = sem("setup")
        setup_act = sem("setup_act")
        bias_zeroed = sem("bias_zeroed")

        setup_stack = ExitStack()
        w_raw = setup_stack.enter_context(nc.sbuf_tensor("w_raw", [P, KD, W_ALL], F32))
        x_loaded = [sig(f"x_loaded{b}", 8) for b in range(2)]
        x_v = x.rearrange("b (i c p) d -> b i p c d", c=CH, p=P)

        with nc.Block() as block:
            @block.sync
            def _(sp):
                for k in range(KD):
                    sp.dma_start(w_raw[:, k, :], w_in[k * P:(k + 1) * P, :]).then_inc(w_load[k], 16)
                sp.dma_start(ident[:, :], ident_d).then_inc(c_load, 16)
                sp.dma_start(tri[:, :], tri_d).then_inc(c_load, 16)
                sp.dma_start(neg_a[:, 0, :], a_log.partition_broadcast(P)).then_inc(c_load, 16)
                sp.wait_ge(bias_zeroed, 1)
                sp.dma_start(bias_dt[0:HEADS, :], dt_bias.unsqueeze(1)).then_inc(c_load, 16)
                sp.dma_start(d_b[:, :], d_skip.partition_broadcast(P)).then_inc(c_load, 16)
                sp.dma_start(cw[:, :, :], conv_w.rearrange("(m p) k -> p m k", p=P)).then_inc(c_load, 16)
                sp.dma_start(cb[:, :], conv_b.rearrange("(m p) -> p m", p=P),
                             allow_slow_non_contiguous=True).then_inc(c_load, 16)
                for b in range(2):
                    sp.dma_start(x_in[:, b, :, :], x_v[b, 0]).then_inc(x_loaded[b].sem, 16)

            @block.scalar
            def _(act):
                for k in range(KD):
                    act.wait_ge(w_load[k], 16)
                    act.activation(w_hi[:, k, :], w_raw[:, k, :], ACT.Copy).then_inc(w_hi_done, 1)
                act.wait_ge(c_load, 16 * 7)
                act.activation(neg_a[:, 0, :], neg_a[:, 0, :], ACT.Exp).then_inc(setup_act, 1)

            @block.vector
            def _(dve):
                dve.memset(state[:, :, :], 0.0).then_inc(setup, 1)
                dve.memset(raw[:, :, 0:HIST], 0.0).then_inc(setup, 1)
                dve.memset(hist[:, :, :, :], 0.0).then_inc(setup, 1)
                dve.memset(ones[:, :], 1.0).then_inc(setup, 1)
                dve.memset(acsT[:, :, :].bitcast(F32), 0.0).then_inc(setup, 1)
                dve.memset(sel[:, :].bitcast(F32), 0.0).then_inc(setup, 1)
                dve.memset(eps_t[:, :], LN_EPS).then_inc(setup, 1)
                dve.memset(power_t[:, :], -0.5).then_inc(setup, 1)
                dve.memset(vT[:, :], 0.0).then_inc(setup, 1)
                dve.memset(w_dt[:, :, :].bitcast(F32), 0.0).then_inc(setup, 1)
                dve.memset(bias_dt[:, :], 0.0).then_inc(bias_zeroed, 1)
                dve.wait_ge(setup, 10)
                for k in range(KD):
                    dve.wait_ge(w_hi_done, k + 1)
                    dve.tensor_tensor(w_lo[:, k, :], w_raw[:, k, :], w_hi[:, k, :].bitcast(F32),
                                      ALU.subtract).then_inc(w_lo_done, 1)
                dve.wait_ge(w_lo_done, KD)
                dt_cols = slice(DT0, DT0 + HEADS)
                dve.tensor_copy(w_dt[:, :, 0:HEADS], w_hi[:, :, dt_cols].bitcast(F32)).then_inc(setup, 1)
                dve.tensor_copy(w_dt[:, :, LO:LO + HEADS], w_lo[:, :, dt_cols].bitcast(F32)
                                ).then_inc(setup, 1)
                dve.wait_ge(c_load, 16 * 7)
                dve.tensor_copy(sel[0:HEADS, :], ident[0:HEADS, 0:HEADS]).then_inc(setup, 1)
                dve.tensor_copy(sel[32:32 + HEADS, :], ident[32:32 + HEADS, 32:32 + HEADS]).then_inc(setup, 1)
                dve.wait_ge(setup_act, 1)
                dve.tensor_scalar(neg_a[:, 0, :], neg_a[:, 0, :], -1.0, None, ALU.mult).then_inc(setup, 1)

        setup_stack.close()
        x_tok = sb("x_tok", [P, 2, CH, DI])
        zs = sb("zs", [P, 2, CH, DI])
        e_buf = sb("e_buf", [P, CH, NQ, QUAD, P])
        xdt = sb("xdt", [P, DI])
        xdd = sb("xdd", [P, DI])
        xd = sb("xd", [P, DI])

        ln_step = sig("ln_step", 4)
        rstd_eps = sig("rstd_eps", 1)
        rstd_ready = sig("rstd_ready", 1)
        xn_ready = sig("xn_ready", 2)
        xnT_ps = sig("xnT_ps", 2)
        hi_ready = sig("hi_ready", 2)
        lo_ready = sig("lo_ready", 2)
        dt_ps = sig("dt_ps", 1)
        dt_vT = sig("dt_vT", 1)
        vT_ps = sig("vT_ps", 1)
        dt_half = sig("dt_half", 1)
        dt_v = sig("dt_v", 1)
        dt_nabs = sig("dt_nabs", 1)
        dt_ex = sig("dt_ex", 1)
        dt_ln = sig("dt_ln", 1)
        dt_ready = sig("dt_ready", 1)
        a_ready = sig("a_ready", 1)
        cum_ps = sig("cum_ps", 1)
        cum_step = sig("cum_step", 4)
        cum_ready = sig("cum_ready", 1)
        ecum_ready = sig("ecum_ready", 1)
        x_ps = sig("x_ps", PAIRS)
        raw_ready = sig("raw_ready", PAIRS)
        tap_ready = sig("tap_ready", PAIRS)
        conv_step = sig("conv_step", MX * (TAPS - 1))
        hist_done = sig("hist_done", 2)
        xc_ready = sig("xc_ready", PAIRS)
        xT_ps = sig("xT_ps", PAIRS)
        x_tok_ready = sig("x_tok_ready", PAIRS)
        z_ps = sig("z_ps", CH * G2)
        z_copied = sig("z_copied", CH * G2)
        zs_ready = sig("zs_ready", 1)
        cb_ps = sig("cb_ps", CH)
        cbm_ready = sig("cbm_ready", CH)
        bc_ps = sig("bc_ps", HEADS // 2)
        seg_ready = sig("seg_ready", HEADS // 2)
        e_ready = sig("e_ready", CH * NQ)
        s_ready = sig("s_ready", CH * NQ)
        off_ps = sig("off_ps", CH * G2)
        y_off = sig("y_off", CH * G2)
        st_ps = sig("st_ps", CH * G2)
        st_decayed = sig("st_decayed", CH)
        st_added = sig("st_added", CH * G2)
        intra_ps = sig("intra_ps", CH * NQ)
        y_intra = sig("y_intra", CH * G2)
        xdt_ready = sig("xdt_ready", CH)
        xdd_ready = sig("xdd_ready", CH)
        xd_ready = sig("xd_ready", CH)
        y_skip = sig("y_skip", CH)
        y_ready = sig("y_ready", CH)
        y_stored = [sig(f"y_stored{c}", 16) for c in range(CH)]

        yg_v = yg.rearrange("b (i c p) d -> b i c p d", c=CH, p=P)

        X_ORDER = ([("x", i) for i in range(PAIRS)] + [("dt", 0)] + [("z", i) for i in range(CH * G2)]
                   + [("cum", 0)] + [("xT", i) for i in range(PAIRS)])
        NX = len(X_ORDER)
        X_FREED = {"dt": dt_vT, "x": tap_ready, "cum": cum_ready, "z": z_copied, "xT": x_tok_ready}
        def x_bank(u, use):
            return ps_x[(u.b * NX + X_ORDER.index(use)) % 2]

        with nc.Block() as block:
            @block.sync
            def _(sp):
                def load(u):
                    if u.exists():
                        wait(sp, xn_ready, u.back(2), CH)
                        sp.dma_start(x_in[:, u.b, :, :], x_v[u.b, u.it]).then_inc(x_loaded[u.b].sem, 16)

                def step(u):
                    load(u.ahead(2))
                    for c in range(CH):
                        wait(sp, y_ready, u, c + 1)
                        sp.dma_start(yg_v[u.b, u.it, c], y[:, c, :]).then_inc(y_stored[c].sem, 16)

                over_units(sp, step)
                for c in range(CH):
                    sp.wait_ge(y_stored[c].sem, 16 * UNITS)

            @block.gpsimd
            def _(pool):
                def ln_root(u):
                    if u.exists():
                        wait(pool, ln_step, u, 4)
                        wait(pool, xn_ready, u.back(2), CH)
                        inverse_root(pool, rstd[:, u.b, :], mv[:, u.b, :, 1], eps_t[:, :],
                                     power_t[:, :], u, rstd_eps, rstd_ready)

                def step(u):
                    for c in range(CH):
                        if c == 1:
                            ln_root(u.ahead(2))
                        if c == 0:
                            wait(pool, x_tok_ready, u, PAIRS)
                        wait(pool, y_skip, u, c)
                        pool.tensor_tensor(
                            xd[:, :].rearrange("p (h d) -> p h d", d=HD),
                            x_tok[:, u.b, c, :].rearrange("p (h d) -> p h d", d=HD),
                            d_b[:, :].unsqueeze(2).to_broadcast([P, HEADS, HD]),
                            ALU.mult).then_inc(xd_ready.sem, 1)

                ln_root(Unit(0, 0))
                ln_root(Unit(0, 1))
                over_units(pool, step)

            @block.tensor
            def _(pe):
                def x_free(u, use):
                    j = X_ORDER.index(use) - 2
                    w = u if j >= 0 else u.back(1)
                    kind, i = X_ORDER[j % NX]
                    wait(pe, X_FREED[kind], w, i + 1)

                def transpose_xn(u, c):
                    if not u.exists():
                        return
                    wait(pe, xn_ready, u, c + 1)
                    if c == 0:
                        wait(pe, dt_v, u.back(1), 1)
                    else:
                        wait(pe, lo_ready, u, c)
                    for k in range(KD):
                        ins = pe.transpose(ps_t[:, k * P:(k + 1) * P], xn[:, c, k * P:(k + 1) * P],
                                           ident[:, :])
                    ins.then_inc(xnT_ps.sem, 1)

                def xn_parts(c0, n):
                    return [[t[:, k, c0:c0 + n] for k in range(KD)] for t in (xnT_hi, xnT_lo)]

                def w_parts(c0, n):
                    return [[t[:, k, c0:c0 + n] for k in range(KD)] for t in (w_hi, w_lo)]

                def project_dt(u):
                    x_free(u, ("dt", 0))
                    both_parts(pe, x_bank(u, ("dt", 0))[0:HL, 0:TOK], w_dt, xnT_hi, xnT_lo
                               ).then_inc(dt_ps.sem, 1)

                def transpose_dt(u):
                    wait(pe, dt_vT, u, 1)
                    for c in range(CH):
                        ins = pe.transpose(ps_t[:, c * P:(c + 1) * P], vT[:, c * P:(c + 1) * P], ident[:, :])
                    ins.then_inc(vT_ps.sem, 1)

                def project_x(u, i):
                    x_free(u, ("x", i))
                    if i == 0:
                        wait(pe, lo_ready, u, CH)
                    bank = x_bank(u, ("x", i))
                    for m in (2 * i, 2 * i + 1):
                        ins = mm3(pe, bank[:, (m % 2) * TOK:(m % 2 + 1) * TOK],
                                  w_parts(X0 + m * P, P), xn_parts(0, TOK))
                    ins.then_inc(x_ps.sem, 1)

                def cumulate(u):
                    x_free(u, ("cum", 0))
                    wait(pe, a_ready, u, 1)
                    bank = x_bank(u, ("cum", 0))
                    a_u = a[:, u.b, :, :].rearrange("p c h -> p (c h)")
                    pe.matmul(bank[:, 0:CH * HEADS], tri[:, :], a_u, start=True, stop=True)
                    pe.matmul(bank[:, 32:32 + CH * HEADS], ones[:, :], a_u, start=True, stop=True)
                    for c in range(CH):
                        ins = pe.matmul(bank[0:HEADS, (c + 1) * P:(c + 2) * P], a[:, u.b, c, :], tri[:, :],
                                        start=True, stop=True)
                    ins.then_inc(cum_ps.sem, 1)

                def project_z(u, i):
                    x_free(u, ("z", i))
                    c, g = divmod(i, G2)
                    mm3(pe, x_bank(u, ("z", i))[:, :], xn_parts(c * P, P),
                        w_parts(Z0 + g * 512, 512)).then_inc(z_ps.sem, 1)

                def transpose_x(u, i):
                    x_free(u, ("xT", i))
                    bank = x_bank(u, ("xT", i))
                    wait(pe, xc_ready, u, i + 1)
                    if i < PAIRS - 1:
                        for c in range(CH):
                            for m in range(2):
                                o = (c * 2 + m) * P
                                ins = pe.transpose(bank[:, o:o + P], acc[:, 2 * i + m, c * P:(c + 1) * P],
                                                   ident[:, :])
                    else:
                        for c in range(CH):
                            ins = pe.transpose(bank[:, c * P:(c + 1) * P], bcT[:, u.b, 0, c * P:(c + 1) * P],
                                               ident[:, :])
                    ins.then_inc(xT_ps.sem, 1)

                def y_bank(c, i):
                    return ps_y[(c * 5 + i) % 2]

                def c_dot_b(u, c):
                    if not u.exists():
                        return
                    if c == 0:
                        wait(pe, xc_ready, u, PAIRS)
                    wait(pe, st_added, u, G2 * c - 1)
                    s = slice(c * P, (c + 1) * P)
                    pe.matmul(y_bank(c, 0)[:, 0:P], bcT[:, u.b, 0, s], bcT[:, u.b, 1, s],
                              start=True, stop=True).then_inc(cb_ps.sem, 1)

                def broadcast(u, pair):
                    if not u.exists():
                        return
                    wait(pe, seg_ready, u, pair - 1)
                    if pair == 0:
                        wait(pe, cum_ready, u, 1)
                    for h in range(2):
                        head = 2 * pair + h
                        ins = pe.matmul(ps_b[pair % 2][:, h * TOK:(h + 1) * TOK],
                                        sel[:, head:head + 1].to_broadcast([48, P]),
                                        acsT[:, u.b, :], start=True, stop=True)
                    ins.then_inc(bc_ps.sem, 1)

                def off_diagonal(u, c, g):
                    wait(pe, st_added, u.back(1 + 1), 2 * G2) if c == 0 else None
                    wait(pe, st_added, u, G2 * c)
                    if g == 1:
                        wait(pe, cbm_ready, u, c + 1)
                    pe.matmul(y_bank(c, 1 + g)[:, :], bcT[:, u.b, 1, c * P:(c + 1) * P],
                              state[:, u.b, g * 512:(g + 1) * 512], start=True, stop=True
                              ).then_inc(off_ps.sem, 1)

                def new_state(u, c, g):
                    wait(pe, y_off, u, G2 * c + g + 1)
                    wait(pe, xdd_ready, u, c + 1)
                    if c == 0 and g == 0:
                        wait(pe, x_tok_ready, u, PAIRS)
                    pe.matmul(y_bank(c, 3 + g)[:, :], b_tok[:, u.b, c, :], xdd[:, g * 512:(g + 1) * 512],
                              start=True, stop=True).then_inc(st_ps.sem, 1)

                def intra(u, c, q):
                    if q % 2 == 0:
                        wait(pe, y_intra, u, G2 * c + q // 2)
                    if q == 0:
                        wait(pe, xdt_ready, u, c + 1)
                    wait(pe, s_ready, u, c * NQ + q + 1)
                    for h in range(QUAD):
                        hh = q * QUAD + h
                        o = (hh % 8) * HD
                        ins = pe.matmul(ps_i[:, o:o + HD], e_buf[:, c, q, h, :],
                                        xdt[:, hh * HD:(hh + 1) * HD], start=True, stop=True)
                    ins.then_inc(intra_ps.sem, 1)

                def step(u):
                    n = u.ahead(1)
                    more = n.exists()

                    def next_x(i):
                        if more:
                            project_x(n, i)

                    def next_z(i):
                        if more:
                            project_z(n, i)

                    def next_turned(i):
                        if more:
                            transpose_x(n, i)

                    next_x(0)
                    broadcast(u, 2)
                    broadcast(u, 3)
                    next_x(1)
                    broadcast(u, 4)
                    next_x(2)
                    broadcast(u, 5)
                    off_diagonal(u, 0, 0)
                    next_x(3)
                    broadcast(u, 6)
                    off_diagonal(u, 0, 1)
                    intra(u, 0, 0)
                    intra(u, 0, 1)
                    broadcast(u, 7)
                    new_state(u, 0, 0)
                    next_x(4)
                    new_state(u, 0, 1)
                    if more:
                        project_dt(n)
                    intra(u, 0, 2)
                    intra(u, 0, 3)
                    next_z(0)
                    c_dot_b(u, 1)
                    next_z(1)
                    if more:
                        transpose_dt(n)
                    next_z(2)
                    off_diagonal(u, 1, 0)
                    off_diagonal(u, 1, 1)
                    next_z(3)
                    intra(u, 1, 0)
                    intra(u, 1, 1)
                    if more:
                        cumulate(n)
                    transpose_xn(n.ahead(1), 0)
                    new_state(u, 1, 0)
                    new_state(u, 1, 1)
                    next_turned(0)
                    next_turned(1)
                    intra(u, 1, 2)
                    transpose_xn(n.ahead(1), 1)
                    intra(u, 1, 3)
                    next_turned(2)
                    next_turned(3)
                    broadcast(n, 0)
                    broadcast(n, 1)
                    next_turned(4)
                    c_dot_b(n, 0)

                u0 = Unit(0, 0)
                for c in range(CH):
                    transpose_xn(u0, c)
                for i in range(PAIRS):
                    project_x(u0, i)
                project_dt(u0)
                for i in range(CH * G2):
                    project_z(u0, i)
                    if i == 1:
                        transpose_dt(u0)
                for c in range(CH):
                    transpose_xn(u0.ahead(1), c)
                cumulate(u0)
                for i in range(PAIRS):
                    transpose_x(u0, i)
                c_dot_b(u0, 0)
                for pair in range(2):
                    broadcast(u0, pair)
                over_units(pe, step)

            @block.scalar
            def _(act):
                def xn_high(u, c):
                    if not u.exists():
                        return
                    wait(act, xnT_ps, u, c + 1)
                    wait(act, z_ps, u.back(1), CH * G2)
                    act.activation(xnT_hi[:, :, c * P:(c + 1) * P],
                                   ps_t[:, :].rearrange("p (k t) -> p k t", k=KD),
                                   ACT.Copy).then_inc(hi_ready.sem, 1)

                def softplus(u):
                    wait(act, dt_nabs, u, 1)
                    act.activation(ex[:, u.b], nabs[:, u.b], ACT.Exp).then_inc(dt_ex.sem, 1)
                    wait(act, dt_ex, u, 1)
                    act.activation(ln1p[:, u.b], ex[:, u.b], ACT.Ln, bias=1.0).then_inc(dt_ln.sem, 1)

                def exp_cum(u):
                    wait(act, cum_ready, u, 1)
                    act.activation(ecum[:, u.b], cum[:, u.b], ACT.Exp).then_inc(ecum_ready.sem, 1)

                def raw_copy(u, i):
                    wait(act, x_ps, u, i + 1)
                    wait(act, hist_done, u.back(1), 2)
                    act.activation(raw[:, 2 * i:2 * i + 2, HIST:HIST + TOK],
                                   x_bank(u, ("x", i))[:, :].rearrange("p (m t) -> p m t", m=2),
                                   ACT.Copy).then_inc(raw_ready.sem, 1)
                    wait(act, xT_ps, u.back(1), min(i + 1, 4))
                    if i == 4:
                        wait(act, xc_ready, u.back(1), PAIRS)
                    for s in range(2):
                        m = 2 * i + s
                        ins = act.activation(acc[:, m, :], x_bank(u, ("x", i))[:, s * TOK:(s + 1) * TOK],
                                             ACT.Identity, bias=cb[:, m:m + 1],
                                             scale=cw[:, m, TAPS - 1:TAPS])
                    ins.then_inc(tap_ready.sem, 1)

                def silu_x(u, i):
                    wait(act, conv_step, u, 2 * (TAPS - 1) * (i + 1))
                    src = acc[:, 2 * i:2 * i + 2, :]
                    dst = src if i < PAIRS - 1 else bcT[:, u.b, :, :]
                    act.activation(dst, src, ACT.Silu).then_inc(xc_ready.sem, 1)

                def x_tok_copy(u, i):
                    wait(act, xT_ps, u, i + 1)
                    if i < PAIRS - 1:
                        act.activation(x_tok[:, u.b, :, i * 256:(i + 1) * 256],
                                       x_bank(u, ("xT", i))[:, :].rearrange("p (c d) -> p c d", c=CH),
                                       ACT.Copy).then_inc(x_tok_ready.sem, 1)
                    else:
                        act.activation(b_tok[:, u.b, :, :],
                                       x_bank(u, ("xT", i))[:, 0:CH * P].rearrange("p (c d) -> p c d", c=CH),
                                       ACT.Copy).then_inc(x_tok_ready.sem, 1)

                def z_copy(u, i):
                    c, g = divmod(i, G2)
                    wait(act, z_ps, u, i + 1)
                    wait(act, y_ready, u.back(2), CH)
                    act.activation(zs[:, u.b, c, g * 512:(g + 1) * 512], x_bank(u, ("z", i))[:, :],
                                   ACT.Copy).then_inc(z_copied.sem, 1)

                def silu_z(u):
                    wait(act, z_copied, u, CH * G2)
                    act.activation(zs[:, u.b], zs[:, u.b], ACT.Silu).then_inc(zs_ready.sem, 1)

                def decay_exponent(u, pair):
                    if not u.exists():
                        return
                    q = pair // 2
                    wait(act, bc_ps, u, pair + 1)
                    wait(act, intra_ps, u.back(1), NQ + q + 1)
                    for h in range(2):
                        head = 2 * pair + h
                        for c in range(CH):
                            o = h * TOK + c * P
                            ins = act.activation(e_buf[:, c, q, head % QUAD, :],
                                                 ps_b[pair % 2][:, o:o + P], ACT.Relu,
                                                 bias=cum[:, u.b, 0, c, head:head + 1], scale=-1.0)
                    ins.then_inc(seg_ready.sem, 1)

                def decay_exp(u, c, q):
                    if not u.exists():
                        return
                    wait(act, seg_ready, u, 2 * q + 2)
                    act.activation(e_buf[:, c, q], e_buf[:, c, q], ACT.Exp, scale=-1.0
                                   ).then_inc(e_ready.sem, 1)

                def step(u):
                    n = u.ahead(1)
                    more = n.exists()
                    if more:
                        raw_copy(n, 0)
                    decay_exponent(u, 2)
                    decay_exponent(u, 3)
                    decay_exp(u, 0, 1)
                    if more:
                        raw_copy(n, 1)
                    decay_exponent(u, 4)
                    if more:
                        raw_copy(n, 2)
                    decay_exponent(u, 5)
                    decay_exp(u, 0, 2)
                    decay_exponent(u, 6)
                    if more:
                        raw_copy(n, 3)
                    decay_exponent(u, 7)
                    decay_exp(u, 0, 3)
                    if more:
                        silu_x(n, 0)
                        silu_x(n, 1)
                        silu_x(n, 2)
                        raw_copy(n, 4)
                    silu_z(u)
                    if more:
                        silu_x(n, 3)
                        z_copy(n, 0)
                        silu_x(n, 4)
                    decay_exp(u, 1, 0)
                    decay_exp(u, 1, 1)
                    if more:
                        z_copy(n, 1)
                        softplus(n)
                        z_copy(n, 2)
                    decay_exp(u, 1, 2)
                    decay_exp(u, 1, 3)
                    if more:
                        z_copy(n, 3)
                        xn_high(n.ahead(1), 0)
                        exp_cum(n)
                        x_tok_copy(n, 0)
                        x_tok_copy(n, 1)
                        xn_high(n.ahead(1), 1)
                        x_tok_copy(n, 2)
                        x_tok_copy(n, 3)
                        decay_exponent(n, 0)
                        decay_exponent(n, 1)
                        decay_exp(n, 0, 0)
                        x_tok_copy(n, 4)

                u0 = Unit(0, 0)
                for c in range(CH):
                    xn_high(u0, c)
                raw_copy(u0, 0)
                for i in range(1, PAIRS):
                    raw_copy(u0, i)
                    silu_x(u0, i - 1)
                silu_x(u0, 4)
                for i in range(CH * G2):
                    z_copy(u0, i)
                softplus(u0)
                for c in range(CH):
                    xn_high(u0.ahead(1), c)
                exp_cum(u0)
                for i in range(PAIRS):
                    x_tok_copy(u0, i)
                decay_exponent(u0, 0)
                decay_exponent(u0, 1)
                decay_exp(u0, 0, 0)
                over_units(act, step)

            @block.vector
            def _(dve):
                def heads(t):
                    return t.rearrange("p (h d) -> p h d", d=HD)

                def per_head(t, n=HEADS):
                    return t.unsqueeze(2).to_broadcast([P, n, HD])

                def statistics(u):
                    if not u.exists():
                        return
                    b = u.b
                    dve.wait_ge(x_loaded[b].sem, (u.it + 1) * 16)
                    for c in range(CH):
                        dve.bn_stats(st[:, b, c, :], x_in[:, b, c, :]).then_inc(ln_step.sem, 1)
                    wait(dve, ln_step, u, CH)
                    dve.memset(pace[:, :], 0.0)
                    for c in range(CH):
                        dve.bn_aggr(mv[:, b, c, :], st[:, b, c, :]).then_inc(ln_step.sem, 1)

                def normalise(u):
                    if not u.exists():
                        return
                    b = u.b
                    wait(dve, rstd_ready, u, 1)
                    wait(dve, xnT_ps, u.back(1), CH)
                    for c in range(CH):
                        dve.tensor_scalar(xn[:, c, :], x_in[:, b, c, :], mv[:, b, c, 0:1],
                                          rstd[:, b, c:c + 1], ALU.subtract, ALU.mult
                                          ).then_inc(xn_ready.sem, 1)

                def xn_low(u, c):
                    if not u.exists():
                        return
                    wait(dve, hi_ready, u, c + 1)
                    dve.tensor_tensor(xnT_lo[:, :, c * P:(c + 1) * P],
                                      ps_t[:, :].rearrange("p (k t) -> p k t", k=KD),
                                      xnT_hi[:, :, c * P:(c + 1) * P].bitcast(F32), ALU.subtract
                                      ).then_inc(lo_ready.sem, 1)

                def dt_bias(u):
                    wait(dve, dt_ps, u, 1)
                    dve.tensor_scalar(vT[0:HL, :], x_bank(u, ("dt", 0))[0:HL, 0:TOK], bias_dt[:, 0:1], None,
                                      ALU.add).then_inc(dt_vT.sem, 1)

                def dt_first(u):
                    b = u.b
                    wait(dve, vT_ps, u, 1)
                    halves = ps_t[:, 0:CH * P].rearrange("p (c h) -> p c h", c=CH)
                    dve.tensor_copy(v[:, b], halves[:, :, 0:HEADS]).then_inc(dt_half.sem, 1)
                    wait(dve, dt_half, u, 1)
                    dve.tensor_tensor(v[:, b], halves[:, :, LO:LO + HEADS], v[:, b], ALU.add
                                      ).then_inc(dt_v.sem, 1)
                    wait(dve, dt_v, u, 1)
                    dve.scalar_tensor_tensor(nabs[:, b], v[:, b], -1.0, v[:, b], ALU.mult, ALU.min
                                             ).then_inc(dt_nabs.sem, 1)

                def dt_second(u):
                    b = u.b
                    wait(dve, dt_ln, u, 1)
                    dve.scalar_tensor_tensor(dt[:, b], v[:, b], 0.0, ln1p[:, b], ALU.max, ALU.add
                                             ).then_inc(dt_ready.sem, 1)
                    wait(dve, dt_ready, u, 1)
                    dve.tensor_tensor(a[:, b], dt[:, b], neg_a[:, :, :].to_broadcast([P, CH, HEADS]),
                                      ALU.mult).then_inc(a_ready.sem, 1)

                def cum_copy(u):
                    b = u.b
                    bank = x_bank(u, ("cum", 0))
                    acs = bank[:, 0:CH * HEADS].rearrange("p (c h) -> p c h", c=CH)
                    tot = bank[:, 32:32 + CH * HEADS].rearrange("p (c h) -> p c h", c=CH)
                    accT = bank[0:HEADS, P:P + TOK]
                    wait(dve, cum_ps, u, 1)
                    dve.tensor_copy(cum[:, b, 0], acs).then_inc(cum_step.sem, 1)
                    dve.tensor_copy(acsT[0:HEADS, b, :], accT).then_inc(cum_step.sem, 1)
                    dve.tensor_copy(cum[:, b, 2], tot).then_inc(cum_step.sem, 1)
                    wait(dve, cum_step, u, 1)
                    dve.tensor_tensor(cum[:, b, 1], tot, cum[:, b, 0], ALU.subtract
                                      ).then_inc(cum_step.sem, 1)
                    wait(dve, cum_step, u, 2)
                    dve.tensor_tensor(acsT[32:32 + HEADS, b, :], accT, acsT[0:HEADS, b, :].bitcast(F32),
                                      ALU.subtract).then_inc(cum_ready.sem, 1)

                def convolve(u, i):
                    b = u.b
                    wait(dve, raw_ready, u, i + 1)
                    wait(dve, tap_ready, u, i + 1)
                    k0 = i * 2 * (TAPS - 1)
                    for j in range(TAPS - 1):
                        tap = TAPS - 2 - j
                        for s in range(2):
                            m = 2 * i + s
                            if j:
                                wait(dve, conv_step, u, k0 + 2 * j + s - 1)
                            dve.scalar_tensor_tensor(acc[:, m, :], raw[:, m, tap:tap + TOK],
                                                     cw[:, m, tap:tap + 1], acc[:, m, :],
                                                     ALU.mult, ALU.add).then_inc(conv_step.sem, 1)

                def keep_history(u):
                    b = u.b
                    wait(dve, conv_step, u, MX * (TAPS - 1))
                    wait(dve, hist_done, u.back(1), 2)
                    dve.tensor_copy(hist[:, b], raw[:, :, TOK:TOK + HIST]).then_inc(hist_done.sem, 1)
                    dve.tensor_copy(raw[:, :, 0:HIST], hist[:, 1 - b]).then_inc(hist_done.sem, 1)

                def mask_cb(u, c):
                    wait(dve, cb_ps, u, c + 1)
                    wait(dve, s_ready, u.back(1), (c + 1) * NQ)
                    dve.tensor_tensor(cbm[:, c, :], ps_y[(c * 5) % 2][:, 0:P], tri[:, :], ALU.mult
                                      ).then_inc(cbm_ready.sem, 1)

                def scale_inputs(u, c):
                    b = u.b
                    wait(dve, intra_ps, u, c * NQ)
                    wait(dve, st_ps, u, G2 * c)
                    if c == 0:
                        wait(dve, x_tok_ready, u, PAIRS)
                        wait(dve, ecum_ready, u, 1)
                    dve.tensor_tensor(heads(xdt[:, :]), heads(x_tok[:, b, c, :]), per_head(dt[:, b, c, :]),
                                      ALU.mult).then_inc(xdt_ready.sem, 1)
                    wait(dve, xdt_ready, u, c + 1)
                    dve.tensor_tensor(heads(xdd[:, :]), heads(xdt[:, :]), per_head(ecum[:, b, 1, c, :]),
                                      ALU.mult).then_inc(xdd_ready.sem, 1)

                def mask(u, c, q):
                    wait(dve, e_ready, u, c * NQ + q + 1)
                    if q == 0:
                        wait(dve, cbm_ready, u, c + 1)
                    e = e_buf[:, c, q]
                    dve.tensor_tensor(e, e, cbm[:, c:c + 1, :].to_broadcast([P, QUAD, P]), ALU.mult
                                      ).then_inc(s_ready.sem, 1)

                def from_state(u, c, g):
                    wait(dve, off_ps, u, G2 * c + g + 1)
                    if g == 0:
                        wait(dve, y_stored[c], u, 0)
                    n = HEADS // G2
                    dve.tensor_tensor(heads(y[:, c, g * 512:(g + 1) * 512]),
                                      heads(ps_y[(c * 5 + 1 + g) % 2][:, :]),
                                      per_head(ecum[:, u.b, 0, c, g * n:(g + 1) * n], n), ALU.mult
                                      ).then_inc(y_off.sem, 1)

                def decay_state(u, c):
                    wait(dve, off_ps, u, G2 * c + 2)
                    wait(dve, st_added, u, G2 * c)
                    dve.tensor_tensor(heads(state[:, u.b, :]), heads(state[:, u.b, :]),
                                      per_head(ecum[:, u.b, 2, c, :]), ALU.mult
                                      ).then_inc(st_decayed.sem, 1)

                def add_state(u, c, g):
                    wait(dve, st_ps, u, G2 * c + g + 1)
                    wait(dve, st_decayed, u, c + 1)
                    s = state[:, u.b, g * 512:(g + 1) * 512]
                    dve.tensor_tensor(s, ps_y[(c * 5 + 3 + g) % 2][:, :], s, ALU.add
                                      ).then_inc(st_added.sem, 1)

                def add_intra(u, c, g):
                    wait(dve, intra_ps, u, c * NQ + 2 * g + 2)
                    wait(dve, y_off, u, G2 * c + g + 1)
                    s = y[:, c, g * 512:(g + 1) * 512]
                    dve.tensor_tensor(s, ps_i[:, :], s, ALU.add).then_inc(y_intra.sem, 1)

                def finish(u, c):
                    wait(dve, xd_ready, u, c + 1)
                    wait(dve, y_intra, u, G2 * c + 2)
                    dve.tensor_tensor(y[:, c, :], y[:, c, :], xd[:, :], ALU.add).then_inc(y_skip.sem, 1)
                    wait(dve, y_skip, u, c + 1)
                    if c == 0:
                        wait(dve, zs_ready, u, 1)
                    dve.tensor_tensor(y[:, c, :], y[:, c, :], zs[:, u.b, c, :], ALU.mult
                                      ).then_inc(y_ready.sem, 1)

                def step(u):
                    n = u.ahead(1)
                    more = n.exists()

                    def next_conv(i):
                        if more:
                            convolve(n, i)

                    mask_cb(u, 0)
                    scale_inputs(u, 0)
                    mask(u, 0, 0)
                    next_conv(0)
                    mask(u, 0, 1)
                    next_conv(1)
                    from_state(u, 0, 0)
                    next_conv(2)
                    from_state(u, 0, 1)
                    decay_state(u, 0)
                    add_intra(u, 0, 0)
                    mask(u, 0, 2)
                    next_conv(3)
                    mask(u, 0, 3)
                    add_state(u, 0, 0)
                    if more:
                        dt_bias(n)
                    next_conv(4)
                    if more:
                        keep_history(n)
                    add_state(u, 0, 1)
                    add_intra(u, 0, 1)
                    mask_cb(u, 1)
                    scale_inputs(u, 1)
                    if more:
                        dt_first(n)
                    mask(u, 1, 0)
                    if more:
                        statistics(n.ahead(1))
                    mask(u, 1, 1)
                    if more:
                        dt_second(n)
                    finish(u, 0)
                    from_state(u, 1, 0)
                    from_state(u, 1, 1)
                    if more:
                        normalise(n.ahead(1))
                    mask(u, 1, 2)
                    add_intra(u, 1, 0)
                    if more:
                        cum_copy(n)
                        xn_low(n.ahead(1), 0)
                    mask(u, 1, 3)
                    decay_state(u, 1)
                    add_state(u, 1, 0)
                    if more:
                        xn_low(n.ahead(1), 1)
                    add_intra(u, 1, 1)
                    add_state(u, 1, 1)
                    finish(u, 1)

                u0 = Unit(0, 0)
                statistics(u0)
                normalise(u0)
                for c in range(CH):
                    xn_low(u0, c)
                statistics(u0.ahead(1))
                for i in range(PAIRS):
                    convolve(u0, i)
                keep_history(u0)
                dt_bias(u0)
                dt_first(u0)
                dt_second(u0)
                normalise(u0.ahead(1))
                for c in range(CH):
                    xn_low(u0.ahead(1), c)
                cum_copy(u0)
                over_units(dve, step)


def phase2(nc, x, yg, norm_w, w_out, w_fc, w_proj, u_t, v_lr, fast_bt, gate, ident_d, out):
    with ExitStack() as ctx:
        def sb(name, shape, dt=F32):
            return ctx.enter_context(nc.sbuf_tensor(name, shape, dt))

        def sem(name):
            return ctx.enter_context(nc.semaphore(name))

        def sig(name, per_unit):
            return Signal(sem(name), per_unit)

        wo_hi = sb("wo_hi", [P, MI, DM], F32R)
        wo_lo = sb("wo_lo", [P, MI, DM], F32R)
        fc = sb("fc", [P, KD, HID], F32R)
        proj = sb("proj", [P, MF, DM], F32R)
        lr_u = sb("lr_u", [LR, HID], F32R)
        lr_v = sb("lr_v", [P, KD, HL], F32R)
        zl = sb("zl", [LR, TOK], F32R)
        so = sb("so", [P, DM])
        sfc = sb("sfc", [P, MF])
        ident = sb("ident2", [P, P])
        ones = sb("ones2", [P, P])
        nw = sb("nw", [P, MI])
        gate_b = sb("gate_b", [P, 1])
        vr = sb("vr", [RANK, DM])
        fbt = sb("fbt", [RANK, RANK])
        st = sb("st2", [P, 2, CH, 6])
        mv = sb("mv2", [P, 2, CH, 2])
        rstd = sb("rstd2", [P, 2, CH])
        yst = sb("yst", [P, 2, CH, 2, 6])
        ymv = sb("ymv", [P, 2, CH, 2])
        msq = sb("msq", [P, 2, CH])
        eps_t = sb("eps2_t", [P, CH])
        pace = sb("pace2", [P, 1])
        power_t = sb("power2_t", [P, CH])
        rms = sb("rms", [P, 2, CH])

        banks = [ctx.enter_context(nc.psum_tensor(f"q{i}", [P, 512], F32)) for i in range(8)]
        ps_t, ps_u, ps_o, ps_d = banks[0:2], banks[2:4], banks[4:6], banks[6:8]

        fc_in = [sem(f"fc_in{i}") for i in range(4)]
        proj_in = [sem(f"proj_in{i}") for i in range(4)]
        const_in = sem("const_in")
        lr_in = sem("lr_in")
        wo_in = sem("wo_in")
        zeroed = sem("zeroed")
        abs_done = sem("abs_done")
        sign_done = sem("sign_done")
        sums_done = sem("sums_done")
        half_done = sem("half_done")
        tern_step = sem("tern_step")
        tern_done = sem("tern_done")
        col_ps = sem("col_ps")
        col_read = sem("col_read")
        inv_ps = sem("inv_ps")
        lr_step = sem("lr_step")
        lr_ps = sem("lr_ps")
        wo_hi_done = sem("wo_hi_done")
        wo_lo_done = sem("wo_lo_done")

        def flat(t):
            return t.rearrange("p a b -> p (a b)")

        setup_stack = ExitStack()

        def tmp(name, shape):
            return setup_stack.enter_context(nc.sbuf_tensor(name, shape, F32))

        proj_src_all = tmp("proj_src", [P, 4, HID])
        fc_src_all = tmp("fc_src", [P, 4, HID])
        wo_raw = tmp("wo_raw", [P, MI, DM])
        half_t = tmp("half", [P, HID])
        u_raw = tmp("u_raw", [RANK, HID])
        inverse = tmp("inverse", [P, MF])
        half = half_t[:, :]
        fc_src = [fc_src_all[:, k, :] for k in range(4)]
        proj_src = [proj_src_all[:, k, :] for k in range(4)]
        fc_w = [fc[:, k, :] for k in range(4)]
        proj_w = [flat(proj[:, 4 * k:4 * k + 4, :]) for k in range(4)]
        ps_sum, ps_proj, ps_lr, ps_inv = banks[0:4], banks[4], banks[5], [banks[i] for i in (6, 7, 0, 1)]

        def ternary(dve, k, w, magnitude, thresholds):
            dve.wait_ge(sums_done, k + 1)
            dve.tensor_tensor(magnitude, magnitude, thresholds, ALU.is_gt).then_inc(tern_step, 1)
            dve.wait_ge(tern_step, k + 1)
            dve.tensor_tensor(w, w.bitcast(F32), magnitude, ALU.mult).then_inc(tern_done, 1)

        with nc.Block() as block:
            @block.sync
            def _(sp):
                sp.dma_start(fc_src[0], w_fc[0:P, :]).then_inc(fc_in[0], 16)
                sp.dma_start(ident[:, :], ident_d).then_inc(const_in, 16)
                sp.dma_start(gate_b[:, :], gate.partition_broadcast(P)).then_inc(const_in, 16)
                sp.dma_start(vr[:, :], v_lr).then_inc(const_in, 16)
                sp.dma_start(fbt[:, :], fast_bt).then_inc(const_in, 16)
                sp.dma_start(nw[:, :], norm_w.rearrange("(m p) -> p m", p=P),
                             allow_slow_non_contiguous=True).then_inc(const_in, 16)
                for k in range(1, 4):
                    sp.dma_start(fc_src[k], w_fc[k * P:(k + 1) * P, :]).then_inc(fc_in[k], 16)
                sp.dma_start(wo_raw[:, :, :], w_out.rearrange("(m p) n -> p m n", p=P)).then_inc(wo_in, 16)
                sp.dma_start(u_raw[:, :], u_t).then_inc(lr_in, 16)
                proj_v = w_proj.rearrange("(j f p) n -> j p f n", f=4, p=P)
                for k in range(4):
                    sp.dma_start(proj_src[k].rearrange("p (f n) -> p f n", f=4), proj_v[k]
                                 ).then_inc(proj_in[k], 16)

            @block.scalar
            def _(act):
                def parts(k, w, src, loaded):
                    act.wait_ge(loaded, 16)
                    act.activation(w, src, ACT.Sign).then_inc(sign_done, 1)
                    act.wait_ge(sign_done, k + 1)
                    act.activation(src, src, ACT.Abs).then_inc(abs_done, 1)

                for k in range(4):
                    parts(k, fc_w[k], fc_src[k], fc_in[k])
                for k in range(4):
                    parts(4 + k, proj_w[k], proj_src[k], proj_in[k])
                act.wait_ge(lr_step, 7)
                act.wait_ge(zeroed, 6)
                for row in (0, 32, 64):
                    act.activation(lr_u[row:row + RANK, :], u_raw[:, :], ACT.Copy).then_inc(lr_step, 1)

            @block.tensor
            def _(pe):
                pe.wait_ge(const_in, 16 * 5)
                for k in range(KD):
                    ins = pe.matmul(ps_lr[:, k * RANK:(k + 1) * RANK], vr[:, k * P:(k + 1) * P],
                                    fbt[:, :], start=True, stop=True)
                ins.then_inc(lr_ps, 1)
                pe.wait_ge(zeroed, 1)
                for k in range(4):
                    pe.wait_ge(abs_done, k + 1)
                    for j in range(4):
                        ins = pe.matmul(ps_sum[j][:, :], ones[:, :],
                                        fc_src[k][:, j * 512:(j + 1) * 512],
                                        start=(k == 0), stop=(k == 3))
                    ins.then_inc(sums_done, 1)
                pe.wait_ge(half_done, 4)
                for j in range(4):
                    for i in range(4):
                        m = 4 * j + i
                        ins = pe.transpose(ps_sum[j][:, i * P:(i + 1) * P],
                                           half[:, m * P:(m + 1) * P], ident[:, :])
                    ins.then_inc(col_ps, 1)
                for j in range(4):
                    if j == 0:
                        pe.wait_ge(lr_step, 3)
                    for i in range(4):
                        m = 4 * j + i
                        ins = pe.matmul(ps_inv[j][0:RANK, i * P:(i + 1) * P],
                                        inverse[:, m:m + 1].to_broadcast([P, RANK]), ident[:, :],
                                        start=True, stop=True)
                    ins.then_inc(inv_ps, 1)
                for k in range(4):
                    pe.wait_ge(abs_done, 4 + k + 1)
                    for f in range(4):
                        ins = pe.matmul(ps_proj[:, :], ones[:, :],
                                        proj_src[k][:, f * 512:(f + 1) * 512],
                                        start=(k == 0 and f == 0), stop=(k == 3 and f == 3))
                    ins.then_inc(sums_done, 1)

            @block.vector
            def _(dve):
                dve.memset(ones[:, :], 1.0).then_inc(zeroed, 1)
                dve.memset(lr_u[:, :].bitcast(F32), 0.0).then_inc(zeroed, 1)
                dve.memset(zl[:, :].bitcast(F32), 0.0).then_inc(zeroed, 1)
                dve.memset(eps_t[:, :], LN_EPS).then_inc(zeroed, 1)
                dve.memset(power_t[:, :], -0.5).then_inc(zeroed, 1)
                dve.memset(lr_v[:, :, :].bitcast(F32), 0.0).then_inc(zeroed, 1)

                dve.wait_ge(lr_ps, 1)
                bv = ps_lr[:, 0:KD * RANK].rearrange("p (k q) -> p k q", k=KD)
                dve.wait_ge(zeroed, 6)
                dve.tensor_copy(lr_v[:, :, 0:RANK], bv).then_inc(lr_step, 1)
                dve.wait_ge(lr_step, 1)
                dve.tensor_tensor(lr_v[:, :, LO:LO + RANK], bv, lr_v[:, :, 0:RANK].bitcast(F32),
                                  ALU.subtract).then_inc(lr_step, 1)
                dve.wait_ge(wo_in, 16)
                dve.wait_ge(const_in, 16 * 5)
                for m in range(MI):
                    dve.tensor_scalar(wo_hi[:, m, :], wo_raw[:, m, :], nw[:, m:m + 1], None, ALU.mult
                                      ).then_inc(wo_hi_done, 1)
                dve.wait_ge(sums_done, 4)
                for j in range(4):
                    dve.tensor_scalar(half[:, j * 512:(j + 1) * 512], ps_sum[j][:, :], 0.5 / DM, 0.5e-5,
                                      ALU.mult, ALU.max).then_inc(half_done, 1)
                for m in range(MI):
                    dve.wait_ge(wo_hi_done, m + 1)
                    dve.scalar_tensor_tensor(wo_lo[:, m, :], wo_raw[:, m, :], nw[:, m:m + 1],
                                             wo_hi[:, m, :].bitcast(F32), ALU.mult, ALU.subtract
                                             ).then_inc(wo_lo_done, 1)
                for j in range(4):
                    dve.wait_ge(col_ps, j + 1)
                    dve.tensor_scalar(sfc[:, 4 * j:4 * j + 4],
                                      ps_sum[j][:, :].rearrange("p (i t) -> p i t", i=4)[:, :, 0],
                                      2.0, None, ALU.mult).then_inc(col_read, 1)
                dve.wait_ge(col_read, 4)
                dve.reciprocal(inverse[:, :], sfc[:, :]).then_inc(lr_step, 1)
                dve.wait_ge(half_done, 4)
                for k in range(2):
                    ternary(dve, k, fc_w[k], fc_src[k], half)
                dve.wait_ge(lr_in, 16)
                for j in range(4):
                    cols = slice(j * 512, (j + 1) * 512)
                    dve.wait_ge(inv_ps, j + 1)
                    dve.scalar_tensor_tensor(u_raw[:, cols], u_raw[:, cols], gate_b[0:RANK, 0:1],
                                             ps_inv[j][0:RANK, :], ALU.mult, ALU.mult
                                             ).then_inc(lr_step, 1)
                for k in range(2, 4):
                    ternary(dve, k, fc_w[k], fc_src[k], half)
                dve.wait_ge(sums_done, 8)
                dve.tensor_scalar(so[:, :], ps_proj[:, :], 0.5 / HID, 0.5e-5, ALU.mult, ALU.max
                                  ).then_inc(half_done, 1)
                dve.wait_ge(lr_step, 10)
                dve.tensor_tensor(lr_u[96:96 + RANK, :], u_raw[:, :], lr_u[0:RANK, :].bitcast(F32),
                                  ALU.subtract).then_inc(lr_step, 1)

        setup_stack.close()

        r_hi = sb("r_hi", [P, MF, TOK], F32R)
        r_lo = sb("r_lo", [P, MF, TOK], F32R)
        y_in = sb("y_in", [P, 2, CH, DI])
        x1 = sb("x1", [P, 2, CH, DM])
        yT_hi = sb("yT_hi", [P, MI, TOK], F32R)
        yT_lo = sb("yT_lo", [P, MI, TOK], F32R)
        xn = sb("xn2", [P, CH, DM])
        xnT_hi = sb("x2T_hi", [P, KD, TOK], F32R)
        xnT_lo = sb("x2T_lo", [P, KD, TOK], F32R)
        r = sb("r", [P, 2, 2, TOK])
        o_buf = sb("o_buf", [P, CH, DM])

        y_loaded = [sig(f"y_loaded{s}", 8) for s in range(2)]
        xr_loaded = [sig(f"xr_loaded{s}", 8) for s in range(2)]
        stored = [sig(f"stored{c}", 16) for c in range(CH)]
        rms_step = sig("rms_step", 8)
        yT_ps = sig("yT_ps", 4)
        yT_hi_ready = sig("yT_hi_ready", 4)
        yT_lo_ready = sig("yT_lo_ready", 4)
        o_ps = sig("o_ps", CH)
        x1_ready = sig("x1_ready", CH)
        ln_step = sig("ln2_step", 4)
        rstd_eps = sig("rstd2_eps", 1)
        rstd_ready = sig("rstd2_ready", 1)
        rms_eps = sig("rms_eps", 1)
        rms_ready = sig("rms_ready", 1)
        xn_ready = sig("xn2_ready", CH)
        xT_ps = sig("x2T_ps", CH)
        xT_hi_ready = sig("x2T_hi_ready", CH)
        xT_lo_ready = sig("x2T_lo_ready", CH)
        zl_ps = sig("zl_ps", 1)
        zl_step = sig("zl_step", 3)
        zl_ready = sig("zl_ready", 1)
        up_ps = sig("up_ps", MF // 2)
        relu_done = sig("relu_done", MF // 2)
        sq_ready = sig("sq_ready", MF // 2)
        r_hi_ready = sig("r_hi_ready", MF // 2)
        r_lo_ready = sig("r_lo_ready", MF // 2)
        down_ps = sig("down_ps", CH)
        scaled = sig("scaled", CH)
        out_ready = sig("out_ready", CH)

        x_v = x.rearrange("b (i s c p) d -> (b i) s p c d", s=2, c=CH, p=P)
        y_v = yg.rearrange("b (i s c p) d -> (b i) s p c d", s=2, c=CH, p=P)
        out_v = out.rearrange("b (i s c p) d -> (b i) s c p d", s=2, c=CH, p=P)

        with nc.Block() as block:
            @block.sync
            def _(sp):
                def load_y(u):
                    if not u.exists():
                        return
                    wait(sp, yT_ps, u.back(2), 4)
                    wait(sp, rms_step, u.back(2), 4)
                    sp.dma_start(y_in[:, u.b], y_v[u.it, u.b]).then_inc(y_loaded[u.b].sem, 16)

                def load_x(u):
                    if not u.exists():
                        return
                    wait(sp, out_ready, u.back(2), CH)
                    sp.dma_start(x1[:, u.b], x_v[u.it, u.b]).then_inc(xr_loaded[u.b].sem, 16)

                def step(u):
                    load_y(u.ahead(2))
                    for c in range(CH):
                        wait(sp, out_ready, u, c + 1)
                        sp.dma_start(out_v[u.it, u.b, c], o_buf[:, c, :]).then_inc(stored[c].sem, 16)
                    load_x(u.ahead(2))

                for b in range(2):
                    load_y(Unit(0, b))
                    load_x(Unit(0, b))
                over_units(sp, step)
                for c in range(CH):
                    sp.wait_ge(stored[c].sem, 16 * UNITS)

            @block.gpsimd
            def _(pool):
                def roots(u):
                    if not u.exists():
                        return
                    wait(pool, rms_step, u, 8)
                    wait(pool, x1_ready, u.back(2), CH)
                    inverse_root(pool, rms[:, u.b, :], msq[:, u.b, :], eps_t[:, :], power_t[:, :],
                                 u, rms_eps, rms_ready)
                    wait(pool, ln_step, u, 4)
                    wait(pool, xn_ready, u.back(2), CH)
                    inverse_root(pool, rstd[:, u.b, :], mv[:, u.b, :, 1], eps_t[:, :], power_t[:, :],
                                 u, rstd_eps, rstd_ready)

                roots(Unit(0, 0))
                over_units(pool, lambda u: roots(u.ahead(1)))

            @block.tensor
            def _(pe):
                def parts(hi, lo, n, c0, w):
                    return [[t[:, k, c0:c0 + w] for k in range(n)] for t in (hi, lo)]

                def transpose_y(u, i):
                    if i == 0:
                        pe.wait_ge(y_loaded[u.b].sem, (u.it + 1) * 16)
                    if i < 2:
                        wait(pe, xT_lo_ready, u.back(1), i + 1)
                    else:
                        wait(pe, yT_lo_ready, u, i - 1)
                    for m in range(2):
                        for c in range(CH):
                            o = (m * CH + c) * P
                            ins = pe.transpose(ps_t[i % 2][:, o:o + P],
                                               y_in[:, u.b, c, (2 * i + m) * P:(2 * i + m + 1) * P],
                                               ident[:, :])
                    ins.then_inc(yT_ps.sem, 1)

                def project_out(u, c):
                    if c == 0:
                        wait(pe, yT_lo_ready, u, 4)
                        wait(pe, zl_ready, u.back(1), 1)
                    else:
                        wait(pe, x1_ready, u.back(1), c + 1)
                    mm3(pe, ps_o[c][:, :], parts(yT_hi, yT_lo, MI, c * P, P),
                        parts(wo_hi, wo_lo, MI, 0, DM)).then_inc(o_ps.sem, 1)

                def transpose_xn(u, c):
                    wait(pe, xn_ready, u, c + 1)
                    wait(pe, yT_lo_ready, u, 3 + c)
                    for k in range(KD):
                        ins = pe.transpose(ps_t[c][:, k * P:(k + 1) * P], xn[:, c, k * P:(k + 1) * P],
                                           ident[:, :])
                    ins.then_inc(xT_ps.sem, 1)

                def low_rank(u):
                    wait(pe, xT_lo_ready, u, CH)
                    wait(pe, x1_ready, u, 1)
                    both_parts(pe, ps_o[0][0:HL, 0:TOK], lr_v, xnT_hi, xnT_lo).then_inc(zl_ps.sem, 1)

                def up(u, i):
                    if i == 0:
                        wait(pe, zl_ready, u, 1)
                    wait(pe, relu_done, u, i - 1)
                    for j in range(2):
                        m = 2 * i + j
                        dst = ps_u[i % 2][:, j * TOK:(j + 1) * TOK]
                        for k in range(KD):
                            w = fc[:, k, m * P:(m + 1) * P]
                            pe.matmul(dst, w, xnT_hi[:, k, :], start=(k == 0), stop=False)
                            pe.matmul(dst, w, xnT_lo[:, k, :], start=False, stop=False)
                        ins = pe.matmul(dst, lr_u[:, m * P:(m + 1) * P], zl[:, :], start=False, stop=True)
                    ins.then_inc(up_ps.sem, 1)

                def down(u, c, f0=0, f1=MF):
                    if f0 == 0:
                        wait(pe, scaled, u.back(1), c + 1)
                    for f in range(f0, f1):
                        if c == 0 and f % 2 == 0:
                            wait(pe, r_lo_ready, u, f // 2 + 1)
                        for t in (r_hi, r_lo):
                            ins = pe.matmul(ps_d[c][:, :], t[:, f, c * P:(c + 1) * P], proj[:, f, :],
                                            start=(f == 0 and t is r_hi), stop=(f == MF - 1 and t is r_lo))
                    if f1 == MF:
                        ins.then_inc(down_ps.sem, 1)

                def step(u):
                    n = u.ahead(1)
                    more = n.exists()
                    for i in range(MF // 2):
                        if more and i % 2 == 0:
                            transpose_y(n, i // 2)
                        up(u, i)
                    if more:
                        for c in range(CH):
                            project_out(n, c)
                    down(u, 0)
                    if more:
                        for c in range(CH):
                            transpose_xn(n, c)
                    down(u, 1, 0, MF // 2)
                    if more:
                        low_rank(n)
                    down(u, 1, MF // 2, MF)

                u0 = Unit(0, 0)
                for i in range(4):
                    transpose_y(u0, i)
                for c in range(CH):
                    project_out(u0, c)
                for c in range(CH):
                    transpose_xn(u0, c)
                low_rank(u0)
                over_units(pe, step)

            @block.scalar
            def _(act):
                def y_high(u, i):
                    wait(act, yT_ps, u, i + 1)
                    wait(act, o_ps, u.back(1), CH)
                    act.activation(flat(yT_hi[:, 2 * i:2 * i + 2, :]), ps_t[i % 2][:, :], ACT.Copy
                                   ).then_inc(yT_hi_ready.sem, 1)

                def x_high(u, c):
                    wait(act, xT_ps, u, c + 1)
                    wait(act, up_ps, u.back(1), MF // 2)
                    act.activation(xnT_hi[:, :, c * P:(c + 1) * P],
                                   ps_t[c][:, :].rearrange("p (k t) -> p k t", k=KD),
                                   ACT.Copy).then_inc(xT_hi_ready.sem, 1)

                def squared_relu(u, i):
                    wait(act, up_ps, u, i + 1)
                    wait(act, r_lo_ready, u, i - 1)
                    for j in range(2):
                        m = 2 * i + j
                        ins = act.activation(r[:, i % 2, j, :], ps_u[i % 2][:, j * TOK:(j + 1) * TOK],
                                             ACT.Relu, scale=sfc[:, m:m + 1])
                    ins.then_inc(relu_done.sem, 1)
                    wait(act, relu_done, u, i + 1)
                    act.activation(r[:, i % 2], r[:, i % 2], ACT.Square).then_inc(sq_ready.sem, 1)

                def step(u):
                    n = u.ahead(1)
                    more = n.exists()
                    for i in range(MF // 2):
                        if more and i % 2 == 0:
                            y_high(n, i // 2)
                        squared_relu(u, i)
                    if more:
                        for c in range(CH):
                            x_high(n, c)

                u0 = Unit(0, 0)
                for i in range(4):
                    y_high(u0, i)
                for c in range(CH):
                    x_high(u0, c)
                over_units(act, step)

            @block.vector
            def _(dve):
                def mean_square(u):
                    b = u.b
                    dve.wait_ge(y_loaded[b].sem, (u.it + 1) * 16)
                    for c in range(CH):
                        for g in range(2):
                            dve.bn_stats(yst[:, b, c, g, :], y_in[:, b, c, g * 512:(g + 1) * 512]
                                         ).then_inc(rms_step.sem, 1)
                    wait(dve, rms_step, u, 2 * CH)
                    dve.memset(pace[:, :], 0.0)
                    for c in range(CH):
                        dve.bn_aggr(ymv[:, b, c, :], yst[:, b, c].rearrange("p g s -> p (g s)")
                                    ).then_inc(rms_step.sem, 1)
                    wait(dve, rms_step, u, 6)
                    dve.tensor_tensor(msq[:, b, :], ymv[:, b, :, 0], ymv[:, b, :, 0], ALU.mult
                                      ).then_inc(rms_step.sem, 1)
                    wait(dve, rms_step, u, 7)
                    dve.tensor_tensor(msq[:, b, :], msq[:, b, :], ymv[:, b, :, 1], ALU.add
                                      ).then_inc(rms_step.sem, 1)

                def y_low(u, i):
                    wait(dve, yT_hi_ready, u, i + 1)
                    hi = flat(yT_hi[:, 2 * i:2 * i + 2, :]).bitcast(F32)
                    dve.tensor_tensor(flat(yT_lo[:, 2 * i:2 * i + 2, :]), ps_t[i % 2][:, :], hi,
                                      ALU.subtract).then_inc(yT_lo_ready.sem, 1)

                def residual(u, c):
                    b = u.b
                    wait(dve, o_ps, u, c + 1)
                    if c == 0:
                        dve.wait_ge(xr_loaded[b].sem, (u.it + 1) * 16)
                        wait(dve, rms_ready, u, 1)
                    dve.scalar_tensor_tensor(x1[:, b, c, :], ps_o[c][:, :], rms[:, b, c:c + 1],
                                             x1[:, b, c, :], ALU.mult, ALU.add).then_inc(x1_ready.sem, 1)

                def normalise(u):
                    b = u.b
                    for c in range(CH):
                        wait(dve, x1_ready, u, c + 1)
                        dve.bn_stats(st[:, b, c, :], x1[:, b, c, :]).then_inc(ln_step.sem, 1)
                    wait(dve, ln_step, u, CH)
                    dve.memset(pace[:, :], 0.0)
                    for c in range(CH):
                        dve.bn_aggr(mv[:, b, c, :], st[:, b, c, :]).then_inc(ln_step.sem, 1)
                    wait(dve, rstd_ready, u, 1)
                    wait(dve, xT_ps, u.back(1), CH)
                    for c in range(CH):
                        dve.tensor_scalar(xn[:, c, :], x1[:, b, c, :], mv[:, b, c, 0:1],
                                          rstd[:, b, c:c + 1], ALU.subtract, ALU.mult
                                          ).then_inc(xn_ready.sem, 1)

                def x_low(u, c):
                    wait(dve, xT_hi_ready, u, c + 1)
                    dve.tensor_tensor(xnT_lo[:, :, c * P:(c + 1) * P],
                                      ps_t[c][:, :].rearrange("p (k t) -> p k t", k=KD),
                                      xnT_hi[:, :, c * P:(c + 1) * P].bitcast(F32), ALU.subtract
                                      ).then_inc(xT_lo_ready.sem, 1)

                def split_low_rank(u):
                    src = ps_o[0][0:RANK, 0:TOK]
                    wait(dve, zl_ps, u, 1)
                    dve.tensor_copy(zl[0:RANK, :], src).then_inc(zl_step.sem, 1)
                    dve.tensor_copy(zl[96:96 + RANK, :], src).then_inc(zl_step.sem, 1)
                    dve.tensor_copy(zl[32:32 + RANK, :], ps_o[0][LO:LO + RANK, 0:TOK]
                                    ).then_inc(zl_step.sem, 1)
                    wait(dve, zl_step, u, 1)
                    dve.tensor_tensor(zl[64:64 + RANK, :], src, zl[0:RANK, :].bitcast(F32), ALU.subtract
                                      ).then_inc(zl_ready.sem, 1)

                def split_squares(u, i):
                    wait(dve, sq_ready, u, i + 1)
                    if i == 0:
                        wait(dve, down_ps, u.back(1), CH)
                    dve.tensor_copy(r_hi[:, 2 * i:2 * i + 2, :], r[:, i % 2]).then_inc(r_hi_ready.sem, 1)
                    wait(dve, r_hi_ready, u, i + 1)
                    dve.tensor_tensor(r_lo[:, 2 * i:2 * i + 2, :], r[:, i % 2],
                                      r_hi[:, 2 * i:2 * i + 2, :].bitcast(F32), ALU.subtract
                                      ).then_inc(r_lo_ready.sem, 1)

                def output(u, c):
                    wait(dve, down_ps, u, c + 1)
                    wait(dve, stored[c], u, 0)
                    dve.tensor_tensor(o_buf[:, c, :], ps_d[c][:, :], so[:, :], ALU.mult
                                      ).then_inc(scaled.sem, 1)
                    wait(dve, scaled, u, c + 1)
                    dve.tensor_tensor(o_buf[:, c, :], o_buf[:, c, :], x1[:, u.b, c, :], ALU.add
                                      ).then_inc(out_ready.sem, 1)

                def step(u):
                    n = u.ahead(1)
                    more = n.exists()
                    for i in range(MF // 2):
                        if more and i % 2 == 0:
                            y_low(n, i // 2)
                        split_squares(u, i)
                    if more:
                        mean_square(n)
                        for c in range(CH):
                            residual(n, c)
                        normalise(n)
                    output(u, 0)
                    if more:
                        for c in range(CH):
                            x_low(n, c)
                        split_low_rank(n)
                    output(u, 1)

                def ternary_proj(k):
                    ternary(dve, 4 + k, proj[:, 4 * k:4 * k + 4, :],
                            proj_src[k].rearrange("p (f n) -> p f n", f=4),
                            so[:, :].unsqueeze(1).to_broadcast([P, 4, DM]))

                u0 = Unit(0, 0)
                for i in range(4):
                    y_low(u0, i)
                mean_square(u0)
                dve.wait_ge(half_done, 5)
                ternary_proj(0)
                residual(u0, 0)
                ternary_proj(1)
                residual(u0, 1)
                normalise(u0)
                for c in range(CH):
                    x_low(u0, c)
                split_low_rank(u0)
                ternary_proj(2)
                ternary_proj(3)
                dve.wait_ge(tern_done, 8)
                dve.tensor_scalar(so[:, :], so[:, :], 2.0, None, ALU.mult).then_inc(half_done, 1)
                dve.wait_ge(half_done, 6)
                over_units(dve, step)


def kernel(**inputs):
    import numpy as np
    import concourse.bacc as bacc
    from concourse.bass_utils import run_bass_kernel_spmd

    def arr(name):
        return np.asarray(inputs[name])

    def turned(name):
        return np.ascontiguousarray(arr(name).T)

    data = {
        "x": arr("L0_attn_u"),
        "w_in": turned("L0_attn_in_proj_w"),
        "conv_w": arr("L0_attn_conv_w"),
        "conv_b": arr("L0_attn_conv_b"),
        "dt_bias": arr("L0_attn_dt_bias"),
        "a_log": arr("L0_attn_A_log"),
        "d_skip": arr("L0_attn_D"),
        "norm_w": arr("L0_attn_norm_w"),
        "w_out": turned("L0_attn_out_proj_w"),
        "w_fc": turned("L0_ffn_w_fc"),
        "w_proj": turned("L0_ffn_w_proj"),
        "u_t": turned("L0_ffn_u"),
        "v_lr": arr("L0_ffn_v"),
        "fast_bt": turned("L0_ffn_fast_b"),
        "gate": arr("L0_ffn_gate").reshape(1),
        "ident": np.eye(P, dtype=np.float32),
        "tri": np.triu(np.ones((P, P), np.float32)),
    }
    nc = bacc.Bacc("TRN2", target_bir_lowering=False, num_devices=1)
    d = {}
    for name, value in data.items():
        value = np.ascontiguousarray(value)
        data[name] = value
        d[name] = nc.dram_tensor(f"{name}_dram", list(value.shape), mybir.dt.from_np(value.dtype),
                                 kind="ExternalInput").ap()
    yg = nc.dram_tensor("gated_dram", [BATCH, SEQ, DI], F32, kind="Internal").ap()
    out = nc.dram_tensor("out_dram", [BATCH, SEQ, DM], F32, kind="ExternalOutput").ap()
    phase1(nc, d["x"], d["w_in"], d["conv_w"], d["conv_b"], d["dt_bias"], d["a_log"], d["d_skip"],
           d["ident"], d["tri"], yg)
    phase2(nc, d["x"], yg, d["norm_w"], d["w_out"], d["w_fc"], d["w_proj"], d["u_t"], d["v_lr"],
           d["fast_bt"], d["gate"], d["ident"], out)
    result = run_bass_kernel_spmd(nc, [{f"{name}_dram": value for name, value in data.items()}], core_ids=[0])
    return result.results[0]["out_dram"]
```
